# Optimizing a Trainium2 kernel written in Bass

```python
import numpy as np
import jax
import jax.numpy as jnp

def _softmax(x, axis=-1):
    return jax.nn.softmax(x, axis=axis)

def _gelu(x):
    return jax.nn.gelu(x, approximate=True)

def _silu(x):
    return jax.nn.silu(x)

def _sigmoid(x):
    return jax.nn.sigmoid(x)

def _layernorm(x, axis=-1, eps=1e-05):
    m = jnp.mean(x, axis=axis, keepdims=True)
    v = jnp.var(x, axis=axis, keepdims=True)
    return (x - m) / jnp.sqrt(v + eps)

def _scatter_add(tgt, idx, src, axis=0):
    return tgt.at[idx].add(src)

def _segment_sum(src, seg, n):
    return jax.ops.segment_sum(src, seg, n)
kernel_name = 'mk_gps_d1_gnn_r8_93eded'

def setup_inputs(seed: int=0):
    np.random.seed(seed)
    _w = jnp.asarray

    def _rec_inputs():
        import jax
        import jax.numpy as jnp
        _gk = jax.random.key(seed)
        x = -0.0003713 + 1 * jax.random.normal(jax.random.fold_in(_gk, 1), (6250, 256), jnp.float32)
        src = jax.random.randint(jax.random.fold_in(_gk, 2), (200000,), 0, 6250, jnp.int32)
        dst = jax.random.randint(jax.random.fold_in(_gk, 3), (200000,), 0, 6250, jnp.int32)
        _o = jnp.argsort(dst, stable=True)
        src = src[_o]
        dst = dst[_o]
        return (x, src, dst)
    x, src, dst = _rec_inputs()

    def _L0_gnn_setup():
        import jax, jax.numpy as jnp
        import numpy as np
        N = 6250
        E = 100000
        IN = 256
        H = 8
        C = 32
        NEG_SLOPE = 0.2
        key = jax.random.key(seed)
        k0, k1, k2, k3, k4 = jax.random.split(key, 5)
        x = jax.random.normal(k0, (N, IN), jnp.float32)
        edge_index = jax.random.randint(k1, (2, E), 0, N, dtype=jnp.int64)
        W = jax.random.normal(k2, (IN, H * C), jnp.float32) / np.sqrt(IN).astype(np.float32)
        att_src = jax.random.normal(k3, (H, C), jnp.float32) * 0.1
        att_dst = jax.random.normal(k4, (H, C), jnp.float32) * 0.1
        bias = jnp.zeros((H * C,), jnp.float32)
        return {'x': x, 'edge_index': edge_index, 'W': W, 'att_src': att_src, 'att_dst': att_dst, 'bias': bias}
    _L0_gnn_all = _L0_gnn_setup()
    _L0_gnn_in = {k: v for k, v in _L0_gnn_all.items() if k in ('W', 'att_src', 'att_dst', 'bias')}
    del _L0_gnn_all

    def _L0_mix_setup():
        import jax, jax.numpy as jnp
        import numpy as np
        NHEAD = 8
        ATT_EPS = 1e-06
        LN_EPS = 1e-05

        def _layernorm(x, g, b):
            mu = jnp.mean(x, axis=-1, keepdims=True)
            var = jnp.mean(jnp.square(x - mu), axis=-1, keepdims=True)
            return (x - mu) * jax.lax.rsqrt(var + LN_EPS) * g + b
        key = jax.random.key(seed)
        ks = jax.random.split(key, 7)
        N, L, C = (4, 2048, 256)
        s = 1.0 / np.sqrt(C)
        return {'x': jax.random.normal(ks[0], (N, L, C), jnp.float32), 'Wq': jax.random.normal(ks[1], (C, C), jnp.float32) * s, 'Wk': jax.random.normal(ks[2], (C, C), jnp.float32) * s, 'Wv': jax.random.normal(ks[3], (C, C), jnp.float32) * s, 'Wm': jax.random.normal(ks[4], (C, C), jnp.float32) * s, 'W1': jax.random.normal(ks[5], (2 * C, 2 * C), jnp.float32) * (1.0 / np.sqrt(2 * C)), 'W2': jax.random.normal(ks[6], (2 * C, C), jnp.float32) * (1.0 / np.sqrt(2 * C)), 'g1': jnp.ones((C,), jnp.float32), 'b1': jnp.zeros((C,), jnp.float32), 'g2': jnp.ones((C,), jnp.float32), 'b2': jnp.zeros((C,), jnp.float32)}
    _L0_mix_all = _L0_mix_setup()
    _L0_mix_in = {k: v for k, v in _L0_mix_all.items() if k in ('Wq', 'Wk', 'Wv', 'Wm', 'W1', 'W2', 'g1', 'b1', 'g2', 'b2')}
    del _L0_mix_all

    def _L0_ffn_setup():
        import jax, jax.numpy as jnp
        import numpy as np
        DIM = 256
        H = 8
        D = 64
        G = 64
        INNER = H * D
        SCALE = D ** (-0.5)
        key = jax.random.key(seed)
        ks = jax.random.split(key, 12)
        B, N = (4, 2048)
        x = jax.random.normal(ks[0], (B, N, DIM), dtype=jnp.float32)
        s = lambda fan_in: 1.0 / np.sqrt(fan_in)
        W_fx = jax.random.normal(ks[1], (DIM, INNER), dtype=jnp.float32) * s(DIM)
        b_fx = jnp.zeros((INNER,), dtype=jnp.float32)
        W_x = jax.random.normal(ks[2], (DIM, INNER), dtype=jnp.float32) * s(DIM)
        b_x = jnp.zeros((INNER,), dtype=jnp.float32)
        A = jax.random.normal(ks[3], (G, D), dtype=jnp.float32)
        Q, _ = jnp.linalg.qr(A.T)
        W_slice = Q[:, :G].astype(jnp.float32)
        b_slice = jnp.zeros((G,), dtype=jnp.float32)
        W_q = jax.random.normal(ks[4], (D, D), dtype=jnp.float32) * s(D)
        W_k = jax.random.normal(ks[5], (D, D), dtype=jnp.float32) * s(D)
        W_v = jax.random.normal(ks[6], (D, D), dtype=jnp.float32) * s(D)
        W_out = jax.random.normal(ks[7], (INNER, DIM), dtype=jnp.float32) * s(INNER)
        b_out = jnp.zeros((DIM,), dtype=jnp.float32)
        temperature = jnp.ones((1, H, 1, 1), dtype=jnp.float32) * 0.5
        return {'x': x, 'W_fx': W_fx, 'b_fx': b_fx, 'W_x': W_x, 'b_x': b_x, 'W_slice': W_slice, 'b_slice': b_slice, 'W_q': W_q, 'W_k': W_k, 'W_v': W_v, 'W_out': W_out, 'b_out': b_out, 'temperature': temperature}
    _L0_ffn_all = _L0_ffn_setup()
    _L0_ffn_in = {k: v for k, v in _L0_ffn_all.items() if k in ('W_fx', 'b_fx', 'W_x', 'b_x', 'W_slice', 'b_slice', 'W_q', 'W_k', 'W_v', 'W_out', 'b_out', 'temperature')}
    del _L0_ffn_all
    return {'x': x, 'src': src, 'dst': dst, 'L0_gnn_W': _L0_gnn_in['W'], 'L0_gnn_att_src': _L0_gnn_in['att_src'], 'L0_gnn_att_dst': _L0_gnn_in['att_dst'], 'L0_gnn_bias': _L0_gnn_in['bias'], 'L0_mix_Wq': _L0_mix_in['Wq'], 'L0_mix_Wk': _L0_mix_in['Wk'], 'L0_mix_Wv': _L0_mix_in['Wv'], 'L0_mix_Wm': _L0_mix_in['Wm'], 'L0_mix_W1': _L0_mix_in['W1'], 'L0_mix_W2': _L0_mix_in['W2'], 'L0_mix_g1': _L0_mix_in['g1'], 'L0_mix_b1': _L0_mix_in['b1'], 'L0_mix_g2': _L0_mix_in['g2'], 'L0_mix_b2': _L0_mix_in['b2'], 'L0_ffn_W_fx': _L0_ffn_in['W_fx'], 'L0_ffn_b_fx': _L0_ffn_in['b_fx'], 'L0_ffn_W_x': _L0_ffn_in['W_x'], 'L0_ffn_b_x': _L0_ffn_in['b_x'], 'L0_ffn_W_slice': _L0_ffn_in['W_slice'], 'L0_ffn_b_slice': _L0_ffn_in['b_slice'], 'L0_ffn_W_q': _L0_ffn_in['W_q'], 'L0_ffn_W_k': _L0_ffn_in['W_k'], 'L0_ffn_W_v': _L0_ffn_in['W_v'], 'L0_ffn_W_out': _L0_ffn_in['W_out'], 'L0_ffn_b_out': _L0_ffn_in['b_out'], 'L0_ffn_temperature': _L0_ffn_in['temperature']}

def reference(x, src, dst, L0_gnn_W, L0_gnn_att_src, L0_gnn_att_dst, L0_gnn_bias, L0_mix_Wq, L0_mix_Wk, L0_mix_Wv, L0_mix_Wm, L0_mix_W1, L0_mix_W2, L0_mix_g1, L0_mix_b1, L0_mix_g2, L0_mix_b2, L0_ffn_W_fx, L0_ffn_b_fx, L0_ffn_W_x, L0_ffn_b_x, L0_ffn_W_slice, L0_ffn_b_slice, L0_ffn_W_q, L0_ffn_W_k, L0_ffn_W_v, L0_ffn_W_out, L0_ffn_b_out, L0_ffn_temperature):
    import jax
    import jax.numpy as jnp

    def _L0_gnn_ref(x, edge_index, W, att_src, att_dst, bias):
        import jax, jax.numpy as jnp
        import numpy as np
        N = 6250
        E = 100000
        IN = 256
        H = 8
        C = 32
        NEG_SLOPE = 0.2
        n = x.shape[0]
        loops = jnp.arange(n, dtype=edge_index.dtype)
        ei = jnp.concatenate([edge_index, jnp.stack([loops, loops], axis=0)], axis=1)
        src, dst = (ei[0], ei[1])
        h = (x @ W).reshape(n, H, C)
        a_src = jnp.sum(h * att_src, axis=-1)
        a_dst = jnp.sum(h * att_dst, axis=-1)
        alpha = jax.nn.leaky_relu(a_src[src] + a_dst[dst], NEG_SLOPE)
        amax = jax.ops.segment_max(alpha, dst, num_segments=n)
        amax = jnp.where(jnp.isfinite(amax), amax, 0.0)
        ex = jnp.exp(alpha - amax[dst])
        denom = jax.ops.segment_sum(ex, dst, num_segments=n)
        coef = ex / (denom[dst] + 1e-16)
        msg = h[src] * coef[:, :, None]
        out = jax.ops.segment_sum(msg, dst, num_segments=n)
        return out.reshape(n, H * C) + bias

    def _L0_mix_ref(x, Wq, Wk, Wv, Wm, W1, W2, g1, b1, g2, b2):
        import jax, jax.numpy as jnp
        import numpy as np
        NHEAD = 8
        ATT_EPS = 1e-06
        LN_EPS = 1e-05

        def _layernorm(x, g, b):
            mu = jnp.mean(x, axis=-1, keepdims=True)
            var = jnp.mean(jnp.square(x - mu), axis=-1, keepdims=True)
            return (x - mu) * jax.lax.rsqrt(var + LN_EPS) * g + b
        N, L, C = x.shape
        H = NHEAD
        D = C // H
        q = (x @ Wq).reshape(N, L, H, D)
        k = (x @ Wk).reshape(N, L, H, D)
        v = (x @ Wv).reshape(N, L, H, D)
        Q = jax.nn.elu(q) + 1.0
        K = jax.nn.elu(k) + 1.0
        v = v / L
        KV = jnp.einsum('nshd,nshv->nhdv', K, v)
        Z = 1.0 / (jnp.einsum('nlhd,nhd->nlh', Q, K.sum(axis=1)) + ATT_EPS)
        msg = jnp.einsum('nlhd,nhdv,nlh->nlhv', Q, KV, Z) * L
        msg = msg.reshape(N, L, C) @ Wm
        msg = _layernorm(msg, g1, b1)
        h = jnp.concatenate([x, msg], axis=-1) @ W1
        h = jax.nn.relu(h) @ W2
        msg = _layernorm(h, g2, b2)
        return x + msg

    def _L0_ffn_ref(x, W_fx, b_fx, W_x, b_x, W_slice, b_slice, W_q, W_k, W_v, W_out, b_out, temperature):
        import jax, jax.numpy as jnp
        import numpy as np
        DIM = 256
        H = 8
        D = 64
        G = 64
        INNER = H * D
        SCALE = D ** (-0.5)
        B, N, _ = x.shape
        fx_mid = (x @ W_fx + b_fx).reshape(B, N, H, D).transpose(0, 2, 1, 3)
        x_mid = (x @ W_x + b_x).reshape(B, N, H, D).transpose(0, 2, 1, 3)
        temp = jnp.clip(temperature, 0.1, 5.0)
        slice_weights = jax.nn.softmax((x_mid @ W_slice + b_slice) / temp, axis=-1)
        slice_norm = slice_weights.sum(axis=2)
        slice_token = jnp.einsum('bhnc,bhng->bhgc', fx_mid, slice_weights)
        slice_token = slice_token / (slice_norm[..., None] + 1e-05)
        q = slice_token @ W_q
        k = slice_token @ W_k
        v = slice_token @ W_v
        attn = jax.nn.softmax(jnp.einsum('bhgc,bhkc->bhgk', q, k) * SCALE, axis=-1)
        out_slice = jnp.einsum('bhgk,bhkc->bhgc', attn, v)
        out_x = jnp.einsum('bhgc,bhng->bhnc', out_slice, slice_weights)
        out_x = out_x.transpose(0, 2, 1, 3).reshape(B, N, INNER)
        return out_x @ W_out + b_out
    edge_index = jnp.stack([src, dst])
    xn = _layernorm(x, axis=-1)
    x = x + _L0_gnn_ref(xn, edge_index, L0_gnn_W, L0_gnn_att_src, L0_gnn_att_dst, L0_gnn_bias) + _L0_mix_ref(xn[None], L0_mix_Wq, L0_mix_Wk, L0_mix_Wv, L0_mix_Wm, L0_mix_W1, L0_mix_W2, L0_mix_g1, L0_mix_b1, L0_mix_g2, L0_mix_b2)[0]
    x = x + _L0_ffn_ref(_layernorm(x, axis=-1)[None], L0_ffn_W_fx, L0_ffn_b_fx, L0_ffn_W_x, L0_ffn_b_x, L0_ffn_W_slice, L0_ffn_b_slice, L0_ffn_W_q, L0_ffn_W_k, L0_ffn_W_v, L0_ffn_W_out, L0_ffn_b_out, L0_ffn_temperature)[0]
    return x

_drawn_inputs = setup_inputs


def setup_inputs(seed=0):
    import zlib

    import numpy as np

    out = dict(_drawn_inputs(seed))
    spreads = {'L0_gnn_bias': (0.0, 0.1),
     'L0_mix_g1': (1.0, 0.2),
     'L0_mix_b1': (0.0, 0.1),
     'L0_mix_g2': (1.0, 0.2),
     'L0_mix_b2': (0.0, 0.1),
     'L0_ffn_b_fx': (0.0, 0.1),
     'L0_ffn_b_x': (0.0, 0.8),
     'L0_ffn_b_slice': (0.0, 0.8),
     'L0_ffn_b_out': (0.0, 0.1),
     'L0_ffn_temperature': (0.5, 0.6)}
    factors = {'L0_gnn_att_dst': 3.935,
     'L0_ffn_W_x': 8.0,
     'L0_ffn_W_slice': 8.0,
     'L0_ffn_W_q': 8.0,
     'L0_ffn_W_k': 8.0}
    for name, (base, spread) in spreads.items():
        noise = np.random.default_rng([zlib.crc32(name.encode()), seed]).standard_normal(out[name].shape)
        drawn = base * np.exp(spread * noise) if base else spread * noise
        out[name] = jnp.asarray(drawn.astype(out[name].dtype))
    for name, factor in factors.items():
        out[name] = (out[name] * factor).astype(out[name].dtype)
    return out
```

```python
import concourse.bass as bass
from concourse import mybir
from contextlib import ExitStack

F32 = mybir.dt.float32
I32 = mybir.dt.int32
ALU = mybir.AluOpType
ACT = mybir.ActivationFunctionType
X = mybir.AxisListType.X

N, E, D = 6250, 200000, 256
H, C = 8, 32
P = 125
NT = N // P
KD = D // 128
CW = C + 1
ROW = H * CW
W1C = NT + 1
T = 4
GE = 128 * T
NG = 448
assert NG >= -(-E // GE) + NT
B = 4
NB = NG // B
HALF = E // P
FH, FD = 8, 64
INNER = FH * FD
BIG = 1.0e38
SLOPE = 0.2
LN_EPS = 1e-5
MIX_EPS = 1e-6
TOK_EPS = 1e-5
DEN_EPS = 1e-16
MW = ROW + H + 1


def program(nc, x, src, dst, gnn_W, att_src, att_dst, gnn_bias, Wq, Wk, Wv, Wm, W1, W2, g1, b1, g2, b2,
            W_fx, b_fx, W_x, b_x, W_slice, b_slice, W_q, W_k, W_v, W_out, b_out, temperature, out):
    h_tab = nc.dram_tensor("h_tab", (N, ROW), F32, kind="Internal").ap()
    rec = nc.dram_tensor("rec", (E + GE, 4), I32, kind="Internal").ap()
    pen = nc.dram_tensor("pen", (E + GE + 8,), F32, kind="Internal").ap()
    xnT_d = nc.dram_tensor("xnT_d", (NT + 2, 128, KD * P), F32, kind="Internal").ap()
    mix_d = nc.dram_tensor("mix_d", (N, D), F32, kind="Internal").ap()
    xpx_d = nc.dram_tensor("xpx_d", (N, D), F32, kind="Internal").ap()
    swT_d = nc.dram_tensor("swT_d", (NT, 128, 4 * P), F32, kind="Internal").ap()

    top = ExitStack()

    def sb(ctx, name, shape, dt=F32):
        return ctx.enter_context(nc.sbuf_tensor(name, shape, dt))

    def ps(ctx, name, shape=(128, 512)):
        return ctx.enter_context(nc.psum_tensor(name, list(shape), F32))

    def sem(ctx, name):
        return ctx.enter_context(nc.semaphore(name))

    def linker(eng, s, base=0):
        n = [0]

        def link(ins):
            n[0] += 1
            ins.then_inc(s, 1)
            eng.wait_ge(s, base + n[0])
        link.count = n
        return link

    with top:
        ident = sb(top, "ident", [128, 128])
        ones = sb(top, "ones", [128, 128])
        iota_d = sb(top, "iota_d", [128, P])
        wbase = sb(top, "wbase", [128, NG])
        sched = sb(top, "sched", [1, 2, NG], I32)
        acc = sb(top, "acc", [P, W1C, ROW])
        ad_all = sb(top, "ad_all", [P, W1C, H])
        m_run = sb(top, "m_run", [P, W1C, H])
        wkv = sb(top, "wkv", [128, KD, 2 * D])
        wq = sb(top, "wq", [128, KD, D])
        wm = sb(top, "wm", [128, KD, D])
        w1 = sb(top, "w1", [128, 2 * KD, 2 * D])
        bias1 = sb(top, "bias1", [128, 4])
        w2 = sb(top, "w2", [128, 2 * KD, D])
        rows = sb(top, "rows", [P, 4, D])
        wc = sb(top, "wc", [128, KD, INNER])
        bc = sb(top, "bc", [P, INNER])

        prologue(nc, sb, ps, sem, linker, locals())
        edges_and_mix(nc, sb, ps, sem, linker, locals())
        slices(nc, sb, ps, sem, linker, locals())


def prologue(nc, sb, ps, sem, linker, v):
    x, src, dst = v["x"], v["src"], v["dst"]
    ident, ones, iota_d, wbase, sched = v["ident"], v["ones"], v["iota_d"], v["wbase"], v["sched"]
    acc, ad_all, m_run = v["acc"], v["ad_all"], v["m_run"]
    h_tab, rec, pen, xnT_d, xpx_d = v["h_tab"], v["rec"], v["pen"], v["xnT_d"], v["xpx_d"]
    wkv, wq, wm, w1, w2, rows, bias1, wc, bc = (v[k] for k in "wkv wq wm w1 w2 rows bias1 wc bc".split())
    with ExitStack() as ctx:
        wg = sb(ctx, "wg", [128, KD, ROW + H])
        wraw = sb(ctx, "wraw", [128, KD, D])
        att = sb(ctx, "att", [128, 2, D])
        prod = sb(ctx, "prod", [128, 2, KD, D])
        src_i = sb(ctx, "src_i", [P, HALF], I32)
        dst_i = sb(ctx, "dst_i", [P, HALF + 1], I32)
        dst_f = sb(ctx, "dst_f", [P, HALF + 1])
        start = sb(ctx, "start", [P, HALF])
        recs = sb(ctx, "recs", [P, HALF, 4], I32)
        pad = sb(ctx, "pad", [128, T, 4], I32)
        padp = sb(ctx, "padp", [1, GE + 8])
        junk = sb(ctx, "junk", [P, HALF], mybir.dt.bfloat16)
        cnt = sb(ctx, "cnt", [P, W1C])
        cdiff = sb(ctx, "cdiff", [P, W1C])
        thr = sb(ctx, "thr", [P, W1C])
        iota_g = sb(ctx, "iota_g", [W1C, NG])
        iota_k = sb(ctx, "iota_k", [W1C, E // GE + 1])
        kjunk = sb(ctx, "kjunk", [W1C, E // GE + 1])
        wcol = sb(ctx, "wcol", [W1C, 1])
        wrep = sb(ctx, "wrep", [W1C, 128])
        below = sb(ctx, "below", [W1C, W1C])
        big50 = sb(ctx, "big50", [W1C, 1])
        cols = sb(ctx, "cols", [W1C, 6])
        ind = sb(ctx, "ind", [W1C, NG])
        ind2 = sb(ctx, "ind2", [W1C, NG])
        sch_f = sb(ctx, "sch_f", [1, 3, NG])
        xn = sb(ctx, "xn", [P, 2, D])
        xpx = sb(ctx, "xpx", [P, 2, D])
        st6 = sb(ctx, "st6", [P, 2, 6])
        mv = sb(ctx, "mv", [P, 2, 2])
        lnv = sb(ctx, "lnv", [P, 2, 1])
        rstd = sb(ctx, "rstd", [P, 2, 1])
        nb = sb(ctx, "nb", [P, 2, 1])
        xnT = sb(ctx, "xnT", [128, 2, KD * P])
        vcols = sb(ctx, "vcols", [128, 2, KD])
        wx = sb(ctx, "wx", [128, KD, INNER])
        wxT = sb(ctx, "wxT", [128, 4, D])
        wsl = sb(ctx, "wsl", [128, 128])
        bxc = sb(ctx, "bxc", [128, 4])
        brow = sb(ctx, "brow", [1, INNER])
        bsl = sb(ctx, "bsl", [1, FD])
        tmp1 = sb(ctx, "tmp1", [1, FH])
        itemp = sb(ctx, "itemp", [128, FH])
        zcol = sb(ctx, "zcol", [128, 2])
        psT = [ps(ctx, f"pA_T{i}") for i in range(2)]
        psH = [ps(ctx, f"pA_H{i}") for i in range(2)]
        psS = ps(ctx, "pA_S")
        psW = ps(ctx, "pA_W")
        psR = ps(ctx, "pA_R")
        psX = ps(ctx, "pA_X")

        edges_in = sem(ctx, "edges_in")
        weights_in = sem(ctx, "weights_in")
        late_in = sem(ctx, "late_in")
        x_in = sem(ctx, "x_in")
        x_read = sem(ctx, "x_read")
        xn_free = sem(ctx, "xn_free")
        xnT_free = sem(ctx, "xnT_free")
        consts = sem(ctx, "consts")
        dstf_ready = sem(ctx, "dstf_ready")
        recs_ready = sem(ctx, "recs_ready")
        pool_chain = sem(ctx, "pool_chain")
        dve_chain = sem(ctx, "dve_chain")
        pro_out = sem(ctx, "pro_out")
        var_ready = sem(ctx, "var_ready")
        lnv_ready = sem(ctx, "lnv_ready")
        rstd_ready = sem(ctx, "rstd_ready")
        xn_ready = sem(ctx, "xn_ready")
        xpx_ready = sem(ctx, "xpx_ready")
        xpx_out = sem(ctx, "xpx_out")
        xT_done = sem(ctx, "xT_done")
        xnT_ready = sem(ctx, "xnT_ready")
        xnT_out = sem(ctx, "xnT_out")
        wg_ready = sem(ctx, "wg_ready")
        h_done = sem(ctx, "h_done")
        h_saved = sem(ctx, "h_saved")
        ad_saved = sem(ctx, "ad_saved")
        tab_out = sem(ctx, "tab_out")
        cnt_ready = sem(ctx, "cnt_ready")
        pe_s = sem(ctx, "sched_products")
        dve_s = sem(ctx, "sched_steps")
        pe_w = sem(ctx, "weight_products")
        dve_w = sem(ctx, "weight_steps")
        act_chain = sem(ctx, "act_chain")

        apart = sem(ctx, "apart")
        block = ctx.enter_context(nc.Block())

        @block.sync
        def _(sp):
            sp.dma_start(wraw[:], v["gnn_W"].rearrange("(k p) n -> p k n", p=128)).then_inc(weights_in, 16)
            sp.dma_start(att[:, 0, :], v["att_src"].rearrange("h c -> (h c)").partition_broadcast(128)).then_inc(weights_in, 16)
            sp.dma_start(att[:, 1, :], v["att_dst"].rearrange("h c -> (h c)").partition_broadcast(128)).then_inc(weights_in, 16)
            sp.dma_start(acc[:, 0:NT, 0:D], x.rearrange("(t p) n -> p t n", p=P)).then_inc(x_in, 16)
            with sp.Fori(0, NT // 2) as it:
                for u in range(2):
                    n = it * 2 + u
                    sp.wait_ge(xnT_ready, n + 1)
                    sp.dma_start(xnT_d[bass.ds(n, 1), :, :].rearrange("a p n -> (a p) n"), xnT[:, u, :]).then_inc(xnT_out, 16)
                    sp.wait_ge(h_saved, n + 1)
                    sp.dma_start(h_tab[bass.ds(n * P, P), :],
                                 acc[:, bass.ds(n, 1), :].rearrange("p a n -> p (a n)")).then_inc(tab_out, 16)
                sp.wait_ge(xnT_out, it * 32 + 32)
                sp.sem_inc(xnT_free, 2)
            sp.wait_ge(tab_out, 16 * NT)
            sp.dma_start(xnT_d[NT:NT + 2, :, :], xnT_d[0:2, :, :]).then_inc(xnT_out, 16)
            sp.wait_ge(xnT_out, 16 * (NT + 1))

        @block.gpsimd
        def _(pool):
            link = linker(pool, pool_chain)
            g = nc.gpsimd
            g.memset(dst_i[0:1, 0:1], -1).then_inc(consts, 1)
            pool.wait_ge(consts, 1)
            pool.dma_start(src_i[:], src.rearrange("(p n) -> p n", p=P)).then_inc(edges_in, 16)
            pool.dma_start(dst_i[:, 1:], dst.rearrange("(p n) -> p n", p=P)).then_inc(edges_in, 16)
            pool.dma_start(dst_i[1:P, 0:1], dst.rearrange("(p n) -> p n", p=P)[0:P - 1, HALF - 1:HALF],
                           allow_slow_non_contiguous=True).then_inc(edges_in, 16)
            link(g.memset(ident[:], 0.0))
            g.affine_select(out=ident[:], in_=ident[:], compare_op=ALU.not_equal, fill=1.0, base=0,
                            pattern=[[-1, 128]], channel_multiplier=1).then_inc(consts, 1)
            g.memset(ones[:], 1.0).then_inc(consts, 1)
            g.iota(iota_d[:], [[1, P]], base=0, channel_multiplier=0, allow_small_or_imprecise_dtypes=True).then_inc(consts, 1)
            g.iota(thr[:], [[P, W1C]], base=0, channel_multiplier=0, allow_small_or_imprecise_dtypes=True).then_inc(consts, 1)
            g.iota(iota_g[:], [[1, NG]], base=0, channel_multiplier=0, allow_small_or_imprecise_dtypes=True).then_inc(consts, 1)
            g.iota(iota_k[:], [[GE, E // GE + 1]], base=0, channel_multiplier=0, allow_small_or_imprecise_dtypes=True).then_inc(consts, 1)
            g.iota(wcol[:], [[0, 1]], base=0, channel_multiplier=1, allow_small_or_imprecise_dtypes=True).then_inc(consts, 1)
            g.iota(wrep[:], [[0, 128]], base=0, channel_multiplier=P, allow_small_or_imprecise_dtypes=True).then_inc(consts, 1)
            link(g.memset(below[:], 1.0))
            g.affine_select(out=below[:], in_=below[:], compare_op=ALU.is_gt, fill=0.0, base=0,
                            pattern=[[1, W1C]], channel_multiplier=-1).then_inc(consts, 1)
            link(g.memset(big50[:], 0.0))
            g.affine_select(out=big50[:], in_=big50[:], compare_op=ALU.not_equal, fill=1.0e6, base=-NT,
                            pattern=[[0, 1]], channel_multiplier=1).then_inc(consts, 1)
            g.memset(zcol[:], LN_EPS).then_inc(consts, 1)
            g.memset(acc[:, NT, :], 0.0)
            g.memset(ad_all[:, NT, :], 0.0)
            g.memset(m_run[:, NT, :], 0.0)
            g.memset(wsl[:], 0.0).then_inc(consts, 1)
            g.memset(pad[:, :, 0], 0)
            g.memset(pad[:, :, 1].bitcast(F32), -1.0)
            g.memset(pad[:, :, 2].bitcast(F32), 1.0)
            g.memset(pad[:, :, 3], 0)
            link(g.memset(padp[:], -BIG))
            pool.dma_start(rec[E:E + GE, :].rearrange("(p t) f -> p (t f)", p=128), pad[:].rearrange("p t f -> p (t f)")).then_inc(pro_out, 16)
            pool.dma_start(pen[E:E + GE + 8].rearrange("(a n) -> a n", a=1), padp[:]).then_inc(pro_out, 16)
            pool.wait_ge(edges_in, 48)
            g.tensor_copy(dst_f[:], dst_i[:]).then_inc(dstf_ready, 1)
            pool.wait_ge(dstf_ready, 1)
            link(g.tensor_tensor(start[:], dst_f[:, 1:], dst_f[:, :HALF], ALU.subtract))
            link(g.tensor_scalar(start[:], start[:], 0.0, None, ALU.is_gt))
            g.tensor_copy(recs[:, :, 0], src_i[:])
            g.tensor_copy(recs[:, :, 1].bitcast(F32), dst_f[:, 1:])
            g.memset(recs[:, :, 3], 0)
            link(g.tensor_copy(recs[:, :, 2].bitcast(F32), start[:]))
            pool.dma_start(rec[0:E, :].rearrange("(p n) f -> p (n f)", p=P), recs[:].rearrange("p n f -> p (n f)")).then_inc(pro_out, 16)
            link(g.tensor_scalar(start[:], start[:], -BIG, None, ALU.mult))
            pool.dma_start(pen[0:E].rearrange("(p n) -> p n", p=P), start[:]).then_inc(pro_out, 16)
            with pool.Fori(0, NT // 2) as it:
                for u in range(2):
                    n = it * 2 + u
                    pool.wait_ge(xn_ready, n + 1)
                    g.tensor_tensor(xpx[:, u, :], acc[:, bass.ds(n, 1), 0:D].rearrange("p a n -> p (a n)"), xn[:, u, :], ALU.add).then_inc(xpx_ready, 1)
                    pool.wait_ge(xpx_ready, n + 1)
                    pool.sem_inc(x_read, 1)
                    pool.dma_start(xpx_d[bass.ds(n * P, P), :], xpx[:, u, :]).then_inc(xpx_out, 16)
                pool.wait_ge(xpx_out, it * 32 + 32)
                pool.sem_inc(xn_free, 2)
            pool.wait_ge(pro_out, 64)

        @block.scalar
        def _(act):
            s = nc.scalar
            act.preload_act_table_set("natural_log_exp_and_others")
            act.sem_inc(xnT_free, 2)
            act.sem_inc(xn_free, 2)

            def load(dstt, srca):
                act.dma_start(dstt, srca).then_inc(late_in, 16)
            load(wkv[:, :, 0:D], v["Wk"].rearrange("(k p) n -> p k n", p=128))
            load(wkv[:, :, D:], v["Wv"].rearrange("(k p) n -> p k n", p=128))
            load(wq[:], v["Wq"].rearrange("(k p) n -> p k n", p=128))
            load(wm[:], v["Wm"].rearrange("(k p) n -> p k n", p=128))
            load(w1[:], v["W1"].rearrange("(k p) n -> p k n", p=128))
            load(w2[:], v["W2"].rearrange("(k p) n -> p k n", p=128))
            for i, r in enumerate(("gnn_bias", "g2", "b2", "b_out")):
                load(rows[:, i, :], v[r].partition_broadcast(P))
            with nc.allow_non_contiguous_dma(reason="a few columns"):
                load(vcols[:, 0, :], v["g1"].rearrange("(k p) -> p k", p=128))
                load(vcols[:, 1, :], v["b1"].rearrange("(k p) -> p k", p=128))
                load(bxc[:], v["b_x"].rearrange("(k p) -> p k", p=128))
            load(wx[:], v["W_x"].rearrange("(k p) n -> p k n", p=128))
            act.wait_ge(consts, 13)
            load(wsl[0:FD, 0:FD], v["W_slice"])
            load(wsl[FD:, FD:], v["W_slice"])
            load(bsl[:], v["b_slice"].rearrange("(a n) -> a n", a=1))
            load(itemp[:], v["temperature"].rearrange("a h b c -> (a h b c)").partition_broadcast(128))
            with act.Fori(0, NT // 2) as it:
                for u in range(2):
                    n = it * 2 + u
                    act.wait_ge(var_ready, n + 1)
                    s.activation(lnv[:, u, :], mv[:, u, 1:2], ACT.Ln, bias=zcol[0:P, 0:1]).then_inc(lnv_ready, 1)
                    act.wait_ge(lnv_ready, n + 1)
                    s.activation(rstd[:, u, :], lnv[:, u, :], ACT.Exp, scale=-0.5).then_inc(rstd_ready, 1)
                for u in range(2):
                    n = it * 2 + u
                    act.wait_ge(xT_done, n + 1)
                    act.wait_ge(xnT_free, n + 1)
                    s.activation(xnT[:, u, :], psT[u][:, 0:KD * P], ACT.Copy).then_inc(xnT_ready, 1)
                for u in range(2):
                    n = it * 2 + u
                    act.wait_ge(h_done, n + 1)
                    act.wait_ge(x_read, n + 1)
                    s.activation(acc[:, bass.ds(n, 1), :].rearrange("p a n -> p (a n)"), psH[u][0:P, 0:ROW], ACT.Copy).then_inc(h_saved, 1)
                    s.activation(ad_all[:, bass.ds(n, 1), :].rearrange("p a n -> p (a n)"), psH[u][0:P, ROW:ROW + H], ACT.Copy).then_inc(ad_saved, 1)

        @block.vector
        def _(dve):
            d = nc.vector
            link = linker(dve, dve_chain)
            dve.wait_ge(weights_in, 48)
            for i in range(2):
                for k in range(KD):
                    d.tensor_tensor(prod[:, i, k, :], wraw[:, k, :], att[:, i, :], ALU.mult)
            wgv = wg[:, :, 0:ROW].rearrange("p k (h c) -> p k h c", c=CW)
            for k in range(KD):
                last = d.tensor_copy(wgv[:, k, :, 0:C], wraw[:, k, :].rearrange("p (h c) -> p h c", c=C))
            link(last)
            for k in range(KD):
                d.tensor_reduce(wgv[:, k, :, C], prod[:, 0, k, :].rearrange("p (h c) -> p h c", c=C), axis=X, op=ALU.add)
                last = d.tensor_reduce(wg[:, k, ROW:], prod[:, 1, k, :].rearrange("p (h c) -> p h c", c=C), axis=X, op=ALU.add)
            last.then_inc(wg_ready, 1)
            K = 2 * 2
            dve.wait_ge(x_in, 16)
            base0 = link.count[0]
            with dve.Fori(0, NT // 2) as it:
                lk = linker(dve, dve_chain, it * K + base0)
                for u in range(2):
                    n = it * 2 + u
                    lk(d.bn_stats(st6[:, u, :], acc[:, bass.ds(n, 1), 0:D].rearrange("p a n -> p (a n)")))
                    dve.sem_inc(apart, 1)
                    d.bn_aggr(mv[:, u, :], st6[:, u, :]).then_inc(var_ready, 1)
                for u in range(2):
                    n = it * 2 + u
                    dve.wait_ge(var_ready, n + 1)
                    dve.wait_ge(rstd_ready, n + 1)
                    lk(d.scalar_tensor_tensor(nb[:, u, :], mv[:, u, 0:1], -1.0, rstd[:, u, :], ALU.mult, ALU.mult))
                    dve.wait_ge(xn_free, n + 1)
                    d.tensor_scalar(xn[:, u, :], acc[:, bass.ds(n, 1), 0:D].rearrange("p a n -> p (a n)"), rstd[:, u, :], nb[:, u, :], ALU.mult, ALU.add).then_inc(xn_ready, 1)
                assert lk.count[0] == K
            link.count[0] = base0 + K * (NT // 2)
            dve.wait_ge(dstf_ready, 1)
            dve.wait_ge(consts, 13)
            with dve.Fori(0, W1C) as w:
                d.tensor_scalar(junk[:], dst_f[:, 1:], thr[:, bass.ds(w, 1)], 0.0, ALU.is_lt, ALU.add,
                                accum_out=cnt[:, bass.ds(w, 1)]).then_inc(cnt_ready, 1)
                dve.wait_ge(cnt_ready, w + 1)
            link(d.memset(cdiff[:, NT:], 0.0))
            d.tensor_tensor(cdiff[:, 0:NT], cnt[:, 1:], cnt[:, 0:NT], ALU.subtract).then_inc(dve_s, 1)
            dve.wait_ge(pe_s, 1)
            link(d.tensor_copy(cols[:, 0:2], psS[0:W1C, 0:2]))
            d.tensor_scalar(kjunk[:], iota_k[:], cols[:, 1:2], 0.0, ALU.is_lt, ALU.add, accum_out=cols[:, 2:3]).then_inc(dve_s, 1)
            dve.wait_ge(dve_s, 2)
            dve.wait_ge(pe_s, 2)
            link(d.tensor_copy(cols[:, 3:4], psS[0:W1C, 2:3]))
            link(d.scalar_tensor_tensor(cols[:, 4:5], cols[:, 3:4], cols[:, 2:3], big50[:], ALU.add, ALU.add))
            d.tensor_scalar(ind[:], iota_g[:], cols[:, 3:4], None, ALU.is_ge)
            link(d.tensor_scalar(ind2[:], iota_g[:], cols[:, 4:5], None, ALU.is_ge))
            link(d.scalar_tensor_tensor(cols[:, 5:6], cols[:, 3:4], float(-GE), cols[:, 0:1], ALU.mult, ALU.add))
            link(d.tensor_tensor(ind[:], ind[:], ind2[:], ALU.subtract))
            dve.sem_inc(dve_s, 1)
            dve.wait_ge(pe_s, 3)
            link(d.scalar_tensor_tensor(sch_f[:, 0, :], iota_g[0:1, :], float(GE), psS[0:1, 0:NG], ALU.mult, ALU.add))
            link(d.tensor_scalar(sch_f[:, 1, :], sch_f[:, 0, :], float(E), None, ALU.min))
            d.tensor_copy(sched[:, 0, :], sch_f[:, 1, :])
            dve.wait_ge(pe_s, 4)
            link(d.tensor_copy(sched[:, 1, :], psR[0:1, 0:NG]))
            dve.wait_ge(pe_s, 5)
            link(d.tensor_copy(wbase[:], psX[:, 0:NG]))
            dve.wait_ge(ad_saved, NT)
            dve.wait_ge(h_saved, NT)
            accv = acc[:].rearrange("p w (h c) -> p w h c", c=CW)
            link(d.tensor_tensor(m_run[:, 0:NT, :], accv[:, 0:NT, :, C], ad_all[:, 0:NT, :], ALU.add))
            link(d.scalar_tensor_tensor(m_run[:, 0:NT, :], m_run[:, 0:NT, :], SLOPE, m_run[:, 0:NT, :], ALU.mult, ALU.max))
            dve.wait_ge(tab_out, 16 * NT)
            link(d.memset(accv[:, 0:NT, :, C], 1.0))
            dve.wait_ge(late_in, 16 * 18)
            link(d.tensor_scalar(itemp[:], itemp[:], 0.1, 5.0, ALU.max, ALU.min))
            link(d.reciprocal(itemp[:], itemp[:]))
            dve.wait_ge(pe_w, 1)
            link(d.tensor_copy(bias1[:], psW[:, 0:4]))
            for k in range(KD):
                d.tensor_scalar(w1[:, KD + k, :], w1[:, KD + k, :], vcols[:, 0, k:k + 1], None, ALU.mult)
            for k in range(KD):
                dve.wait_ge(pe_w, 2 + 2 * k)
                link(d.tensor_copy(wxT[:, :, k * 128:(k + 1) * 128], psT[k][:, :].rearrange("p (j n) -> p j n", j=4)))
                dve.sem_inc(dve_w, 1)
                dve.wait_ge(pe_w, 3 + 2 * k)
                d.tensor_tensor(wc[:, k, :].rearrange("p (h g) -> p h g", g=FD), psH[k][:, :].rearrange("p (h g) -> p h g", g=FD),
                                itemp[:, :].unsqueeze(2).broadcast_to([128, FH, FD]), ALU.mult)
            dve.wait_ge(pe_w, 6)
            bv = brow[:].rearrange("p (h g) -> p h g", g=FD)
            link(d.tensor_tensor(bv, psW[0:1, :].rearrange("p (h g) -> p h g", g=FD),
                                 bsl[:].unsqueeze(1).broadcast_to([1, FH, FD]), ALU.add))
            link(d.tensor_tensor(bv, bv, itemp[0:1, :].unsqueeze(2).broadcast_to([1, FH, FD]), ALU.mult))
            dve.sem_inc(dve_w, 1)
            dve.wait_ge(pe_w, 7)
            link(d.tensor_copy(bc[:], psW[0:P, :]))

        @block.tensor
        def _(pe):
            t = nc.tensor
            pe.wait_ge(consts, 13)
            pe.wait_ge(wg_ready, 1)
            with pe.Fori(0, NT // 2) as it:
                for u in range(2):
                    n = it * 2 + u
                    pe.wait_ge(xn_ready, n + 1)
                    for k in range(KD):
                        last = t.transpose(psT[u][:, k * P:(k + 1) * P], xn[:, u, k * 128:(k + 1) * 128], ident[0:P, 0:P])
                    last.then_inc(xT_done, 1)
                for u in range(2):
                    n = it * 2 + u
                    pe.wait_ge(xnT_ready, n + 1)
                    for k in range(KD):
                        last = t.matmul(psH[u][0:P, 0:ROW + H], xnT[:, u, k * P:(k + 1) * P], wg[:, k, :], start=(k == 0), stop=(k == KD - 1))
                    last.then_inc(h_done, 1)
            pe.wait_ge(late_in, 16 * 18)
            for m in range(4):
                for k in range(KD):
                    last = t.matmul(psW[:, m:m + 1], w1[:, KD + k, m * 128:(m + 1) * 128], vcols[:, 1, k:k + 1], start=(k == 0), stop=(k == KD - 1))
            last.then_inc(pe_w, 1)
            pe.wait_ge(dve_s, 1)
            t.matmul(psS[0:W1C, 0:1], cnt[:], ones[0:P, 0:1], start=True, stop=True)
            t.matmul(psS[0:W1C, 1:2], cdiff[:], ones[0:P, 0:1], start=True, stop=True).then_inc(pe_s, 1)
            pe.wait_ge(dve_s, 2)
            t.matmul(psS[0:W1C, 2:3], below[:], cols[:, 2:3], start=True, stop=True).then_inc(pe_s, 1)
            pe.wait_ge(dve_s, 3)
            t.matmul(psS[0:1, 0:NG], cols[:, 5:6], ind[:], start=True, stop=True).then_inc(pe_s, 1)
            t.matmul(psR[0:1, 0:NG], wcol[:], ind[:], start=True, stop=True).then_inc(pe_s, 1)
            t.matmul(psX[:, 0:NG], wrep[:], ind[:], start=True, stop=True).then_inc(pe_s, 1)
            pe.wait_ge(h_saved, NT)
            pe.wait_ge(ad_saved, NT)
            for k in range(KD):
                for j in range(4):
                    last = t.transpose(psT[k][:, j * 128:(j + 1) * 128], wx[:, k, j * 128:(j + 1) * 128], ident[:])
                last.then_inc(pe_w, 1)
                pe.wait_ge(dve_w, k + 1)
                for j in range(4):
                    last = t.matmul(psH[k][:, j * 128:(j + 1) * 128], wxT[:, j, k * 128:(k + 1) * 128], wsl[:], start=True, stop=True)
                last.then_inc(pe_w, 1)
            for j in range(4):
                last = t.matmul(psW[0:1, j * 128:(j + 1) * 128], bxc[:, j:j + 1], wsl[:], start=True, stop=True)
            last.then_inc(pe_w, 1)
            pe.wait_ge(dve_w, 3)
            t.matmul(psW[0:P, :], ones[0:1, 0:P], brow[:], start=True, stop=True).then_inc(pe_w, 1)


def edges_and_mix(nc, sb, ps, sem, linker, v):
    ident, ones, iota_d, wbase, sched = v["ident"], v["ones"], v["iota_d"], v["wbase"], v["sched"]
    acc, ad_all, m_run = v["acc"], v["ad_all"], v["m_run"]
    h_tab, rec, pen, xnT_d, xpx_d, mix_d = v["h_tab"], v["rec"], v["pen"], v["xnT_d"], v["xpx_d"], v["mix_d"]
    wkv, wq, wm, w1, w2, rows, bias1 = (v[k] for k in "wkv wq wm w1 w2 rows bias1".split())
    BT = B * T
    HB = H * B
    KV1, KV2, PLAIN = range(3)
    with ExitStack() as ctx:
        ring = [sb(ctx, f"ring{i}", [128, BT, MW]) for i in range(2)]
        recs = [sb(ctx, f"recb{i}", [128, B, T * 4], I32) for i in range(2)]
        pens = [sb(ctx, f"penb{i}", [HB, GE + 1]) for i in range(2)]
        oh = [sb(ctx, f"oh{i}", [128, BT, P]) for i in range(2)]
        ohT = [sb(ctx, f"ohT{i}", [P, GE]) for i in range(2)]
        adst = sb(ctx, "adst", [P, B, H])
        dloc = sb(ctx, "dloc", [128, B, T])
        first = sb(ctx, "first", [128, B, T])
        asc = sb(ctx, "asc", [128, T, B * H])
        scf = sb(ctx, "scf", [HB, GE])
        scb = sb(ctx, "scb", [HB, GE])
        ad_e = sb(ctx, "ad_e", [128, BT, H])
        zz = sb(ctx, "zz", [128, 2, BT, H])
        df = sb(ctx, "df", [128, BT, H])
        part = [sb(ctx, f"part{i}", [P, B, MW]) for i in range(2)]
        pm = sb(ctx, "pm", [P, B, 1])
        sg = sb(ctx, "sg", [P, B, H])
        mns = sb(ctx, "mns", [P, B, H])
        dd = sb(ctx, "dd", [P, 2, B, H])
        ww = sb(ctx, "ww", [P, 2, B, H])
        xm = [sb(ctx, f"xm{i}", [128, KD * P]) for i in range(2)]
        xr = [sb(ctx, f"xr{i}", [P, D]) for i in range(2)]
        mo = [sb(ctx, f"mo{i}", [P, D]) for i in range(2)]
        kq = sb(ctx, "kq", [128, KD * 128])
        kmin = sb(ctx, "kmin", [128, KD * 128])
        kex = sb(ctx, "kex", [128, KD * 128])
        kk = sb(ctx, "kk", [128, KD * 128])
        vst = sb(ctx, "vst", [P, KD, 129])
        kvs = sb(ctx, "kvs", [128, KD, 129])
        kvd = sb(ctx, "kvd", [128, KD, 128])
        ksd = sb(ctx, "ksd", [128, KD, 128])
        den = sb(ctx, "den", [128, KD * P])
        msgT = sb(ctx, "msgT", [128, KD * P])
        st6 = sb(ctx, "st6b", [P, 6])
        mv = sb(ctx, "mvb", [P, 2])
        lnv = sb(ctx, "lnvb", [P, 1])
        rstd = sb(ctx, "rstdb", [P, 1])
        nb = sb(ctx, "nbb", [P, 1])
        n1 = sb(ctx, "n1", [P, D])
        n1T = sb(ctx, "n1T", [128, KD * P])
        hT = sb(ctx, "hT", [128, 4, P])
        n2 = sb(ctx, "n2", [P, D])
        zeros = sb(ctx, "zeros", [128, KD * 129])
        epsc = sb(ctx, "epsc", [128, 1])
        psT = ps(ctx, "pB_T")
        psE = ps(ctx, "pB_E")
        psO = [ps(ctx, f"pB_O{i}") for i in range(2)]
        psP = [ps(ctx, f"pB_P{i}") for i in range(2)]
        M0 = ps(ctx, "pB_M0")
        M1 = ps(ctx, "pB_M1")

        names = """asc_ready apart main_done asT_done scans_done sT_done eprep_done ex_done msg_ready part_saved
            oh_ready ad_staged ohT_done ohT_saved adE_done adE_saved dd_ready ww_ready chain small consts
            mixa_done mixa_saved kmin_ready kex_ready kk_ready mixb_done kvd_ready kv_closed msgT_ready mixc_done st1_ready
            rs1_ready n1_ready mixd_done n1T_ready mixe_done hT_ready mixf_done st2_ready rs2_ready mo_ready""".split()
        S = {n: sem(ctx, "e_" + n) for n in names}
        rec_in = [sem(ctx, f"rec_in{i}") for i in range(2)]
        pen_in = [sem(ctx, f"pen_in{i}") for i in range(2)]
        gathered = [sem(ctx, f"gathered{i}") for i in range(2)]
        xm_in = [sem(ctx, f"xm_in{i}") for i in range(2)]
        xr_in = [sem(ctx, f"xr_in{i}") for i in range(2)]
        mo_out = sem(ctx, "mo_out")
        block = ctx.enter_context(nc.Block())

        def steps(eng, body):
            with eng.Fori(0, NT // 2) as it:
                for u in range(2):
                    body(it * 2 + u, it, u, it * 2 + u, KV1, False)
            if between.get(eng.engine) is not None:
                between[eng.engine]()
            with eng.Fori(0, NT // 2) as it:
                for u in range(2):
                    body(it * 2 + u + NT, it + NT // 2, u, it * 2 + u, KV2, False)
            done = 2 * NT
            with eng.Fori(0, (NB - done) // 2 - 1) as it:
                for u in range(2):
                    body(it * 2 + u + done, it + NT, u, None, PLAIN, False)
            for u in range(2):
                body(NB - 2 + u, NB // 2 - 1, u, None, PLAIN, u == 1)

        between = {}

        def ringv(u):
            return ring[u][:, :, 0:ROW].rearrange("p t (h c) -> p t h c", c=CW)

        @block.sync
        def _(sp):
            def edge_loads(b, u):
                for g in range(B):
                    e0 = sp.value_load(sched[0:1, 0, bass.ds(b * B + g, 1)], min_val=0, max_val=E)
                    sp.dma_start(recs[u][:, g, :], rec[bass.ds(e0, GE), :].rearrange("(p t) f -> p (t f)", t=T)).then_inc(rec_in[u], 16)
                    sp.dma_start(pens[u][g * H:(g + 1) * H, :], pen[bass.ds(e0, GE + 1)].partition_broadcast(H)).then_inc(pen_in[u], 16)

            for u in range(2):
                edge_loads(u, u)
                sp.dma_start(xm[u][:], xnT_d[u, :, :]).then_inc(xm_in[u], 16)

            def step(b, k, u, n, kind, last):
                if kind == KV2:
                    sp.dma_start(xr[u][:], xpx_d[bass.ds(n * P, P), :]).then_inc(xr_in[u], 16)
                if not last and not (kind == PLAIN and isinstance(b, int)):
                    sp.wait_ge(S["eprep_done"], b + 1)
                    edge_loads(b + 2, u)
                if kind == KV1:
                    sp.wait_ge(S["mixa_done"], n + 1)
                    sp.dma_start(xm[u][:], xnT_d[bass.ds(n + 2, 1), :, :].rearrange("a p n -> (a p) n")).then_inc(xm_in[u], 16)
                if kind == KV2:
                    sp.wait_ge(S["mixe_done"], n + 1)
                    sp.dma_start(xm[u][:], xnT_d[bass.ds(n + 2, 1), :, :].rearrange("a p n -> (a p) n")).then_inc(xm_in[u], 16)
                    sp.wait_ge(S["mo_ready"], n + 1)
                    sp.dma_start(mix_d[bass.ds(n * P, P), :], mo[u][:]).then_inc(mo_out, 16)
            steps(sp, step)
            for u in range(2):
                sp.wait_ge(xm_in[u], 16 * (NT + 1))
            sp.wait_ge(mo_out, 16 * NT)

        @block.gpsimd
        def _(pool):
            def step(b, k, u, n, kind, last):
                pool.wait_ge(rec_in[u], k * (16 * B) + 16 * B)
                for g in range(B):
                    pool.wait_ge(S["main_done"], b * B + g + 1)
                    pool.sem_inc(S["apart"], 1)
                    for t in range(T):
                        pool.indirect_dma_start(out=ring[u][:, g * T + t, 0:ROW], out_offset=None, in_=h_tab[:, :],
                                                in_offset=bass.IndirectOffsetOnAxis(ap=recs[u][:, g, t * 4:t * 4 + 1], axis=0)
                                                ).then_inc(gathered[u], 16)
            steps(pool, step)

        @block.tensor
        def _(pe):
            t_ = nc.tensor

            def onehots_T(b, u):
                def tr(g):
                    if g == 0:
                        pe.wait_ge(S["oh_ready"], b + 1)
                    pe.wait_ge(S["ohT_saved"], b * B + g + 1)
                    for t in range(T):
                        last = t_.transpose(psO[g % 2][0:P, t * 128:(t + 1) * 128], oh[u][:, g * T + t, :], ident[:])
                    last.then_inc(S["ohT_done"], 1)

                def mm(g):
                    pe.wait_ge(S["ohT_saved"], b * B + g + 3)
                    if g == 0:
                        pe.wait_ge(S["ad_staged"], b + 1)
                    for t in range(T):
                        i = g * T + t
                        last = t_.matmul(psE[:, i * H:(i + 1) * H], ohT[g % 2][:, t * 128:(t + 1) * 128], adst[:, g, :], start=True, stop=True)
                    if g == B - 1:
                        last.then_inc(S["adE_done"], 1)
                tr(0)
                tr(1)
                mm(0)
                tr(2)
                mm(1)
                tr(3)
                mm(2)
                mm(3)

            def main(b, u, g):
                pe.wait_ge(S["msg_ready"], b * B + g + 1)
                pe.wait_ge(S["part_saved"], b * B + g + 1)
                for t in range(T):
                    last = t_.matmul(psP[g % 2][0:P, 0:MW], oh[u][:, g * T + t, :], ring[u][:, g * T + t, :], start=(t == 0), stop=(t == T - 1))
                last.then_inc(S["main_done"], 1)

            pe.sem_inc(S["main_done"], 2 * B)
            pe.wait_ge(S["consts"], 1)
            t_.matmul(M1[:, 0:KD * 129], zeros[:, 0:128], zeros[:], start=True, stop=False)
            onehots_T(0, 0)

            def close_kv():
                t_.matmul(M1[:, 0:KD * 129], zeros[:, 0:128], zeros[:], start=False, stop=True).then_inc(S["kv_closed"], 1)
            between[pe.engine] = close_kv

            def step(b, k, u, n, kind, last):
                pe.wait_ge(S["asc_ready"], b + 1)
                for t in range(T):
                    la = t_.transpose(psT[0:HB, t:GE:T], asc[:, t, :], ident[:])
                la.then_inc(S["asT_done"], 1)
                if kind == KV1:
                    pe.wait_ge(xm_in[u], k * 16 + 16)
                    for c in range(KD):
                        la = t_.matmul(M0[0:P, :], xm[u][:, c * P:(c + 1) * P], wkv[:, c, :], start=(c == 0), stop=(c == KD - 1))
                    la.then_inc(S["mixa_done"], 1)
                elif kind == KV2:
                    pe.wait_ge(xm_in[u], k * 16 + 16)
                    for m in range(KD):
                        for c in range(KD):
                            la = t_.matmul(M0[:, m * P:(m + 1) * P], wq[:, c, m * 128:(m + 1) * 128], xm[u][:, c * P:(c + 1) * P], start=(c == 0), stop=(c == KD - 1))
                    la.then_inc(S["mixa_done"], 1)
                pe.wait_ge(S["scans_done"], b + 1)
                pe.sem_inc(S["apart"], 1)
                for t in range(T):
                    la = t_.transpose(psE[:, 128 + t * HB:128 + (t + 1) * HB], scb[:, t:GE:T], ident[0:HB, 0:HB])
                la.then_inc(S["sT_done"], 1)
                if kind == KV1:
                    pe.wait_ge(S["kk_ready"], n + 1)
                    for m in range(KD):
                        la = t_.matmul(M1[:, m * 129:(m + 1) * 129], kk[0:P, m * 128:(m + 1) * 128], vst[:, m, :], start=False, stop=False)
                    la.then_inc(S["mixb_done"], 1)
                elif kind == KV2:
                    pe.wait_ge(S["kk_ready"], n + NT + 1)
                    pe.wait_ge(S["kvd_ready"], 1)
                    for i, w in enumerate((kvd, ksd)):
                        for m in range(KD):
                            o = (i * KD + m) * P
                            la = t_.matmul(M1[:, o:o + P], w[:, m, :], kk[:, m * P:(m + 1) * P], start=True, stop=True)
                    la.then_inc(S["mixb_done"], 1)
                main(b, u, 0)
                if kind == KV2:
                    pe.wait_ge(S["msgT_ready"], n + 1)
                    for m in range(KD):
                        la = t_.matmul(M0[0:P, 0:D], msgT[:, m * P:(m + 1) * P], wm[:, m, :], start=(m == 0), stop=(m == KD - 1))
                    la.then_inc(S["mixc_done"], 1)
                main(b, u, 1)
                main(b, u, 2)
                if kind == KV2:
                    pe.wait_ge(S["n1_ready"], n + 1)
                    for m in range(KD):
                        la = t_.transpose(M1[:, m * P:(m + 1) * P], n1[:, m * 128:(m + 1) * 128], ident[0:P, 0:P])
                    la.then_inc(S["mixd_done"], 1)
                main(b, u, 3)
                if kind == KV2:
                    pe.wait_ge(S["n1T_ready"], n + 1)
                    for m in range(4):
                        for c in range(2 * KD):
                            r = (xm[u] if c < KD else n1T)[:, (c % KD) * P:(c % KD + 1) * P]
                            la = t_.matmul(M0[:, m * P:(m + 1) * P], w1[:, c, m * 128:(m + 1) * 128], r, start=(c == 0), stop=(c == 2 * KD - 1))
                    la.then_inc(S["mixe_done"], 1)
                if not last:
                    onehots_T(b + 1, 1 - u)
                if kind == KV2:
                    pe.wait_ge(S["hT_ready"], n + 1)
                    for m in range(4):
                        la = t_.matmul(M1[0:P, 0:D], hT[:, m, :], w2[:, m, :], start=(m == 0), stop=(m == 3))
                    la.then_inc(S["mixf_done"], 1)
            steps(pe, step)

        @block.scalar
        def _(act):
            s = nc.scalar
            act.preload_act_table_set("natural_log_exp_and_others")
            act.sem_inc(S["ohT_saved"], 2)
            act.sem_inc(S["part_saved"], 2)

            def copy(o, i, sm):
                s.activation(o, i, ACT.Copy).then_inc(S[sm], 1)

            def onehots_T(b):
                for g in range(B):
                    act.wait_ge(S["ohT_done"], b * B + g + 1)
                    copy(ohT[g % 2][:], psO[g % 2][0:P, :], "ohT_saved")
                act.wait_ge(S["adE_done"], b + 1)
                copy(ad_e[:], psE[:, 0:BT * H].rearrange("p (i h) -> p i h", h=H), "adE_saved")
            onehots_T(0)

            def save(b, u, g):
                act.wait_ge(S["main_done"], b * B + (2 * B + g + 1))
                copy(part[u][:, g, :], psP[g % 2][0:P, 0:MW], "part_saved")

            def step(b, k, u, n, kind, last):
                act.wait_ge(gathered[u], k * (16 * BT) + 16 * BT)
                s.activation(asc[:].rearrange("p t (g h) -> p g t h", h=H), ringv(u)[:, :, :, C].rearrange("p (g t) h -> p g t h", t=T),
                             ACT.Copy).then_inc(S["asc_ready"], 1)
                if kind == KV1:
                    act.wait_ge(S["mixa_done"], n + 1)
                    s.activation(vst[:, :, 0:128], M0[0:P, D:2 * D].rearrange("p (m c) -> p m c", m=KD), ACT.Copy)
                    copy(kq[0:P, 0:D], M0[0:P, 0:D], "mixa_saved")
                    act.wait_ge(S["kmin_ready"], n + 1)
                    s.activation(kex[0:P, 0:D], kmin[0:P, 0:D], ACT.Exp).then_inc(S["kex_ready"], 1)
                elif kind == KV2:
                    act.wait_ge(S["mixa_done"], n + NT + 1)
                    copy(kq[:, 0:KD * P], M0[:, 0:KD * P], "mixa_saved")
                    act.wait_ge(S["kmin_ready"], n + NT + 1)
                    s.activation(kex[:, 0:KD * P], kmin[:, 0:KD * P], ACT.Exp).then_inc(S["kex_ready"], 1)
                act.wait_ge(S["eprep_done"], b + 1)
                s.activation(ringv(u)[:, :, :, C], df[:], ACT.Exp).then_inc(S["ex_done"], 1)
                save(b, u, 0)
                if kind == KV2:
                    act.wait_ge(S["st1_ready"], n + 1)
                    s.activation(lnv[:], mv[:, 1:2], ACT.Ln, bias=epsc[0:P, :]).then_inc(S["small"], 1)
                    act.wait_ge(S["small"], n * 2 + 1)
                    s.activation(rstd[:], lnv[:], ACT.Exp, scale=-0.5).then_inc(S["rs1_ready"], 1)
                save(b, u, 1)
                save(b, u, 2)
                if kind == KV2:
                    act.wait_ge(S["mixd_done"], n + 1)
                    copy(n1T[:], M1[:, 0:KD * P], "n1T_ready")
                save(b, u, 3)
                if kind == KV2:
                    act.wait_ge(S["mixe_done"], n + 1)
                    for m in range(4):
                        la = s.activation(hT[:, m, :], M0[:, m * P:(m + 1) * P], ACT.Relu, bias=bias1[:, m:m + 1])
                    la.then_inc(S["hT_ready"], 1)
                if not last:
                    onehots_T(b + 1)
                if kind == KV2:
                    act.wait_ge(S["st2_ready"], n + 1)
                    s.activation(lnv[:], mv[:, 1:2], ACT.Ln, bias=epsc[0:P, :]).then_inc(S["small"], 1)
                    act.wait_ge(S["small"], n * 2 + 2)
                    s.activation(rstd[:], lnv[:], ACT.Exp, scale=-0.5).then_inc(S["rs2_ready"], 1)
                act.wait_ge(S["dd_ready"], b + 1)
                s.activation(ww[:], dd[:], ACT.Exp).then_inc(S["ww_ready"], 1)
            steps(act, step)

        @block.vector
        def _(dve):
            d = nc.vector
            KE, K1, K2 = 28, 0, 9
            used = [0]

            def onehots(b, u, w, lk):
                dst = recs[u][:].bitcast(F32).rearrange("p g (t f) -> p g t f", f=4)[:, :, :, 1]
                lk(d.tensor_tensor(dloc[:], dst, wbase[:, bass.ds(b * B, B)].unsqueeze(2).broadcast_to([128, B, T]), ALU.subtract))
                for g in range(B):
                    la = d.tensor_tensor(oh[u][:, g * T:(g + 1) * T, :], iota_d[:].unsqueeze(1).broadcast_to([128, T, P]),
                                         dloc[:, g, :].unsqueeze(2).broadcast_to([128, T, P]), ALU.is_equal)
                la.then_inc(S["oh_ready"], 1)
                for g in range(B):
                    la = d.tensor_copy(adst[:, g, :], ad_all[:, bass.ds(w[g], 1), :].rearrange("p a h -> p (a h)"))
                la.then_inc(S["ad_staged"], 1)

            def windows(b):
                return [dve.value_load(sched[0:1, 1, bass.ds(b * B + g, 1)], min_val=0, max_val=NT) for g in range(B)]

            link = linker(dve, S["chain"])
            d.memset(vst[:, :, 128], 1.0)
            d.memset(epsc[:], LN_EPS)
            d.memset(kvd[:], 0.0)
            d.memset(zeros[:], 0.0)
            link(d.memset(ksd[:], 0.0))
            link(d.memset(first[:], 0.0))
            d.memset(first[0:1, :, 0], 1.0).then_inc(S["consts"], 1)
            dve.wait_ge(S["consts"], 1)
            dve.wait_ge(rec_in[0], 16 * B)
            onehots(0, 0, windows(0), link)
            used[0] = link.count[0]

            def block_diagonals():
                link = linker(dve, S["chain"], used[0])
                dve.wait_ge(S["kv_closed"], 1)
                link(d.tensor_copy(kvs[:], M1[:, 0:258].rearrange("p (m c) -> p m c", m=KD)))
                for m in range(KD):
                    for i in range(4):
                        q = slice(32 * i, 32 * i + 32)
                        d.tensor_scalar(kvd[q, m, q], kvs[q, m, q], 1.0 / N, None, ALU.mult)
                        la = d.tensor_scalar(ksd[q, m, q], ones[q, 0:32], kvs[q, m, 128:129], None, ALU.mult)
                la.then_inc(S["kvd_ready"], 1)
                used[0] += 1
            between[dve.engine] = block_diagonals

            def ln_stats(src, lk, ready):
                lk(d.bn_stats(st6[:], src))
                dve.sem_inc(S["apart"], 1)
                d.bn_aggr(mv[:], st6[:]).then_inc(S[ready], 1)

            def ln_shift(lk):
                lk(d.scalar_tensor_tensor(nb[:], mv[:, 0:1], -1.0, rstd[:], ALU.mult, ALU.mult))

            def step(b, k, u, n, kind, last):
                per = {KV1: KE + K1, KV2: KE + K2, PLAIN: KE}[kind]
                first_b = {KV1: 0, KV2: NT, PLAIN: 2 * NT}[kind]
                base = (b - first_b) * per + used[0]
                lk = linker(dve, S["chain"], base)
                dve.wait_ge(pen_in[u], k * (16 * B) + 16 * B)
                dve.wait_ge(S["asT_done"], b + 1)
                lk(d.tensor_tensor_scan(scf[:], pens[u][:, 0:GE], psT[0:HB, :], -BIG, ALU.add, ALU.max))
                d.tensor_tensor_scan(scb[:, ::-1], pens[u][:, GE:0:-1], scf[:, ::-1], -BIG, ALU.add, ALU.max).then_inc(S["scans_done"], 1)
                if kind == KV1:
                    dve.wait_ge(S["mixa_saved"], n + 1)
                    d.tensor_scalar(kmin[0:P, 0:D], kq[0:P, 0:D], 0.0, None, ALU.min).then_inc(S["kmin_ready"], 1)
                elif kind == KV2:
                    dve.wait_ge(S["mixa_saved"], n + NT + 1)
                    d.tensor_scalar(kmin[:, 0:KD * P], kq[:, 0:KD * P], 0.0, None, ALU.min).then_inc(S["kmin_ready"], 1)
                dve.wait_ge(S["adE_saved"], b + 1)
                rv = ringv(u)
                d.tensor_tensor(zz[:, 0], rv[:, :, :, C], ad_e[:], ALU.add)
                flags = recs[u][:].bitcast(F32).rearrange("p g (t f) -> p g t f", f=4)[:, :, :, 2]
                d.tensor_tensor(ring[u][:, :, MW - 1].rearrange("p (g t) -> p g t", t=T), flags, first[:], ALU.max)
                dve.wait_ge(S["sT_done"], b + 1)
                lk(d.tensor_tensor(zz[:, 1].rearrange("p (g t) h -> p t g h", t=T), psE[:, 128:256].rearrange("p (t g h) -> p t g h", t=T, h=H),
                                   ad_e[:].rearrange("p (g t) h -> p t g h", t=T), ALU.add))
                lk(d.scalar_tensor_tensor(zz[:], zz[:], SLOPE, zz[:], ALU.mult, ALU.max))
                d.tensor_tensor(df[:], zz[:, 0], zz[:, 1], ALU.subtract).then_inc(S["eprep_done"], 1)
                lk(d.tensor_tensor(ring[u][:, :, ROW:ROW + H], zz[:, 1], ring[u][:, :, MW - 1:MW].broadcast_to([128, BT, H]), ALU.mult))
                if kind == KV1:
                    dve.wait_ge(S["kex_ready"], n + 1)
                    d.scalar_tensor_tensor(kk[0:P, 0:D], kq[0:P, 0:D], 0.0, kex[0:P, 0:D], ALU.max, ALU.add).then_inc(S["kk_ready"], 1)
                elif kind == KV2:
                    dve.wait_ge(S["kex_ready"], n + NT + 1)
                    d.scalar_tensor_tensor(kk[:, 0:KD * P], kq[:, 0:KD * P], 0.0, kex[:, 0:KD * P], ALU.max, ALU.add).then_inc(S["kk_ready"], 1)

                def weigh(g):
                    if g == 0:
                        dve.wait_ge(S["ex_done"], b + 1)
                    q = slice(g * T, (g + 1) * T)
                    d.tensor_tensor(rv[:, q, :, 0:C], rv[:, q, :, 0:C], rv[:, q, :, C:CW].broadcast_to([128, T, H, C]), ALU.mult).then_inc(S["msg_ready"], 1)
                weigh(0)
                if kind == KV2:
                    dve.wait_ge(S["mixb_done"], n + NT + 1)
                    lk(d.tensor_scalar(den[:], M1[:, KD * P:2 * KD * P], MIX_EPS, None, ALU.add))
                    lk(d.reciprocal(den[:], den[:]))
                    d.scalar_tensor_tensor(msgT[:], M1[:, 0:KD * P], float(N), den[:], ALU.mult, ALU.mult).then_inc(S["msgT_ready"], 1)
                weigh(1)
                if kind == KV2:
                    dve.wait_ge(S["mixc_done"], n + 1)
                    ln_stats(M0[0:P, 0:D], lk, "st1_ready")
                weigh(2)
                if kind == KV2:
                    dve.wait_ge(S["rs1_ready"], n + 1)
                    ln_shift(lk)
                    d.tensor_scalar(n1[:], M0[0:P, 0:D], rstd[:], nb[:], ALU.mult, ALU.add).then_inc(S["n1_ready"], 1)
                weigh(3)
                if not last:
                    dve.wait_ge(rec_in[1 - u], (k + u) * (16 * B) + 16 * B)
                    onehots(b + 1, 1 - u, windows(b + 1), lk)
                if kind == KV2:
                    dve.wait_ge(S["mixf_done"], n + 1)
                    ln_stats(M1[0:P, 0:D], lk, "st2_ready")
                w = windows(b)
                dve.wait_ge(S["part_saved"], b * B + (B + 2))
                pt = part[u]
                ptv = pt[:, :, 0:ROW].rearrange("p g (h c) -> p g h c", c=CW)
                lk(d.tensor_scalar(pm[:], pt[:, :, MW - 1:MW], 1.0, BIG, ALU.subtract, ALU.mult))
                lk(d.tensor_tensor(sg[:], pt[:, :, ROW:ROW + H], pm[:].broadcast_to([P, B, H]), ALU.add))
                for g in range(B):
                    m = m_run[:, bass.ds(w[g], 1), :].rearrange("p a h -> p (a h)")
                    lk(d.tensor_tensor(mns[:, g, :], m, sg[:, g, :], ALU.max))
                    lk(d.tensor_tensor(dd[:, 0, g, :], m, mns[:, g, :], ALU.subtract))
                    lk(d.tensor_tensor(m, m, sg[:, g, :], ALU.max))
                d.tensor_tensor(dd[:, 1], sg[:], mns[:], ALU.subtract).then_inc(S["dd_ready"], 1)
                if kind == KV2:
                    dve.wait_ge(S["rs2_ready"], n + 1)
                    ln_shift(lk)
                    lk(d.tensor_scalar(n2[:], M1[0:P, 0:D], rstd[:], nb[:], ALU.mult, ALU.add))
                    lk(d.tensor_tensor(n2[:], n2[:], rows[:, 1, :], ALU.mult))
                    dve.wait_ge(xr_in[u], (k - NT // 2) * 16 + 16)
                    lk(d.tensor_tensor(n2[:], n2[:], rows[:, 2, :], ALU.add))
                    d.tensor_tensor(mo[u][:], n2[:], xr[u][:], ALU.add).then_inc(S["mo_ready"], 1)
                dve.wait_ge(S["ww_ready"], b + 1)
                lk(d.tensor_tensor(ptv, ptv, ww[:, 1].unsqueeze(3).broadcast_to([P, B, H, CW]), ALU.mult))
                for g in range(B):
                    a = acc[:, bass.ds(w[g], 1), :].rearrange("p a (h c) -> p (a h) c", c=CW)
                    lk(d.tensor_tensor(a, a, ww[:, 0, g, :].unsqueeze(2).broadcast_to([P, H, CW]), ALU.mult))
                    lk(d.tensor_tensor(a, a, ptv[:, g], ALU.add))
                if not last:
                    assert lk.count[0] == per, (lk.count[0], per)
                ends[kind] = used[0] + {KV1: NT, KV2: NT, PLAIN: 0}[kind] * per
                if kind != PLAIN and u == 1:
                    used[0] = ends[kind]
            ends = {}
            steps(dve, step)


def slices(nc, sb, ps, sem, linker, v):
    ident, ones, acc, wc, bc, rows = (v[k] for k in "ident ones acc wc bc rows".split())
    mix_d, swT_d, out = v["mix_d"], v["swT_d"], v["out"]
    TW = D + 1
    Q = 5
    with ExitStack() as ctx:
        gm = [sb(ctx, f"gm{i}", [P, D]) for i in range(2)]
        mixt = [sb(ctx, f"mixt{i}", [P, D]) for i in range(2)]
        rden = sb(ctx, "rden", [P, H])
        st6 = sb(ctx, "st6c", [P, 6])
        mv = sb(ctx, "mvc", [P, 2])
        lnv = sb(ctx, "lnvc", [P, 1])
        rstd = sb(ctx, "rstdc", [P, 1])
        nb = sb(ctx, "nbc", [P, 1])
        xn = [sb(ctx, f"xnc{i}", [P, TW]) for i in range(2)]
        xnT = [sb(ctx, f"xnTc{i}", [128, KD * P]) for i in range(2)]
        lg = [sb(ctx, f"lg{i}", [P, INNER]) for i in range(2)]
        ex = [sb(ctx, f"ex{i}", [P, INNER]) for i in range(2)]
        sw = [sb(ctx, f"sw{i}", [P, INNER]) for i in range(2)]
        swT = [sb(ctx, f"swT{i}", [128, 4 * P]) for i in range(2)]
        mx = [sb(ctx, f"mx{i}", [P, FH]) for i in range(2)]
        sm = [sb(ctx, f"sm{i}", [P, FH]) for i in range(2)]
        epsc = sb(ctx, "epscc", [128, 1])
        zer = sb(ctx, "zer", [128, TW])
        tok = sb(ctx, "tok", [128, 4, TW])
        tokT = sb(ctx, "tokT", [128, KD, 4, 128])
        wfx = sb(ctx, "wfx", [128, KD, INNER])
        bfx = sb(ctx, "bfx", [1, INNER])
        wqkv = sb(ctx, "wqkv", [FD, 3, FD])
        wo = sb(ctx, "wo", [FD, FH, D])
        nrow = sb(ctx, "nrow", [1, INNER])
        rrow = sb(ctx, "rrow", [1, INNER])
        rbc = sb(ctx, "rbc", [FD, INNER])
        stT = sb(ctx, "stT", [FD, INNER])
        qT = sb(ctx, "qT", [FD, INNER])
        kT = sb(ctx, "kT", [FD, INNER])
        vv = sb(ctx, "vv", [FD, INNER])
        sc = sb(ctx, "sc", [FD, INNER])
        se = sb(ctx, "se", [FD, INNER])
        aT = sb(ctx, "aT", [FD, INNER])
        smx = sb(ctx, "smx", [FD, FH])
        ssum = sb(ctx, "ssum", [FD, FH])
        osT = sb(ctx, "osT", [FD, INNER])
        mm = sb(ctx, "mm", [128, 4, D])
        back = [sb(ctx, f"back{i}", [128, 4 * P]) for i in range(Q)]
        ot = [sb(ctx, f"ot{i}", [P, D]) for i in range(Q)]
        res = [sb(ctx, f"res{i}", [P, D]) for i in range(Q)]
        psT = ps(ctx, "pC_T")
        psL = ps(ctx, "pC_L")
        psW = ps(ctx, "pC_W")
        psK = [ps(ctx, f"pC_K{i}") for i in range(4)]
        psY = ps(ctx, "pC_Y")
        names = """gm_ready sum_free x1_ready var_ready lnv_ready rstd_ready xn_ready xT_done xnT_ready lg_done lgb_ready mx_ready
            sub_ready ex_ready sm_ready sw_ready tok_done swT_done swT_ready swT_free chain apart consts weights_in swT_out
            pe_m dve_m act_m y_done y_read pchain""".split()
        S = {n: sem(ctx, "s_" + n) for n in names}
        mix_in = [sem(ctx, f"s_mix_in{i}") for i in range(2)]
        back_in = [sem(ctx, f"s_back_in{i}") for i in range(Q)]
        out_done = sem(ctx, "out_done")
        o_ready = sem(ctx, "o_ready")
        o_free = sem(ctx, "o_free")
        block = ctx.enter_context(nc.Block())

        def hd(a):
            return a.rearrange("p (h g) -> p h g", g=FD)

        def wide(a, p=P):
            return a.unsqueeze(2).broadcast_to([p, FH, FD])

        def pipeline(eng, head, body):
            head()
            with eng.Fori(0, NT // 2 - 1) as it:
                for u in range(2):
                    body(it * 2 + u, it, u, False)
            for u in range(2):
                body(NT - 2 + u, NT // 2 - 1, u, u == 1)

        @block.sync
        def _(sp):
            for u in range(2):
                sp.dma_start(mixt[u][:], mix_d[u * P:(u + 1) * P, :]).then_inc(mix_in[u], 16)
            sp.dma_start(wfx[:], v["W_fx"].rearrange("(k p) n -> p k n", p=128)).then_inc(S["weights_in"], 16)
            sp.dma_start(bfx[:], v["b_fx"].rearrange("(a n) -> a n", a=1)).then_inc(S["weights_in"], 16)
            for i, w in enumerate(("W_q", "W_k", "W_v")):
                sp.dma_start(wqkv[:, i, :], v[w]).then_inc(S["weights_in"], 16)
            sp.dma_start(wo[:], v["W_out"].rearrange("(h c) n -> c h n", c=FD)).then_inc(S["weights_in"], 16)

            def body(n, k, u, last):
                if not (isinstance(n, int)):
                    sp.wait_ge(S["x1_ready"], n + 1)
                    sp.dma_start(mixt[u][:], mix_d[bass.ds(n * P + 2 * P, P), :]).then_inc(mix_in[u], 16)
                sp.wait_ge(S["swT_ready"], n + 1)
                sp.dma_start(swT_d[bass.ds(n, 1), :, :].rearrange("a p n -> (a p) n"), swT[u][:]).then_inc(S["swT_out"], 16)
                sp.wait_ge(S["swT_out"], n * 16 + 16)
                sp.sem_inc(S["swT_free"], 1)
            pipeline(sp, lambda: None, body)
            for i in range(Q):
                sp.dma_start(back[i][:], swT_d[i, :, :]).then_inc(back_in[i], 16)
            with sp.Fori(0, NT // Q - 1) as it:
                for i in range(Q):
                    sp.wait_ge(S["y_done"], it * Q + i + 1)
                    sp.dma_start(back[i][:], swT_d[bass.ds(it * Q + (Q + i), 1), :, :].rearrange("a p n -> (a p) n")).then_inc(back_in[i], 16)

        @block.gpsimd
        def _(pool):
            g = nc.gpsimd

            def front(n, u, k):
                pool.wait_ge(S["gm_ready"], n + 1)
                g.tensor_tensor(gm[u][:], gm[u][:], rows[:, 0, :], ALU.add).then_inc(S["pchain"], 1)
                pool.wait_ge(S["pchain"], n + 1)
                pool.wait_ge(mix_in[u], k * 16 + 16)
                pool.sem_inc(S["apart"], 1)
                g.tensor_tensor(acc[:, bass.ds(n, 1), 0:D].rearrange("p a n -> p (a n)"), gm[u][:], mixt[u][:], ALU.add).then_inc(S["x1_ready"], 1)

            def body(n, k, u, last):
                pool.wait_ge(S["mx_ready"], n + 1)
                g.tensor_tensor(hd(lg[u][:]), hd(lg[u][:]), wide(mx[u][:]), ALU.subtract).then_inc(S["sub_ready"], 1)
                if not last:
                    front(n + 1, 1 - u, k + u)
                pool.wait_ge(S["sm_ready"], n + 1)
                g.tensor_tensor(hd(sw[u][:]), hd(ex[u][:]), wide(sm[u][:]), ALU.mult).then_inc(S["sw_ready"], 1)
            pipeline(pool, lambda: front(0, 0, 0), body)

        @block.scalar
        def _(act):
            s = nc.scalar
            act.preload_act_table_set("natural_log_exp_and_others")
            act.sem_inc(S["swT_free"], 2)
            act.wait_ge(S["consts"], 1)

            def front(n, u, k):
                act.wait_ge(S["var_ready"], n + 1)
                s.activation(lnv[:], mv[:, 1:2], ACT.Ln, bias=epsc[0:P, :]).then_inc(S["lnv_ready"], 1)
                act.wait_ge(S["lnv_ready"], n + 1)
                s.activation(rstd[:], lnv[:], ACT.Exp, scale=-0.5).then_inc(S["rstd_ready"], 1)
                act.wait_ge(S["xT_done"], n + 1)
                s.activation(xnT[u][:], psT[:, 0:KD * P], ACT.Copy).then_inc(S["xnT_ready"], 1)

            def body(n, k, u, last):
                act.wait_ge(S["sub_ready"], n + 1)
                s.activation(ex[u][:], lg[u][:], ACT.Exp).then_inc(S["ex_ready"], 1)
                if not last:
                    front(n + 1, 1 - u, k + u)
                act.wait_ge(S["swT_done"], n + 1)
                act.wait_ge(S["swT_free"], n + 1)
                s.activation(swT[u][:], psW[:, 0:4 * P], ACT.Copy).then_inc(S["swT_ready"], 1)
            pipeline(act, lambda: front(0, 0, 0), body)
            act.wait_ge(S["dve_m"], 9)
            s.activation(se[:], sc[:], ACT.Exp, scale=float(FD) ** -0.5).then_inc(S["act_m"], 1)
            act.sem_inc(o_free, Q)
            with act.Fori(0, NT // Q) as it:
                for i in range(Q):
                    act.wait_ge(o_ready, it * Q + i + 1)
                    act.dma_start(out[bass.ds((it * Q + i) * P, P), :], res[i][:]).then_inc(out_done, 16)
                act.wait_ge(out_done, it * (16 * Q) + 16 * Q)
                act.sem_inc(o_free, Q)

        @block.vector
        def _(dve):
            d = nc.vector
            d.memset(epsc[:], LN_EPS)
            d.memset(zer[:], 0.0)
            for u in range(2):
                la = d.memset(xn[u][:, D:TW], 1.0)
            la.then_inc(S["consts"], 1)
            dve.wait_ge(S["consts"], 1)
            KF, KS = 4, 1

            def front(n, u, k, lk):
                a = acc[:, bass.ds(n, 1), :].rearrange("p a (h c) -> p (a h) c", c=CW)
                lk(d.tensor_scalar(rden[:], a[:, :, C], DEN_EPS, None, ALU.add))
                lk(d.reciprocal(rden[:], rden[:]))
                d.tensor_tensor(gm[u][:].rearrange("p (h c) -> p h c", c=C), a[:, :, 0:C], rden[:].unsqueeze(2).broadcast_to([P, H, C]),
                                ALU.mult).then_inc(S["gm_ready"], 1)

            def front2(n, u, k, lk):
                x1 = acc[:, bass.ds(n, 1), 0:D].rearrange("p a n -> p (a n)")
                dve.wait_ge(S["x1_ready"], n + 1)
                dve.sem_inc(S["apart"], 1)
                lk(d.bn_stats(st6[:], x1))
                dve.sem_inc(S["apart"], 1)
                d.bn_aggr(mv[:], st6[:]).then_inc(S["var_ready"], 1)
                dve.wait_ge(S["rstd_ready"], n + 1)
                if not (isinstance(n, int) and n == 0):
                    dve.wait_ge(S["tok_done"], n)
                lk(d.scalar_tensor_tensor(nb[:], mv[:, 0:1], -1.0, rstd[:], ALU.mult, ALU.mult))
                d.tensor_scalar(xn[u][:, 0:D], x1, rstd[:], nb[:], ALU.mult, ALU.add).then_inc(S["xn_ready"], 1)

            def head():
                lk = linker(dve, S["chain"])
                front(0, 0, 0, lk)
                front2(0, 0, 0, lk)
                assert lk.count[0] == KF

            def body(n, k, u, last):
                lk = linker(dve, S["chain"], n * (KF + KS) + KF)
                dve.wait_ge(S["lg_done"], n + 1)
                d.tensor_tensor(lg[u][:], psL[0:P, :], bc[:], ALU.add).then_inc(S["lgb_ready"], 1)
                dve.wait_ge(S["lgb_ready"], n + 1)
                d.tensor_reduce(mx[u][:], hd(lg[u][:]), axis=X, op=ALU.max).then_inc(S["mx_ready"], 1)
                if not last:
                    front(n + 1, 1 - u, k + u, lk)
                dve.wait_ge(S["ex_ready"], n + 1)
                lk(d.tensor_reduce(sm[u][:], hd(ex[u][:]), axis=X, op=ALU.add))
                d.reciprocal(sm[u][:], sm[u][:]).then_inc(S["sm_ready"], 1)
                if not last:
                    front2(n + 1, 1 - u, k + u, lk)
                    assert lk.count[0] == KF + KS
            pipeline(dve, head, body)

            done = linker(dve, S["dve_m"])
            dve.wait_ge(S["pe_m"], 1)
            for j in range(4):
                la = d.tensor_copy(tok[:, j, :], psK[j][:, 0:TW])
            done(la)
            dve.wait_ge(S["pe_m"], 2)
            for k in range(KD):
                d.tensor_copy(tokT[:, k, :, :], psK[k][:, :].rearrange("p (j n) -> p j n", j=4))
            la = d.tensor_copy(nrow[:], psK[2][0:1, :])
            done(la)
            done(d.tensor_scalar(rrow[:], nrow[:], TOK_EPS, None, ALU.add))
            done(d.reciprocal(rrow[:], rrow[:]))
            dve.wait_ge(S["pe_m"], 3)
            done(d.tensor_copy(rbc[:], psK[3][0:FD, :]))
            done(d.tensor_tensor(stT[:], psL[0:FD, :], rbc[:], ALU.mult))
            dve.wait_ge(S["pe_m"], 4)
            d.tensor_copy(qT[:], psK[0][0:FD, :])
            d.tensor_copy(kT[:], psK[1][0:FD, :])
            done(d.tensor_copy(vv[:], psK[2][0:FD, :]))
            dve.wait_ge(S["pe_m"], 5)
            done(d.tensor_reduce(smx[:], hd(psL[0:FD, :]), axis=X, op=ALU.max))
            done(d.tensor_tensor(hd(sc[:]), hd(psL[0:FD, :]), wide(smx[:], FD), ALU.subtract))
            dve.wait_ge(S["act_m"], 1)
            done(d.tensor_reduce(ssum[:], hd(se[:]), axis=X, op=ALU.add))
            done(d.reciprocal(ssum[:], ssum[:]))
            done(d.tensor_tensor(hd(se[:]), hd(se[:]), wide(ssum[:], FD), ALU.mult))
            dve.wait_ge(S["pe_m"], 6)
            done(d.tensor_copy(aT[:], psK[3][0:FD, :]))
            dve.wait_ge(S["pe_m"], 7)
            done(d.tensor_copy(osT[:], psL[0:FD, :]))
            dve.wait_ge(S["pe_m"], 8)
            for j in range(4):
                d.tensor_copy(mm[0:FD, j, :], psK[j][0:FD, 0:D])
                la = d.tensor_copy(mm[FD:, j, :], psK[j][FD:, D:2 * D])
            done(la)
            with dve.Fori(0, NT // Q) as it:
                for i in range(Q):
                    n = it * Q + i
                    dve.wait_ge(S["y_done"], n + 1)
                    d.tensor_tensor(ot[i][:], psK[i % 4][0:P, 0:D] if i < 4 else psL[0:P, 0:D], rows[:, 3, :], ALU.add).then_inc(S["y_read"], 1)
                    dve.wait_ge(S["y_read"], n + (Q + 1))
                    dve.wait_ge(o_free, n + 1)
                    d.tensor_tensor(res[i][:], ot[i][:], acc[:, bass.ds(n, 1), 0:D].rearrange("p a n -> p (a n)"), ALU.add).then_inc(o_ready, 1)

        @block.tensor
        def _(pe):
            t_ = nc.tensor

            def front(n, u, k):
                pe.wait_ge(S["xn_ready"], n + 1)
                for c in range(KD):
                    la = t_.transpose(psT[:, c * P:(c + 1) * P], xn[u][:, c * 128:(c + 1) * 128], ident[0:P, 0:P])
                la.then_inc(S["xT_done"], 1)
                pe.wait_ge(S["xnT_ready"], n + 1)
                for c in range(KD):
                    la = t_.matmul(psL[0:P, :], xnT[u][:, c * P:(c + 1) * P], wc[:, c, :], start=(c == 0), stop=(c == KD - 1))
                la.then_inc(S["lg_done"], 1)

            def body(n, k, u, last):
                if not last:
                    front(n + 1, 1 - u, k + u)
                pe.wait_ge(S["sw_ready"], n + 1)
                for j in range(4):
                    la = t_.matmul(psK[j][:, 0:TW], sw[u][:, j * 128:(j + 1) * 128], xn[u][:], start=False, stop=False)
                la.then_inc(S["tok_done"], 1)
                for j in range(4):
                    la = t_.transpose(psW[:, j * P:(j + 1) * P], sw[u][:, j * 128:(j + 1) * 128], ident[0:P, 0:P])
                la.then_inc(S["swT_done"], 1)

            def head():
                pe.wait_ge(S["consts"], 1)
                for j in range(4):
                    t_.matmul(psK[j][:, 0:TW], zer[:, 0:128], zer[:, 0:TW], start=True, stop=False)
                pe.sem_inc(S["tok_done"], 1)
                front(0, 0, 0)
            pipeline(pe, head, body)
            for j in range(4):
                la = t_.matmul(psK[j][:, 0:TW], zer[:, 0:128], zer[:, 0:TW], start=False, stop=True)
            la.then_inc(S["pe_m"], 1)
            pe.wait_ge(S["dve_m"], 1)
            for k in range(KD):
                for j in range(4):
                    t_.transpose(psK[k][:, j * 128:(j + 1) * 128], tok[:, j, k * 128:(k + 1) * 128], ident[:])
            for j in range(4):
                la = t_.matmul(psK[2][0:1, j * 128:(j + 1) * 128], tok[:, j, D:TW], ident[:], start=True, stop=True)
            la.then_inc(S["pe_m"], 1)
            pe.wait_ge(S["dve_m"], 4)
            pe.wait_ge(S["weights_in"], 16 * 6)
            t_.matmul(psK[3][0:FD, :], ones[0:1, 0:FD], rrow[:], start=True, stop=True)
            for h in range(FH):
                q = slice(h * FD, (h + 1) * FD)
                for k in range(KD):
                    t_.matmul(psL[0:FD, q], wfx[:, k, q], tokT[:, k, :, :].rearrange("p j n -> p (j n)")[:, q], start=(k == 0), stop=False)
                la = t_.matmul(psL[0:FD, q], bfx[:, q], nrow[:, q], start=False, stop=True)
            la.then_inc(S["pe_m"], 1)
            pe.wait_ge(S["dve_m"], 6)
            for i in range(2):
                t_.matmul(psK[i][0:FD, :], wqkv[:, i, :], stT[:], start=True, stop=True)
            for h in range(FH):
                q = slice(h * FD, (h + 1) * FD)
                la = t_.matmul(psK[2][0:FD, q], stT[:, q], wqkv[:, 2, :], start=True, stop=True)
            la.then_inc(S["pe_m"], 1)
            pe.wait_ge(S["dve_m"], 7)
            for h in range(FH):
                q = slice(h * FD, (h + 1) * FD)
                la = t_.matmul(psL[0:FD, q], qT[:, q], kT[:, q], start=True, stop=True)
            la.then_inc(S["pe_m"], 1)
            pe.wait_ge(S["dve_m"], 12)
            for h in range(FH):
                q = slice(h * FD, (h + 1) * FD)
                la = t_.transpose(psK[3][0:FD, q], se[:, q], ident[0:FD, 0:FD])
            la.then_inc(S["pe_m"], 1)
            pe.wait_ge(S["dve_m"], 13)
            for h in range(FH):
                q = slice(h * FD, (h + 1) * FD)
                la = t_.matmul(psL[0:FD, q], vv[:, q], aT[:, q], start=True, stop=True)
            la.then_inc(S["pe_m"], 1)
            pe.wait_ge(S["dve_m"], 14)
            for j in range(4):
                for i in range(2):
                    la = t_.matmul(psK[j][:, i * D:(i + 1) * D], osT[:, j * 128:(j + 1) * 128], wo[:, 2 * j + i, :], start=True, stop=True)
            la.then_inc(S["pe_m"], 1)
            pe.wait_ge(S["dve_m"], 15)
            pe.sem_inc(S["y_read"], Q)
            with pe.Fori(0, NT // Q) as it:
                for i in range(Q):
                    n = it * Q + i
                    pe.wait_ge(back_in[i], it * 16 + 16)
                    bank = psK[i % 4] if i < 4 else psL
                    pe.wait_ge(S["y_read"], n + 1)
                    for j in range(4):
                        la = t_.matmul(bank[0:P, 0:D], back[i][:, j * P:(j + 1) * P], mm[:, j, :], start=(j == 0), stop=(j == 3))
                    la.then_inc(S["y_done"], 1)


_INS = ['x', 'src', 'dst', 'L0_gnn_W', 'L0_gnn_att_src', 'L0_gnn_att_dst', 'L0_gnn_bias', 'L0_mix_Wq', 'L0_mix_Wk', 'L0_mix_Wv',
        'L0_mix_Wm', 'L0_mix_W1', 'L0_mix_W2', 'L0_mix_g1', 'L0_mix_b1', 'L0_mix_g2', 'L0_mix_b2', 'L0_ffn_W_fx', 'L0_ffn_b_fx',
        'L0_ffn_W_x', 'L0_ffn_b_x', 'L0_ffn_W_slice', 'L0_ffn_b_slice', 'L0_ffn_W_q', 'L0_ffn_W_k', 'L0_ffn_W_v', 'L0_ffn_W_out',
        'L0_ffn_b_out', 'L0_ffn_temperature']


def kernel(**inputs):
    import numpy as _np
    import concourse.bacc as _bacc
    from concourse import mybir as _mybir
    from concourse.bass_utils import run_bass_kernel_spmd as _run

    nc = _bacc.Bacc("TRN2", target_bir_lowering=False, num_devices=1)
    arrays, args = {}, []
    for name in _INS:
        a = _np.ascontiguousarray(inputs[name])
        arrays[f"in_{name}_dram"] = a
        args.append(nc.dram_tensor(f"in_{name}_dram", a.shape, _mybir.dt.from_np(a.dtype), kind="ExternalInput").ap())
    out = nc.dram_tensor("out_0_dram", (N, D), F32, kind="ExternalOutput").ap()
    program(nc, *args, out)
    r = _run(nc, [arrays], core_ids=[0])
    return r.results[0]["out_0_dram"]
```

```python
import concourse.bass as bass
from concourse import mybir
from contextlib import ExitStack

F32 = mybir.dt.float32
I32 = mybir.dt.int32
BF16 = mybir.dt.bfloat16
ALU = mybir.AluOpType
ACT = mybir.ActivationFunctionType
X = mybir.AxisListType.X

N, E, D = 6250, 200000, 256
H, C = 8, 32
P = 125
NT = N // P
KD = D // 128
CW = C + 1
ROW = H * CW
W1C = NT + 1
T = 4
GE = 128 * T
NG = 448
assert NG >= -(-E // GE) + NT
B = 4
NB = NG // B
HALF = E // P
FH, FD = 8, 64
INNER = FH * FD
BIG = 1.0e38
SLOPE = 0.2
LN_EPS = 1e-5
MIX_EPS = 1e-6
TOK_EPS = 1e-5
DEN_EPS = 1e-16
MW = ROW + H + 1


def program(nc, x, src, dst, gnn_W, att_src, att_dst, gnn_bias, Wq, Wk, Wv, Wm, W1, W2, g1, b1, g2, b2,
            W_fx, b_fx, W_x, b_x, W_slice, b_slice, W_q, W_k, W_v, W_out, b_out, temperature, out):
    h_tab = nc.dram_tensor("h_tab", (N, ROW), F32, kind="Internal").ap()
    rec = nc.dram_tensor("rec", (E + GE, 4), I32, kind="Internal").ap()
    pen = nc.dram_tensor("pen", (E + GE + 8,), F32, kind="Internal").ap()
    xnT_d = nc.dram_tensor("xnT_d", (NT + 2, 128, KD * P), F32, kind="Internal").ap()
    mix_d = nc.dram_tensor("mix_d", (N, D), F32, kind="Internal").ap()
    xpx_d = nc.dram_tensor("xpx_d", (N, D), F32, kind="Internal").ap()
    swT_d = nc.dram_tensor("swT_d", (NT, 128, 4 * P), F32, kind="Internal").ap()

    top = ExitStack()

    def sb(ctx, name, shape, dt=F32):
        return ctx.enter_context(nc.sbuf_tensor(name, shape, dt))

    def ps(ctx, name, shape=(128, 512)):
        return ctx.enter_context(nc.psum_tensor(name, list(shape), F32))

    def sem(ctx, name):
        return ctx.enter_context(nc.semaphore(name))

    def linker(eng, s, base=0):
        n = [0]

        def link(ins):
            n[0] += 1
            ins.then_inc(s, 1)
            eng.wait_ge(s, base + n[0])
        link.count = n
        return link

    with top:
        ident = sb(top, "ident", [128, 128])
        ones = sb(top, "ones", [128, 128])
        iota_d = sb(top, "iota_d", [128, P])
        wbase = sb(top, "wbase", [128, NG])
        sched = sb(top, "sched", [1, 2, B + NG], I32)
        acc = sb(top, "acc", [P, W1C, ROW])
        ad_all = sb(top, "ad_all", [P, W1C, H])
        m_run = sb(top, "m_run", [P, W1C, H])
        wq = sb(top, "wq", [128, KD, D])
        wm = sb(top, "wm", [128, KD, D])
        w1 = sb(top, "w1", [128, 2 * KD, 2 * D])
        bias1 = sb(top, "bias1", [128, 4])
        w2 = sb(top, "w2", [128, 2 * KD, D])
        rows = sb(top, "rows", [P, 4, D])
        wc = sb(top, "wc", [128, KD, INNER])
        bc = sb(top, "bc", [P, INNER])
        kvd = sb(top, "kvd", [128, KD, 128])
        ksd = sb(top, "ksd", [128, KD, 128])
        ad3 = sb(top, "ad3", [P, W1C, 3, H], BF16)

        prologue(nc, sb, ps, sem, linker, locals())
        edges_and_mix(nc, sb, ps, sem, linker, locals())
        slices(nc, sb, ps, sem, linker, locals())


def pipeline(eng, unroll, stages):
    lead = max(a for a, _ in stages)
    assert lead <= unroll and NT % unroll == 0
    for n in range(-lead, 0):
        for a, step in stages:
            if n + a >= 0:
                step(n + a, (n + a) // unroll, (n + a) % unroll)
    with eng.Fori(0, NT // unroll - 1) as it:
        for i in range(unroll):
            for a, step in stages:
                step(it * unroll + (i + a), it + (i + a) // unroll, (i + a) % unroll)
    for n in range(NT - unroll, NT):
        for a, step in stages:
            if n + a < NT:
                step(n + a, (n + a) // unroll, (n + a) % unroll)


def prologue(nc, sb, ps, sem, linker, v):
    x, src, dst = v["x"], v["src"], v["dst"]
    ident, ones, iota_d, wbase, sched = v["ident"], v["ones"], v["iota_d"], v["wbase"], v["sched"]
    acc, ad_all, m_run = v["acc"], v["ad_all"], v["m_run"]
    h_tab, rec, pen, xnT_d, xpx_d = v["h_tab"], v["rec"], v["pen"], v["xnT_d"], v["xpx_d"]
    wq, wm, w1, w2, rows, bias1, wc, bc, kvd, ksd, ad3 = (v[k] for k in "wq wm w1 w2 rows bias1 wc bc kvd ksd ad3".split())
    with ExitStack() as ctx:
        wkv = sb(ctx, "wkv", [128, KD, 2 * D])
        kex = sb(ctx, "kex", [P, D])
        krl = sb(ctx, "krl", [P, D])
        kk = sb(ctx, "kk", [P, 2, D])
        vst = sb(ctx, "vst", [P, 2, KD, 129])
        kvs = sb(ctx, "kvs", [128, KD, 129])
        zeros = sb(ctx, "zeros", [128, KD * 129])
        adr = sb(ctx, "adr", [P, NT, H])
        wg = sb(ctx, "wg", [128, KD, ROW + H])
        wraw = sb(ctx, "wraw", [128, KD, D])
        att = sb(ctx, "att", [128, 2, D])
        prod = sb(ctx, "prod", [128, 2, KD, D])
        src_i = sb(ctx, "src_i", [P, HALF], I32)
        dst_i = sb(ctx, "dst_i", [P, HALF + 1], I32)
        dst_f = sb(ctx, "dst_f", [P, HALF + 1])
        start = sb(ctx, "start", [P, HALF])
        recs = sb(ctx, "recs", [P, HALF, 4], I32)
        pad = sb(ctx, "pad", [128, T, 4], I32)
        padp = sb(ctx, "padp", [1, GE + 8])
        junk = sb(ctx, "junk", [P, HALF], mybir.dt.bfloat16)
        cnt = sb(ctx, "cnt", [P, W1C])
        cdiff = sb(ctx, "cdiff", [P, W1C])
        thr = sb(ctx, "thr", [P, W1C])
        iota_g = sb(ctx, "iota_g", [W1C, NG])
        iota_k = sb(ctx, "iota_k", [W1C, E // GE + 1])
        kjunk = sb(ctx, "kjunk", [W1C, E // GE + 1])
        wcol = sb(ctx, "wcol", [W1C, 1])
        wrep = sb(ctx, "wrep", [W1C, 128])
        below = sb(ctx, "below", [W1C, W1C])
        big50 = sb(ctx, "big50", [W1C, 1])
        cols = sb(ctx, "cols", [W1C, 6])
        ind = sb(ctx, "ind", [W1C, NG])
        ind2 = sb(ctx, "ind2", [W1C, NG])
        sch_f = sb(ctx, "sch_f", [1, 3, NG])
        xn = sb(ctx, "xn", [P, 2, D])
        xpx = sb(ctx, "xpx", [P, 2, D])
        st6 = sb(ctx, "st6", [P, 2, 6])
        mv = sb(ctx, "mv", [P, 2, 2])
        lnv = sb(ctx, "lnv", [P, 2, 1])
        rstd = sb(ctx, "rstd", [P, 2, 1])
        nb = sb(ctx, "nb", [P, 2, 1])
        xnT = sb(ctx, "xnT", [128, 2, KD * P])
        vcols = sb(ctx, "vcols", [128, 2, KD])
        wx = sb(ctx, "wx", [128, KD, INNER])
        wxT = sb(ctx, "wxT", [128, 4, D])
        wsl = sb(ctx, "wsl", [128, 128])
        bxc = sb(ctx, "bxc", [128, 4])
        brow = sb(ctx, "brow", [1, INNER])
        bsl = sb(ctx, "bsl", [1, FD])
        tmp1 = sb(ctx, "tmp1", [1, FH])
        itemp = sb(ctx, "itemp", [128, FH])
        zcol = sb(ctx, "zcol", [128, 2])
        psT = [ps(ctx, "pA_T"), ps(ctx, "pA_X")]
        psH = [ps(ctx, "pA_H"), ps(ctx, "pA_K")]
        psM = ps(ctx, "pA_M")
        psS = ps(ctx, "pA_S")
        psW = ps(ctx, "pA_W")
        psR = ps(ctx, "pA_R")

        edges_in = sem(ctx, "edges_in")
        weights_in = sem(ctx, "weights_in")
        late_in = sem(ctx, "late_in")
        x_in = sem(ctx, "x_in")
        x_read = sem(ctx, "x_read")
        xn_free = sem(ctx, "xn_free")
        xnT_free = sem(ctx, "xnT_free")
        consts = sem(ctx, "consts")
        dstf_ready = sem(ctx, "dstf_ready")
        recs_ready = sem(ctx, "recs_ready")
        pool_chain = sem(ctx, "pool_chain")
        dve_chain = sem(ctx, "dve_chain")
        pro_out = sem(ctx, "pro_out")
        var_ready = sem(ctx, "var_ready")
        lnv_ready = sem(ctx, "lnv_ready")
        st_ready = sem(ctx, "st_ready")
        nb_ready = sem(ctx, "nb_ready")
        rstd_ready = sem(ctx, "rstd_ready")
        xn_ready = sem(ctx, "xn_ready")
        xpx_ready = sem(ctx, "xpx_ready")
        xpx_out = [sem(ctx, f"xpx_out{i}") for i in range(2)]
        xpx_free = sem(ctx, "xpx_free")
        rows_in = sem(ctx, "rows_in")
        kvw_in = sem(ctx, "kvw_in")
        xT_done = sem(ctx, "xT_done")
        xnT_ready = sem(ctx, "xnT_ready")
        xnT_out = [sem(ctx, f"xnT_out{i}") for i in range(2)]
        k_done = sem(ctx, "k_done")
        kparts_ready = sem(ctx, "kparts_ready")
        v_saved = sem(ctx, "v_saved")
        kk_ready = sem(ctx, "kk_ready")
        kv_added = sem(ctx, "kv_added")
        kv_closed = sem(ctx, "kv_closed")
        setup = sem(ctx, "setup")
        wg_ready = sem(ctx, "wg_ready")
        h_done = sem(ctx, "h_done")
        h_saved = sem(ctx, "h_saved")
        ad_saved = sem(ctx, "ad_saved")
        tab_out = sem(ctx, "tab_out")
        cnt_ready = sem(ctx, "cnt_ready")
        pe_s = sem(ctx, "sched_products")
        dve_s = sem(ctx, "sched_steps")
        pe_w = sem(ctx, "weight_products")
        dve_w = sem(ctx, "weight_steps")
        act_chain = sem(ctx, "act_chain")

        apart = sem(ctx, "apart")
        block = ctx.enter_context(nc.Block())

        @block.sync
        def _(sp):
            sp.dma_start(wraw[:], v["gnn_W"].rearrange("(k p) n -> p k n", p=128)).then_inc(weights_in, 16)
            sp.dma_start(att[:, 0, :], v["att_src"].rearrange("h c -> (h c)").partition_broadcast(128)).then_inc(weights_in, 16)
            sp.dma_start(att[:, 1, :], v["att_dst"].rearrange("h c -> (h c)").partition_broadcast(128)).then_inc(weights_in, 16)
            sp.dma_start(acc[:, 0:NT, 0:D], x.rearrange("(t p) n -> p t n", p=P)).then_inc(x_in, 16)

            def store(t, q, u):
                sp.wait_ge(xnT_ready, t + 1)
                sp.dma_start(xnT_d[bass.ds(t, 1), :, :].rearrange("a p n -> (a p) n"), xnT[:, u, :]).then_inc(xnT_out[u], 16)

            def free(t, q, u):
                sp.wait_ge(h_saved, t + 1)
                sp.dma_start(h_tab[bass.ds(t * P, P), :], acc[:, bass.ds(t, 1), :].rearrange("p a n -> p (a n)")).then_inc(tab_out, 16)
                sp.wait_ge(xnT_out[u], q * 16 + 16)
                sp.sem_inc(xnT_free, 1)
            pipeline(sp, 2, [(1, store), (0, free)])
            for u in range(2):
                sp.dma_start(xnT_d[NT + u, :, :], xnT[:, u, :]).then_inc(xnT_out[u], 16)
            for u in range(2):
                sp.wait_ge(xnT_out[u], 16 * (NT // 2 + 1))
            sp.wait_ge(tab_out, 16 * NT)

        @block.gpsimd
        def _(pool):
            link = linker(pool, pool_chain)
            g = nc.gpsimd
            g.memset(dst_i[0:1, 0:1], -1).then_inc(consts, 1)
            pool.wait_ge(consts, 1)
            pool.dma_start(src_i[:], src.rearrange("(p n) -> p n", p=P)).then_inc(edges_in, 16)
            pool.dma_start(dst_i[:, 1:], dst.rearrange("(p n) -> p n", p=P)).then_inc(edges_in, 16)
            pool.dma_start(dst_i[1:P, 0:1], dst.rearrange("(p n) -> p n", p=P)[0:P - 1, HALF - 1:HALF],
                           allow_slow_non_contiguous=True).then_inc(edges_in, 16)
            link(g.memset(ident[:], 0.0))
            g.affine_select(out=ident[:], in_=ident[:], compare_op=ALU.not_equal, fill=1.0, base=0,
                            pattern=[[-1, 128]], channel_multiplier=1).then_inc(consts, 1)
            g.memset(ones[:], 1.0).then_inc(consts, 1)
            g.iota(iota_d[:], [[1, P]], base=0, channel_multiplier=0, allow_small_or_imprecise_dtypes=True).then_inc(consts, 1)
            g.iota(thr[:], [[P, W1C]], base=0, channel_multiplier=0, allow_small_or_imprecise_dtypes=True).then_inc(consts, 1)
            g.iota(iota_g[:], [[1, NG]], base=0, channel_multiplier=0, allow_small_or_imprecise_dtypes=True).then_inc(consts, 1)
            g.iota(iota_k[:], [[GE, E // GE + 1]], base=0, channel_multiplier=0, allow_small_or_imprecise_dtypes=True).then_inc(consts, 1)
            g.iota(wcol[:], [[0, 1]], base=0, channel_multiplier=1, allow_small_or_imprecise_dtypes=True).then_inc(consts, 1)
            g.iota(wrep[:], [[0, 128]], base=0, channel_multiplier=P, allow_small_or_imprecise_dtypes=True).then_inc(consts, 1)
            link(g.memset(below[:], 1.0))
            g.affine_select(out=below[:], in_=below[:], compare_op=ALU.is_gt, fill=0.0, base=0,
                            pattern=[[1, W1C]], channel_multiplier=-1).then_inc(consts, 1)
            link(g.memset(big50[:], 0.0))
            g.affine_select(out=big50[:], in_=big50[:], compare_op=ALU.not_equal, fill=1.0e6, base=-NT,
                            pattern=[[0, 1]], channel_multiplier=1).then_inc(consts, 1)
            g.memset(zcol[:], LN_EPS).then_inc(consts, 1)
            g.memset(acc[:, NT, :], 0.0)
            g.memset(ad_all[:, NT, :], 0.0)
            g.memset(m_run[:, NT, :], 0.0)
            g.memset(wsl[:], 0.0).then_inc(consts, 1)
            g.memset(pad[:, :, 0], 0)
            g.memset(pad[:, :, 1].bitcast(F32), -1.0)
            g.memset(pad[:, :, 2].bitcast(F32), 1.0)
            g.memset(pad[:, :, 3], 0)
            link(g.memset(padp[:], -BIG))
            pool.dma_start(rec[E:E + GE, :].rearrange("(p t) f -> p (t f)", p=128), pad[:].rearrange("p t f -> p (t f)")).then_inc(pro_out, 16)
            pool.dma_start(pen[E:E + GE + 8].rearrange("(a n) -> a n", a=1), padp[:]).then_inc(pro_out, 16)
            pool.wait_ge(edges_in, 48)
            g.tensor_copy(dst_f[:], dst_i[:]).then_inc(dstf_ready, 1)
            pool.wait_ge(dstf_ready, 1)
            link(g.tensor_tensor(start[:], dst_f[:, 1:], dst_f[:, :HALF], ALU.subtract))
            link(g.tensor_scalar(start[:], start[:], 0.0, None, ALU.is_gt))
            g.tensor_copy(recs[:, :, 0], src_i[:])
            g.tensor_copy(recs[:, :, 1].bitcast(F32), dst_f[:, 1:])
            g.memset(recs[:, :, 3], 0)
            link(g.tensor_copy(recs[:, :, 2].bitcast(F32), start[:]))
            pool.dma_start(rec[0:E, :].rearrange("(p n) f -> p (n f)", p=P), recs[:].rearrange("p n f -> p (n f)")).then_inc(pro_out, 16)
            link(g.tensor_scalar(start[:], start[:], -BIG, None, ALU.mult))
            pool.dma_start(pen[0:E].rearrange("(p n) -> p n", p=P), start[:]).then_inc(pro_out, 16)
            pool.wait_ge(rows_in, 64)

            def residual(t, q, u):
                pool.wait_ge(xn_ready, t + 1)
                pool.wait_ge(xpx_free, t + 1)
                pool.sem_inc(apart, 1)
                g.tensor_tensor(xpx[:, u, :], acc[:, bass.ds(t, 1), 0:D].rearrange("p a n -> p (a n)"), xn[:, u, :], ALU.add).then_inc(x_read, 1)
                pool.wait_ge(x_read, t + 1)
                g.tensor_tensor(xpx[:, u, :], xpx[:, u, :], rows[:, 2, :], ALU.add).then_inc(xpx_ready, 1)
                pool.wait_ge(xpx_ready, t + 1)
                pool.sem_inc(xn_free, 1)
                pool.dma_start(xpx_d[bass.ds(t * P, P), :], xpx[:, u, :]).then_inc(xpx_out[u], 16)

            def stored(t, q, u):
                pool.wait_ge(xpx_out[u], q * 16 + 16)
                pool.sem_inc(xpx_free, 1)
            pipeline(pool, 2, [(1, residual), (0, stored)])
            pool.wait_ge(pro_out, 64)

        @block.scalar
        def _(act):
            s = nc.scalar
            act.preload_act_table_set("natural_log_exp_and_others")
            act.sem_inc(xnT_free, 2)
            act.sem_inc(xn_free, 2)
            act.sem_inc(xpx_free, 2)

            def load(dstt, srca, sm=late_in):
                act.dma_start(dstt, srca).then_inc(sm, 16)
            load(wkv[:, :, 0:D], v["Wk"].rearrange("(k p) n -> p k n", p=128), kvw_in)
            load(wkv[:, :, D:], v["Wv"].rearrange("(k p) n -> p k n", p=128), kvw_in)
            for i, r in enumerate(("gnn_bias", "g2", "b2", "b_out")):
                load(rows[:, i, :], v[r].partition_broadcast(P), rows_in)
            load(wq[:], v["Wq"].rearrange("(k p) n -> p k n", p=128))
            load(wm[:], v["Wm"].rearrange("(k p) n -> p k n", p=128))
            load(w1[:], v["W1"].rearrange("(k p) n -> p k n", p=128))
            load(w2[:], v["W2"].rearrange("(k p) n -> p k n", p=128))
            with nc.allow_non_contiguous_dma(reason="a few columns"):
                load(vcols[:, 0, :], v["g1"].rearrange("(k p) -> p k", p=128))
                load(vcols[:, 1, :], v["b1"].rearrange("(k p) -> p k", p=128))
                load(bxc[:], v["b_x"].rearrange("(k p) -> p k", p=128))
            load(wx[:], v["W_x"].rearrange("(k p) n -> p k n", p=128))
            act.wait_ge(consts, 13)
            load(wsl[0:FD, 0:FD], v["W_slice"])
            load(wsl[FD:, FD:], v["W_slice"])
            load(bsl[:], v["b_slice"].rearrange("(a n) -> a n", a=1))
            load(itemp[:], v["temperature"].rearrange("a h b c -> (a h b c)").partition_broadcast(128))
            act.wait_ge(setup, 1)

            def deviations(t, q, u):
                act.wait_ge(var_ready, t + 1)
                s.activation(lnv[:, u, :], mv[:, u, 1:2], ACT.Ln, bias=zcol[0:P, 0:1]).then_inc(lnv_ready, 1)
                act.wait_ge(lnv_ready, t + 1)
                s.activation(rstd[:, u, :], lnv[:, u, :], ACT.Exp, scale=-0.5).then_inc(rstd_ready, 1)

            def transposed(t, q, u):
                act.wait_ge(xT_done, t + 1)
                act.wait_ge(xnT_free, t + 1)
                s.activation(xnT[:, u, :], psT[0][:, 0:KD * P], ACT.Copy).then_inc(xnT_ready, 1)

            def keys_values(t, q, u):
                act.wait_ge(k_done, t + 1)
                s.activation(kex[:], psH[1][0:P, 0:D], ACT.Exp)
                s.activation(krl[:], psH[1][0:P, 0:D], ACT.Relu).then_inc(kparts_ready, 1)
                s.activation(vst[:, u, :, 0:128], psH[1][0:P, D:].rearrange("p (m c) -> p m c", m=KD), ACT.Copy).then_inc(v_saved, 1)

            def projected(t, q, u):
                act.wait_ge(h_done, t + 1)
                act.wait_ge(x_read, t + 1)
                s.activation(acc[:, bass.ds(t, 1), :].rearrange("p a n -> p (a n)"), psH[0][0:P, 0:ROW], ACT.Copy).then_inc(h_saved, 1)
                s.activation(ad_all[:, bass.ds(t, 1), :].rearrange("p a n -> p (a n)"), psH[0][0:P, ROW:ROW + H], ACT.Copy).then_inc(ad_saved, 1)
            act.sem_inc(v_saved, 1)
            act.sem_inc(ad_saved, 1)
            pipeline(act, 2, [(2, deviations), (0, keys_values), (1, transposed), (0, projected)])

        @block.vector
        def _(dve):
            d = nc.vector
            link = linker(dve, dve_chain)
            dve.wait_ge(weights_in, 48)
            for i in range(2):
                for k in range(KD):
                    d.tensor_tensor(prod[:, i, k, :], wraw[:, k, :], att[:, i, :], ALU.mult)
            wgv = wg[:, :, 0:ROW].rearrange("p k (h c) -> p k h c", c=CW)
            for k in range(KD):
                last = d.tensor_copy(wgv[:, k, :, 0:C], wraw[:, k, :].rearrange("p (h c) -> p h c", c=C))
            link(last)
            for k in range(KD):
                d.tensor_reduce(wgv[:, k, :, C], prod[:, 0, k, :].rearrange("p (h c) -> p h c", c=C), axis=X, op=ALU.add)
                last = d.tensor_reduce(wg[:, k, ROW:], prod[:, 1, k, :].rearrange("p (h c) -> p h c", c=C), axis=X, op=ALU.add)
            last.then_inc(wg_ready, 1)
            d.memset(zeros[:], 0.0)
            d.memset(kvd[:], 0.0)
            d.memset(ksd[:], 0.0)
            d.memset(vst[:, :, :, 128], 1.0).then_inc(setup, 1)
            dve.wait_ge(x_in, 16)
            dve.wait_ge(dstf_ready, 1)
            dve.wait_ge(consts, 13)

            def count(w):
                d.tensor_scalar(junk[:], dst_f[:, 1:], thr[:, bass.ds(w, 1)], 0.0, ALU.is_lt, ALU.add,
                                accum_out=cnt[:, bass.ds(w, 1)]).then_inc(cnt_ready, 1)

            def stats(t, q, u):
                d.bn_stats(st6[:, u, :], acc[:, bass.ds(t, 1), 0:D].rearrange("p a n -> p (a n)")).then_inc(st_ready, 1)
                dve.wait_ge(st_ready, t + 1)
                dve.sem_inc(apart, 1)
                d.bn_aggr(mv[:, u, :], st6[:, u, :]).then_inc(var_ready, 1)

            def normed(t, q, u):
                dve.wait_ge(rstd_ready, t + 1)
                d.scalar_tensor_tensor(nb[:, u, :], mv[:, u, 0:1], -1.0, rstd[:, u, :], ALU.mult, ALU.mult).then_inc(nb_ready, 1)
                dve.wait_ge(nb_ready, t + 1)
                dve.wait_ge(xn_free, t + 1)
                d.tensor_scalar(xn[:, u, :], acc[:, bass.ds(t, 1), 0:D].rearrange("p a n -> p (a n)"), rstd[:, u, :], nb[:, u, :],
                                ALU.mult, ALU.add).then_inc(xn_ready, 1)

            def keys(t, q, u):
                dve.wait_ge(kparts_ready, t + 1)
                d.scalar_tensor_tensor(kk[:, u, :], kex[:], 1.0, krl[:], ALU.min, ALU.add).then_inc(kk_ready, 1)

            def counted(t, q, u):
                dve.wait_ge(cnt_ready, t + 1)
                count(t)
            d.memset(junk[:], 0.0).then_inc(cnt_ready, 1)
            pipeline(dve, 2, [(1, normed), (2, stats), (0, keys), (0, counted)])
            dve.wait_ge(cnt_ready, NT + 1)
            count(NT)
            dve.wait_ge(cnt_ready, NT + 2)
            link(d.memset(cdiff[:, NT:], 0.0))
            d.tensor_tensor(cdiff[:, 0:NT], cnt[:, 1:], cnt[:, 0:NT], ALU.subtract).then_inc(dve_s, 1)
            dve.wait_ge(pe_s, 1)
            link(d.tensor_copy(cols[:, 0:2], psS[0:W1C, 0:2]))
            d.tensor_scalar(kjunk[:], iota_k[:], cols[:, 1:2], 0.0, ALU.is_lt, ALU.add, accum_out=cols[:, 2:3]).then_inc(dve_s, 1)
            dve.wait_ge(dve_s, 2)
            dve.wait_ge(pe_s, 2)
            link(d.tensor_copy(cols[:, 3:4], psS[0:W1C, 2:3]))
            link(d.scalar_tensor_tensor(cols[:, 4:5], cols[:, 3:4], cols[:, 2:3], big50[:], ALU.add, ALU.add))
            d.tensor_scalar(ind[:], iota_g[:], cols[:, 3:4], None, ALU.is_ge)
            link(d.tensor_scalar(ind2[:], iota_g[:], cols[:, 4:5], None, ALU.is_ge))
            link(d.scalar_tensor_tensor(cols[:, 5:6], cols[:, 3:4], float(-GE), cols[:, 0:1], ALU.mult, ALU.add))
            link(d.tensor_tensor(ind[:], ind[:], ind2[:], ALU.subtract))
            dve.sem_inc(dve_s, 1)
            dve.wait_ge(pe_s, 3)
            link(d.scalar_tensor_tensor(sch_f[:, 0, :], iota_g[0:1, :], float(GE), psS[0:1, 0:NG], ALU.mult, ALU.add))
            link(d.tensor_scalar(sch_f[:, 1, :], sch_f[:, 0, :], float(E), None, ALU.min))
            d.tensor_copy(sched[:, 0, B:], sch_f[:, 1, :])
            dve.wait_ge(pe_s, 4)
            link(d.tensor_copy(sched[:, 1, B:], psR[0:1, 0:NG]))
            link(d.memset(sched[:, :, 0:B], NT))
            dve.wait_ge(pe_s, 5)
            link(d.tensor_copy(wbase[:], psT[1][:, 0:NG]))
            dve.wait_ge(ad_saved, NT + 1)
            dve.wait_ge(h_saved, NT)
            accv = acc[:].rearrange("p w (h c) -> p w h c", c=CW)
            link(d.tensor_tensor(m_run[:, 0:NT, :], accv[:, 0:NT, :, C], ad_all[:, 0:NT, :], ALU.add))
            link(d.scalar_tensor_tensor(m_run[:, 0:NT, :], m_run[:, 0:NT, :], SLOPE, m_run[:, 0:NT, :], ALU.mult, ALU.max))
            dve.wait_ge(tab_out, 16 * NT)
            link(d.memset(accv[:, 0:NT, :, C], 1.0))
            rest = ad_all[:, 0:NT, :]
            link(d.memset(ad3[:, NT, :, :], 0.0))
            for i in range(3):
                link(d.tensor_copy(ad3[:, 0:NT, i, :], rest))
                if i < 2:
                    link(d.tensor_tensor(adr[:], rest, ad3[:, 0:NT, i, :], ALU.subtract))
                    rest = adr[:]
            dve.wait_ge(kv_closed, 1)
            link(d.tensor_copy(kvs[:], psM[:, 0:KD * 129].rearrange("p (m c) -> p m c", m=KD)))
            for m in range(KD):
                for i in range(4):
                    q = slice(32 * i, 32 * i + 32)
                    d.tensor_scalar(kvd[q, m, q], kvs[q, m, q], 1.0 / N, None, ALU.mult)
                    d.tensor_scalar(ksd[q, m, q], ones[q, 0:32], kvs[q, m, 128:129], None, ALU.mult)
            dve.wait_ge(late_in, 16 * 12)
            link(d.tensor_scalar(itemp[:], itemp[:], 0.1, 5.0, ALU.max, ALU.min))
            link(d.reciprocal(itemp[:], itemp[:]))
            dve.wait_ge(pe_w, 1)
            link(d.tensor_copy(bias1[:], psW[:, 0:4]))
            for k in range(KD):
                d.tensor_scalar(w1[:, KD + k, :], w1[:, KD + k, :], vcols[:, 0, k:k + 1], None, ALU.mult)
            for k in range(KD):
                dve.wait_ge(pe_w, 2 + 2 * k)
                link(d.tensor_copy(wxT[:, :, k * 128:(k + 1) * 128], psT[k][:, :].rearrange("p (j n) -> p j n", j=4)))
                dve.sem_inc(dve_w, 1)
                dve.wait_ge(pe_w, 3 + 2 * k)
                d.tensor_tensor(wc[:, k, :].rearrange("p (h g) -> p h g", g=FD), psH[k][:, :].rearrange("p (h g) -> p h g", g=FD),
                                itemp[:, :].unsqueeze(2).broadcast_to([128, FH, FD]), ALU.mult)
            dve.wait_ge(pe_w, 6)
            bv = brow[:].rearrange("p (h g) -> p h g", g=FD)
            link(d.tensor_tensor(bv, psW[0:1, :].rearrange("p (h g) -> p h g", g=FD),
                                 bsl[:].unsqueeze(1).broadcast_to([1, FH, FD]), ALU.add))
            link(d.tensor_tensor(bv, bv, itemp[0:1, :].unsqueeze(2).broadcast_to([1, FH, FD]), ALU.mult))
            dve.sem_inc(dve_w, 1)
            dve.wait_ge(pe_w, 7)
            link(d.tensor_copy(bc[:], psW[0:P, :]))

        @block.tensor
        def _(pe):
            t = nc.tensor
            pe.wait_ge(consts, 13)
            pe.wait_ge(wg_ready, 1)
            pe.wait_ge(kvw_in, 32)
            pe.wait_ge(setup, 1)
            t.matmul(psM[:, 0:KD * 129], zeros[:, 0:128], zeros[:], start=True, stop=False)

            def turned(n, q, u):
                pe.wait_ge(xn_ready, n + 1)
                for k in range(KD):
                    last = t.transpose(psT[0][:, k * P:(k + 1) * P], xn[:, u, k * 128:(k + 1) * 128], ident[0:P, 0:P])
                last.then_inc(xT_done, 1)

            def products(n, q, u):
                pe.wait_ge(xnT_ready, n + 1)
                pe.wait_ge(v_saved, n + 1)
                for k in range(KD):
                    last = t.matmul(psH[1][0:P, :], xnT[:, u, k * P:(k + 1) * P], wkv[:, k, :], start=(k == 0), stop=(k == KD - 1))
                last.then_inc(k_done, 1)
                pe.wait_ge(ad_saved, n + 1)
                for k in range(KD):
                    last = t.matmul(psH[0][0:P, 0:ROW + H], xnT[:, u, k * P:(k + 1) * P], wg[:, k, :], start=(k == 0), stop=(k == KD - 1))
                last.then_inc(h_done, 1)

            def sums(n, q, u):
                pe.wait_ge(kk_ready, n + 1)
                pe.wait_ge(v_saved, n + 2)
                for m in range(KD):
                    last = t.matmul(psM[:, m * 129:(m + 1) * 129], kk[:, u, m * 128:(m + 1) * 128], vst[:, u, m, :], start=False, stop=False)
                last.then_inc(kv_added, 1)
            pipeline(pe, 2, [(0, products), (1, turned), (0, sums)])
            t.matmul(psM[:, 0:KD * 129], zeros[:, 0:128], zeros[:], start=False, stop=True).then_inc(kv_closed, 1)
            pe.wait_ge(late_in, 16 * 12)
            for m in range(4):
                for k in range(KD):
                    last = t.matmul(psW[:, m:m + 1], w1[:, KD + k, m * 128:(m + 1) * 128], vcols[:, 1, k:k + 1], start=(k == 0), stop=(k == KD - 1))
            last.then_inc(pe_w, 1)
            pe.wait_ge(dve_s, 1)
            t.matmul(psS[0:W1C, 0:1], cnt[:], ones[0:P, 0:1], start=True, stop=True)
            t.matmul(psS[0:W1C, 1:2], cdiff[:], ones[0:P, 0:1], start=True, stop=True).then_inc(pe_s, 1)
            pe.wait_ge(dve_s, 2)
            t.matmul(psS[0:W1C, 2:3], below[:], cols[:, 2:3], start=True, stop=True).then_inc(pe_s, 1)
            pe.wait_ge(dve_s, 3)
            t.matmul(psS[0:1, 0:NG], cols[:, 5:6], ind[:], start=True, stop=True).then_inc(pe_s, 1)
            t.matmul(psR[0:1, 0:NG], wcol[:], ind[:], start=True, stop=True).then_inc(pe_s, 1)
            t.matmul(psT[1][:, 0:NG], wrep[:], ind[:], start=True, stop=True).then_inc(pe_s, 1)
            pe.wait_ge(h_saved, NT)
            pe.wait_ge(ad_saved, NT + 1)
            for k in range(KD):
                for j in range(4):
                    last = t.transpose(psT[k][:, j * 128:(j + 1) * 128], wx[:, k, j * 128:(j + 1) * 128], ident[:])
                last.then_inc(pe_w, 1)
                pe.wait_ge(dve_w, k + 1)
                for j in range(4):
                    last = t.matmul(psH[k][:, j * 128:(j + 1) * 128], wxT[:, j, k * 128:(k + 1) * 128], wsl[:], start=True, stop=True)
                last.then_inc(pe_w, 1)
            for j in range(4):
                last = t.matmul(psW[0:1, j * 128:(j + 1) * 128], bxc[:, j:j + 1], wsl[:], start=True, stop=True)
            last.then_inc(pe_w, 1)
            pe.wait_ge(dve_w, 3)
            t.matmul(psW[0:P, :], ones[0:1, 0:P], brow[:], start=True, stop=True).then_inc(pe_w, 1)


def edges_and_mix(nc, sb, ps, sem, linker, v):
    ident, iota_d, wbase, sched = v["ident"], v["iota_d"], v["wbase"], v["sched"]
    acc, ad3, m_run, kvd, ksd = v["acc"], v["ad3"], v["m_run"], v["kvd"], v["ksd"]
    h_tab, rec, pen, xnT_d, xpx_d, mix_d = v["h_tab"], v["rec"], v["pen"], v["xnT_d"], v["xpx_d"], v["mix_d"]
    wq, wm, w1, w2, rows, bias1 = (v[k] for k in "wq wm w1 w2 rows bias1".split())
    BT = B * T
    HB = H * B
    AW = 3 * H
    with ExitStack() as ctx:
        ring = [sb(ctx, f"ring{i}", [128, BT, MW]) for i in range(2)]
        recs = [sb(ctx, f"recb{i}", [128, B, T * 4], I32) for i in range(2)]
        pens = [sb(ctx, f"penb{i}", [HB, GE + 1]) for i in range(2)]
        oh = [sb(ctx, f"oh{i}", [128, BT, P]) for i in range(2)]
        ohT = [sb(ctx, f"ohT{i}", [P, GE], BF16) for i in range(2)]
        adst = sb(ctx, "adst", [P, B, AW], BF16)
        dloc = sb(ctx, "dloc", [128, B, T])
        first = sb(ctx, "first", [128, B, T])
        asc = sb(ctx, "asc", [128, T, B * H])
        scf = sb(ctx, "scf", [HB, GE])
        scb = sb(ctx, "scb", [HB, GE])
        ad_e = sb(ctx, "ad_e", [128, BT, H])
        zz = sb(ctx, "zz", [128, 2, BT, H])
        df = sb(ctx, "df", [128, BT, H])
        part = [sb(ctx, f"part{i}", [P, B, MW]) for i in range(2)]
        pm = sb(ctx, "pm", [P, B, 1])
        sg = sb(ctx, "sg", [P, B, H])
        mns = sb(ctx, "mns", [P, B, H])
        dd = [sb(ctx, f"dd{i}", [P, 2, B, H]) for i in range(2)]
        ww = [sb(ctx, f"ww{i}", [P, 2, B, H]) for i in range(2)]
        xm = [sb(ctx, f"xm{i}", [128, KD * P]) for i in range(2)]
        xr = [sb(ctx, f"xr{i}", [P, D]) for i in range(2)]
        mo = [sb(ctx, f"mo{i}", [P, D]) for i in range(2)]
        qex = sb(ctx, "qex", [128, KD * P])
        qrl = sb(ctx, "qrl", [128, KD * P])
        qq = sb(ctx, "qq", [128, KD * P])
        den = sb(ctx, "den", [128, KD * P])
        msgT = sb(ctx, "msgT", [128, KD * P])
        st6 = sb(ctx, "st6b", [P, 2, 6])
        mv = sb(ctx, "mvb", [P, 2, 2])
        lnv = sb(ctx, "lnvb", [P, 2, 1])
        rstd = sb(ctx, "rstdb", [P, 2, 1])
        nb = sb(ctx, "nbb", [P, 2, 1])
        n1 = sb(ctx, "n1", [P, D])
        n1T = sb(ctx, "n1T", [128, KD * P])
        hT = sb(ctx, "hT", [128, 4, P])
        n2 = sb(ctx, "n2", [P, D])
        nm = sb(ctx, "nm", [P, 2, 1])
        fix = sb(ctx, "fix", [128, KD * P])
        lden = sb(ctx, "lden", [128, KD * P])
        epsc = sb(ctx, "epsc", [128, 3])
        psT = ps(ctx, "pB_T")
        psE = ps(ctx, "pB_E")
        psO = [ps(ctx, f"pB_O{i}") for i in range(2)]
        psP = [ps(ctx, f"pB_P{i}") for i in range(2)]
        M0 = ps(ctx, "pB_M0")
        M1 = ps(ctx, "pB_M1")

        names = """asc_ready apart main_done asT_done ad_summed scans_done sT_done zz_ready al_ready flags_ready eprep_done ex_done
            msg_ready part_saved dloc_ready oh_ready ad_staged ohT_done ohT_saved adE_done dd_ready ww_ready pm_ready sg_ready
            m_steps a_steps p_scaled consts
            q_done qparts_ready qq_ready nd_done den_ready rden_ready fix_ready msgT_ready wm_done st_ready var_ready lnv_ready rstd_ready
            nb_ready n1_ready n1_turned n1T_ready w1_done hT_ready w2_done n2_ready n2_scaled mo_ready mo_free""".split()
        S = {n: sem(ctx, "e_" + n) for n in names}
        rec_in = [sem(ctx, f"rec_in{i}") for i in range(2)]
        pen_in = [sem(ctx, f"pen_in{i}") for i in range(2)]
        gathered = [sem(ctx, f"gathered{i}") for i in range(2)]
        xm_in = [sem(ctx, f"xm_in{i}") for i in range(2)]
        xr_in = [sem(ctx, f"xr_in{i}") for i in range(2)]
        mo_out = sem(ctx, "mo_out")
        block = ctx.enter_context(nc.Block())

        def steps(eng, body):
            with eng.Fori(0, NT // 2) as it:
                for i in range(4):
                    body(it * 4 + i, it * 2 + i // 2, i % 2, it * 2 + i // 2, it, i // 2, False)
            with eng.Fori(0, NB // 2 - NT - 1) as it:
                for u in range(2):
                    body(it * 2 + u + 2 * NT, it + NT, u, None, None, None, False)
            for u in range(2):
                body(NB - 2 + u, NB // 2 - 1, u, None, None, None, u == 1)

        def ringv(u):
            return ring[u][:, :, 0:ROW].rearrange("p t (h c) -> p t h c", c=CW)

        @block.sync
        def _(sp):
            def edge_loads(b, u):
                for g in range(B):
                    e0 = sp.value_load(sched[0:1, 0, bass.ds(b * B + (B + g), 1)], min_val=0, max_val=E)
                    sp.dma_start(recs[u][:, g, :], rec[bass.ds(e0, GE), :].rearrange("(p t) f -> p (t f)", t=T)).then_inc(rec_in[u], 16)
                    sp.dma_start(pens[u][g * H:(g + 1) * H, :], pen[bass.ds(e0, GE + 1)].partition_broadcast(H)).then_inc(pen_in[u], 16)

            for u in range(2):
                edge_loads(u, u)
                sp.dma_start(xm[u][:], xnT_d[u, :, :]).then_inc(xm_in[u], 16)

            def step(b, k, u, n, nk, j, last):
                if not (isinstance(b, int)):
                    sp.wait_ge(S["eprep_done"], b + 1)
                    edge_loads(b + 2, u)
                if n is not None and u == 0:
                    sp.dma_start(xr[j][:], xpx_d[bass.ds(n * P, P), :]).then_inc(xr_in[j], 16)
                if n is not None and u == 1:
                    sp.wait_ge(S["w1_done"], n + 1)
                    sp.dma_start(xm[j][:], xnT_d[bass.ds(n + 2, 1), :, :].rearrange("a p n -> (a p) n")).then_inc(xm_in[j], 16)
                    sp.wait_ge(S["mo_ready"], n + 1)
                    sp.dma_start(mix_d[bass.ds(n * P, P), :], mo[j][:]).then_inc(mo_out, 16)
                    sp.wait_ge(mo_out, n * 16 + 16)
                    sp.sem_inc(S["mo_free"], 1)
            steps(sp, step)
            for u in range(2):
                sp.wait_ge(xm_in[u], 16 * (NT // 2 + 1))
            sp.wait_ge(mo_out, 16 * NT)

        @block.gpsimd
        def _(pool):
            def step(b, k, u, n, nk, j, last):
                pool.wait_ge(rec_in[u], k * (16 * B) + 16 * B)
                for g in range(B):
                    pool.wait_ge(S["main_done"], b * B + g + 1)
                    pool.sem_inc(S["apart"], 1)
                    for t in range(T):
                        pool.indirect_dma_start(out=ring[u][:, g * T + t, 0:ROW], out_offset=None, in_=h_tab[:, :],
                                                in_offset=bass.IndirectOffsetOnAxis(ap=recs[u][:, g, t * 4:t * 4 + 1], axis=0)
                                                ).then_inc(gathered[u], 16)
            steps(pool, step)

        @block.tensor
        def _(pe):
            t_ = nc.tensor

            def onehots_T(b, u):
                def tr(g):
                    pe.wait_ge(S["oh_ready"], b * B + g + 1)
                    pe.wait_ge(S["ohT_saved"], b * B + g + 1)
                    for t in range(T):
                        last = t_.transpose(psO[g % 2][0:P, t * 128:(t + 1) * 128], oh[u][:, g * T + t, :], ident[:])
                    last.then_inc(S["ohT_done"], 1)

                def mm(g):
                    pe.wait_ge(S["ohT_saved"], b * B + g + 3)
                    if g == 0:
                        pe.wait_ge(S["ad_staged"], b + 1)
                    for t in range(T):
                        i = g * T + t
                        last = t_.matmul(psE[:, i * AW:(i + 1) * AW], ohT[g % 2][:, t * 128:(t + 1) * 128], adst[:, g, :], start=True, stop=True)
                    if g == B - 1:
                        last.then_inc(S["adE_done"], 1)
                tr(0)
                tr(1)
                mm(0)
                tr(2)
                mm(1)
                tr(3)
                mm(2)
                mm(3)

            def main(b, u, g):
                pe.wait_ge(S["msg_ready"], b * B + g + 1)
                pe.wait_ge(S["part_saved"], b * B + g + 1)
                for t in range(T):
                    last = t_.matmul(psP[g % 2][0:P, 0:MW], oh[u][:, g * T + t, :], ring[u][:, g * T + t, :], start=(t == 0), stop=(t == T - 1))
                last.then_inc(S["main_done"], 1)

            pe.sem_inc(S["main_done"], 2 * B)
            onehots_T(0, 0)

            def step(b, k, u, n, nk, j, last):
                pe.wait_ge(S["asc_ready"], b + 1)
                for t in range(T):
                    la = t_.transpose(psT[0:HB, t:GE:T], asc[:, t, :], ident[:])
                la.then_inc(S["asT_done"], 1)
                if n is not None and u == 0:
                    pe.wait_ge(xm_in[j], nk * 16 + 16)
                    for m in range(KD):
                        for c in range(KD):
                            la = t_.matmul(M0[:, m * P:(m + 1) * P], wq[:, c, m * 128:(m + 1) * 128], xm[j][:, c * P:(c + 1) * P], start=(c == 0), stop=(c == KD - 1))
                    la.then_inc(S["q_done"], 1)
                elif n is not None:
                    pe.wait_ge(S["n1_ready"], n + 1)
                    for m in range(KD):
                        la = t_.transpose(M1[:, m * P:(m + 1) * P], n1[:, m * 128:(m + 1) * 128], ident[0:P, 0:P])
                    la.then_inc(S["n1_turned"], 1)
                pe.wait_ge(S["scans_done"], b * 2 + 2)
                pe.sem_inc(S["apart"], 1)
                for t in range(T):
                    la = t_.transpose(psE[:, 384 + t * HB:384 + (t + 1) * HB], scb[:, t:GE:T], ident[0:HB, 0:HB])
                la.then_inc(S["sT_done"], 1)
                if n is not None and u == 0:
                    pe.wait_ge(S["qq_ready"], n + 1)
                    for i, w in enumerate((kvd, ksd)):
                        for m in range(KD):
                            o = (i * KD + m) * P
                            la = t_.matmul(M1[:, o:o + P], w[:, m, :], qq[:, m * P:(m + 1) * P], start=True, stop=True)
                    la.then_inc(S["nd_done"], 1)
                elif n is not None:
                    pe.wait_ge(S["n1T_ready"], n + 1)
                    for m in range(4):
                        for c in range(2 * KD):
                            r = (xm[j] if c < KD else n1T)[:, (c % KD) * P:(c % KD + 1) * P]
                            la = t_.matmul(M0[:, m * P:(m + 1) * P], w1[:, c, m * 128:(m + 1) * 128], r, start=(c == 0), stop=(c == 2 * KD - 1))
                    la.then_inc(S["w1_done"], 1)
                main(b, u, 0)
                main(b, u, 1)
                if n is not None and u == 0:
                    pe.wait_ge(S["msgT_ready"], n + 1)
                    for m in range(KD):
                        la = t_.matmul(M0[0:P, 0:D], msgT[:, m * P:(m + 1) * P], wm[:, m, :], start=(m == 0), stop=(m == KD - 1))
                    la.then_inc(S["wm_done"], 1)
                elif n is not None:
                    pe.wait_ge(S["hT_ready"], n + 1)
                    for m in range(4):
                        la = t_.matmul(M1[0:P, 0:D], hT[:, m, :], w2[:, m, :], start=(m == 0), stop=(m == 3))
                    la.then_inc(S["w2_done"], 1)
                main(b, u, 2)
                main(b, u, 3)
                if not last:
                    onehots_T(b + 1, 1 - u)
            steps(pe, step)

        @block.scalar
        def _(act):
            s = nc.scalar
            act.preload_act_table_set("natural_log_exp_and_others")
            act.sem_inc(S["ohT_saved"], 2)
            act.sem_inc(S["part_saved"], 2)
            act.sem_inc(S["mo_free"], 2)
            act.wait_ge(S["consts"], 1)

            def windows(b):
                return nc.values_load_multi_w_load_instructions(sched[0:1, 1, bass.ds(b * B + B, B)], engines=(act.engine,), min_val=0, max_val=NT)[1]

            def stage_logits(b):
                w = windows(b)
                if not (isinstance(b, int) and b == 0):
                    act.wait_ge(S["adE_done"], b)
                for g in range(B):
                    la = s.activation(adst[:, g, :], ad3[:, bass.ds(w[g], 1), :, :].rearrange("p a c h -> p (a c h)"), ACT.Copy)
                la.then_inc(S["ad_staged"], 1)

            def onehots_T(b):
                for g in range(B):
                    act.wait_ge(S["ohT_done"], b * B + g + 1)
                    s.activation(ohT[g % 2][:], psO[g % 2][0:P, :], ACT.Copy).then_inc(S["ohT_saved"], 1)
            stage_logits(0)
            onehots_T(0)

            def save(b, u, g):
                act.wait_ge(S["main_done"], b * B + (2 * B + g + 1))
                s.activation(part[u][:, g, :], psP[g % 2][0:P, 0:MW], ACT.Copy).then_inc(S["part_saved"], 1)

            def normalised(i, x, y, src):
                act.wait_ge(S["var_ready"], x + 1)
                s.activation(lnv[:, i, :], mv[:, i, 1:2], ACT.Ln, bias=epsc[0:P, 0:1]).then_inc(S["lnv_ready"], 1)
                s.activation(nm[:, i, :], mv[:, i, 0:1], ACT.Copy, scale=-1.0)
                act.wait_ge(S["lnv_ready"], x + 1)
                s.activation(rstd[:, i, :], lnv[:, i, :], ACT.Exp, scale=-0.5).then_inc(S["rstd_ready"], 1)
                act.wait_ge(S["rstd_ready"], x + 1)
                s.activation(nb[:, i, :], nm[:, i, :], ACT.Identity, scale=rstd[:, i, :], bias=epsc[0:P, 2:3]).then_inc(S["nb_ready"], 1)
                act.wait_ge(S["nb_ready"], x + 1)
                return s.activation(y[:], src, ACT.Identity, scale=rstd[:, i, :], bias=nb[:, i, :])

            def step(b, k, u, n, nk, j, last):
                act.wait_ge(gathered[u], k * (16 * BT) + 16 * BT)
                s.activation(asc[:].rearrange("p t (g h) -> p g t h", h=H), ringv(u)[:, :, :, C].rearrange("p (g t) h -> p g t h", t=T),
                             ACT.Copy).then_inc(S["asc_ready"], 1)
                if n is not None and u == 0:
                    act.wait_ge(S["q_done"], n + 1)
                    s.activation(qex[:], M0[:, 0:KD * P], ACT.Exp)
                    s.activation(qrl[:], M0[:, 0:KD * P], ACT.Relu).then_inc(S["qparts_ready"], 1)
                elif n is not None:
                    act.wait_ge(S["n1_turned"], n + 1)
                    s.activation(n1T[:], M1[:, 0:KD * P], ACT.Copy).then_inc(S["n1T_ready"], 1)
                act.wait_ge(S["eprep_done"], b + 1)
                s.activation(ringv(u)[:, :, :, C], df[:], ACT.Exp).then_inc(S["ex_done"], 1)
                if n is not None and u == 0:
                    act.wait_ge(S["nd_done"], n + 1)
                    s.activation(lden[:], M1[:, KD * P:2 * KD * P], ACT.Ln, bias=epsc[:, 1:2]).then_inc(S["den_ready"], 1)
                    act.wait_ge(S["den_ready"], n + 1)
                    s.activation(den[:], lden[:], ACT.Exp, scale=-1.0).then_inc(S["rden_ready"], 1)
                    save(b, u, 0)
                    save(b, u, 1)
                elif n is not None:
                    act.wait_ge(S["w1_done"], n + 1)
                    for m in range(4):
                        la = s.activation(hT[:, m, :], M0[:, m * P:(m + 1) * P], ACT.Relu, bias=bias1[:, m:m + 1])
                    la.then_inc(S["hT_ready"], 1)
                rescale(b, 1 - u)
                if not last:
                    stage_logits(b + 1)
                if n is None or u == 1:
                    save(b, u, 0)
                    save(b, u, 1)
                save(b, u, 2)
                if n is not None and u == 1:
                    act.wait_ge(S["w2_done"], n + 1)
                    normalised(1, n * 2 + 1, n2, M1[0:P, 0:D]).then_inc(S["n2_ready"], 1)
                save(b, u, 3)
                if not last:
                    onehots_T(b + 1)
                if n is not None and u == 0:
                    act.wait_ge(S["wm_done"], n + 1)
                    normalised(0, n * 2, n1, M0[0:P, 0:D]).then_inc(S["n1_ready"], 1)

            def rescale(b, u):
                act.wait_ge(S["dd_ready"], b + 1)
                s.activation(ww[u][:], dd[u][:], ACT.Exp).then_inc(S["ww_ready"], 1)
            steps(act, step)
            rescale(NB, 1)

        @block.vector
        def _(dve):
            d = nc.vector

            def places(b, u):
                dst = recs[u][:].bitcast(F32).rearrange("p g (t f) -> p g t f", f=4)[:, :, :, 1]
                d.tensor_tensor(dloc[:], dst, wbase[:, bass.ds(b * B, B)].unsqueeze(2).broadcast_to([128, B, T]), ALU.subtract).then_inc(S["dloc_ready"], 1)

            def onehots(b, u):
                dve.wait_ge(S["dloc_ready"], b + 1)
                for g in range(B):
                    d.tensor_tensor(oh[u][:, g * T:(g + 1) * T, :], iota_d[:].unsqueeze(1).broadcast_to([128, T, P]),
                                    dloc[:, g, :].unsqueeze(2).broadcast_to([128, T, P]), ALU.is_equal).then_inc(S["oh_ready"], 1)

            def windows(b):
                return nc.values_load_multi_w_load_instructions(sched[0:1, 1, bass.ds(b * B, B)], engines=(dve.engine,), min_val=0, max_val=NT)[1]

            d.memset(epsc[:, 0:1], LN_EPS)
            d.memset(epsc[:, 1:2], MIX_EPS)
            d.memset(epsc[:, 2:3], 0.0)
            d.memset(first[:], 0.0).then_inc(S["consts"], 1)
            dve.wait_ge(S["consts"], 1)
            d.memset(first[0:1, :, 0], 1.0).then_inc(S["consts"], 1)
            dve.wait_ge(rec_in[0], 16 * B)
            places(0, 0)
            onehots(0, 0)

            def accv(w):
                return acc[:, bass.ds(w, 1), :].rearrange("p a (h c) -> p (a h) c", c=CW)

            def statistics(i, x, src):
                d.bn_stats(st6[:, i, :], src).then_inc(S["st_ready"], 1)
                dve.wait_ge(S["st_ready"], x + 1)
                dve.sem_inc(S["apart"], 1)
                d.bn_aggr(mv[:, i, :], st6[:, i, :]).then_inc(S["var_ready"], 1)

            def presence(b, u):
                dve.wait_ge(S["part_saved"], b * B + 2)
                d.tensor_scalar(pm[:], part[u][:, :, MW - 1:MW], 1.0, BIG, ALU.subtract, ALU.mult).then_inc(S["pm_ready"], 1)

            def present_maxima(b, u):
                dve.wait_ge(S["pm_ready"], b + 1)
                d.tensor_tensor(sg[:], part[u][:, :, ROW:ROW + H], pm[:].broadcast_to([P, B, H]), ALU.add).then_inc(S["sg_ready"], 1)

            def running(w, g):
                return m_run[:, bass.ds(w[g], 1), :].rearrange("p a h -> p (a h)")

            def new_maximum(b, w, g):
                if g == 0:
                    dve.wait_ge(S["sg_ready"], b + 1)
                else:
                    dve.wait_ge(S["m_steps"], b * (3 * B) + 3 * g)
                d.tensor_tensor(mns[:, g, :], running(w, g), sg[:, g, :], ALU.max).then_inc(S["m_steps"], 1)

            def old_under_new(b, w, g, u):
                dve.wait_ge(S["m_steps"], b * (3 * B) + (3 * g + 1))
                d.tensor_tensor(dd[u][:, 0, g, :], running(w, g), mns[:, g, :], ALU.subtract).then_inc(S["m_steps"], 1)

            def kept_maximum(b, w, g):
                dve.wait_ge(S["m_steps"], b * (3 * B) + (3 * g + 2))
                d.tensor_tensor(running(w, g), running(w, g), sg[:, g, :], ALU.max).then_inc(S["m_steps"], 1)

            def batch_under_new(u):
                d.tensor_tensor(dd[u][:, 1], sg[:], mns[:], ALU.subtract).then_inc(S["dd_ready"], 1)

            def scaled_part(u, g):
                v = part[u][:, g, 0:ROW].rearrange("p (h c) -> p h c", c=CW)
                d.tensor_tensor(v, v, ww[u][:, 1, g, :].unsqueeze(2).broadcast_to([P, H, CW]), ALU.mult).then_inc(S["p_scaled"], 1)

            def scaled_sum(b, u, w, g):
                if g > 0:
                    dve.wait_ge(S["a_steps"], b * (2 * B) + 2 * g)
                a = accv(w[g])
                d.tensor_tensor(a, a, ww[u][:, 0, g, :].unsqueeze(2).broadcast_to([P, H, CW]), ALU.mult).then_inc(S["a_steps"], 1)

            def added(b, u, w, g):
                dve.wait_ge(S["p_scaled"], b * B + g + 1)
                dve.wait_ge(S["a_steps"], b * (2 * B) + (2 * g + 1))
                a = accv(w[g])
                d.tensor_tensor(a, a, part[u][:, g, 0:ROW].rearrange("p (h c) -> p h c", c=CW), ALU.add).then_inc(S["a_steps"], 1)

            def sums_added(b, u, w, between=None):
                dve.wait_ge(S["ww_ready"], b + 1)
                scaled_part(u, 0)
                for g in range(B):
                    scaled_sum(b, u, w, g)
                    if g + 1 < B:
                        scaled_part(u, g + 1)
                    added(b, u, w, g)
                    if g == 1 and between:
                        between()

            def step(b, k, u, n, nk, j, last):
                rv = ringv(u)
                o = 1 - u
                w = windows(b)
                dve.wait_ge(S["adE_done"], b + 1)
                d.tensor_reduce(ad_e[:], psE[:, 0:BT * AW].rearrange("p (i c h) -> p i h c", c=3, h=H), axis=X, op=ALU.add).then_inc(S["ad_summed"], 1)
                dve.wait_ge(pen_in[u], k * (16 * B) + 16 * B)
                dve.wait_ge(S["asT_done"], b + 1)
                d.tensor_tensor_scan(scf[:], pens[u][:, 0:GE], psT[0:HB, :], -BIG, ALU.add, ALU.max).then_inc(S["scans_done"], 1)
                presence(b, o)
                flags = recs[u][:].bitcast(F32).rearrange("p g (t f) -> p g t f", f=4)[:, :, :, 2]
                d.tensor_tensor(ring[u][:, :, MW - 1].rearrange("p (g t) -> p g t", t=T), flags, first[:], ALU.max).then_inc(S["flags_ready"], 1)
                dve.wait_ge(S["scans_done"], b * 2 + 1)
                d.tensor_tensor_scan(scb[:, ::-1], pens[u][:, GE:0:-1], scf[:, ::-1], -BIG, ALU.add, ALU.max).then_inc(S["scans_done"], 1)
                present_maxima(b, o)
                if n is not None and u == 0:
                    dve.wait_ge(S["qparts_ready"], n + 1)
                    d.scalar_tensor_tensor(qq[:], qex[:], 1.0, qrl[:], ALU.min, ALU.add).then_inc(S["qq_ready"], 1)
                dve.wait_ge(S["ad_summed"], b + 1)
                d.tensor_tensor(zz[:, 0], rv[:, :, :, C], ad_e[:], ALU.add)
                new_maximum(b, w, 0)
                dve.wait_ge(S["sT_done"], b + 1)
                d.tensor_tensor(zz[:, 1].rearrange("p (g t) h -> p t g h", t=T), psE[:, 384:512].rearrange("p (t g h) -> p t g h", t=T, h=H),
                                ad_e[:].rearrange("p (g t) h -> p t g h", t=T), ALU.add).then_inc(S["zz_ready"], 1)
                old_under_new(b, w, 0, o)
                dve.wait_ge(S["zz_ready"], b + 1)
                d.scalar_tensor_tensor(zz[:], zz[:], SLOPE, zz[:], ALU.mult, ALU.max).then_inc(S["al_ready"], 1)
                kept_maximum(b, w, 0)
                dve.wait_ge(S["al_ready"], b + 1)
                d.tensor_tensor(df[:], zz[:, 0], zz[:, 1], ALU.subtract).then_inc(S["eprep_done"], 1)
                new_maximum(b, w, 1)
                dve.wait_ge(S["flags_ready"], b + 1)
                d.tensor_tensor(ring[u][:, :, ROW:ROW + H], zz[:, 1], ring[u][:, :, MW - 1:MW].broadcast_to([128, BT, H]), ALU.mult)
                old_under_new(b, w, 1, o)

                def weigh(g):
                    if g == 0:
                        dve.wait_ge(S["ex_done"], b + 1)
                    q = slice(g * T, (g + 1) * T)
                    d.tensor_tensor(rv[:, q, :, 0:C], rv[:, q, :, 0:C], rv[:, q, :, C:CW].broadcast_to([128, T, H, C]), ALU.mult).then_inc(S["msg_ready"], 1)
                weigh(0)
                kept_maximum(b, w, 1)
                if n is not None and u == 0:
                    dve.wait_ge(S["rden_ready"], n + 1)
                    d.scalar_tensor_tensor(fix[:], M1[:, KD * P:2 * KD * P], MIX_EPS, den[:], ALU.add, ALU.mult).then_inc(S["fix_ready"], 1)
                weigh(1)
                if n is not None and u == 0:
                    dve.wait_ge(S["fix_ready"], n * 2 + 1)
                    d.scalar_tensor_tensor(den[:], fix[:], 2.0, den[:], ALU.subtract, ALU.mult).then_inc(S["fix_ready"], 1)
                new_maximum(b, w, 2)
                if n is not None and u == 0:
                    dve.wait_ge(S["fix_ready"], n * 2 + 2)
                    d.scalar_tensor_tensor(msgT[:], M1[:, 0:KD * P], float(-N), den[:], ALU.mult, ALU.mult).then_inc(S["msgT_ready"], 1)
                old_under_new(b, w, 2, o)
                weigh(2)
                kept_maximum(b, w, 2)
                weigh(3)
                new_maximum(b, w, 3)
                if not last:
                    dve.wait_ge(rec_in[o], (k + u) * (16 * B) + 16 * B)
                    places(b + 1, o)
                old_under_new(b, w, 3, o)
                batch_under_new(o)
                kept_maximum(b, w, 3)
                if not last:
                    onehots(b + 1, o)

                def mixed():
                    if n is not None:
                        dve.wait_ge(S["wm_done"] if u == 0 else S["w2_done"], n + 1)
                        statistics(u, n * 2 + u, (M0 if u == 0 else M1)[0:P, 0:D])
                sums_added(b, o, w, mixed)
                if n is not None and u == 1:
                    dve.wait_ge(S["n2_ready"], n + 1)
                    d.tensor_tensor(n2[:], n2[:], rows[:, 1, :], ALU.mult).then_inc(S["n2_scaled"], 1)
                    dve.wait_ge(S["n2_scaled"], n + 1)
                    dve.wait_ge(S["mo_free"], n + 1)
                    dve.wait_ge(xr_in[j], nk * 16 + 16)
                    d.tensor_tensor(mo[j][:], n2[:], xr[j][:], ALU.add).then_inc(S["mo_ready"], 1)

            d.memset(part[1][:], 0.0).then_inc(S["consts"], 1)
            dve.wait_ge(S["consts"], 3)
            steps(dve, step)
            w = windows(NB)
            presence(NB, 1)
            present_maxima(NB, 1)
            for g in range(B):
                new_maximum(NB, w, g)
                old_under_new(NB, w, g, 1)
                kept_maximum(NB, w, g)
            batch_under_new(1)
            sums_added(NB, 1, w)


def slices(nc, sb, ps, sem, linker, v):
    ident, ones, acc, wc, bc, rows = (v[k] for k in "ident ones acc wc bc rows".split())
    mix_d, swT_d, out = v["mix_d"], v["swT_d"], v["out"]
    TW = D + 1
    Q = 5
    with ExitStack() as ctx:
        gm = [sb(ctx, f"gm{i}", [P, D]) for i in range(2)]
        mixt = [sb(ctx, f"mixt{i}", [P, D]) for i in range(2)]
        rden = sb(ctx, "rden", [P, H])
        st6 = sb(ctx, "st6c", [P, 6])
        mv = sb(ctx, "mvc", [P, 2])
        lnv = sb(ctx, "lnvc", [P, 1])
        rstd = sb(ctx, "rstdc", [P, 1])
        nb = sb(ctx, "nbc", [P, 1])
        xn = [sb(ctx, f"xnc{i}", [P, TW]) for i in range(2)]
        xnT = [sb(ctx, f"xnTc{i}", [128, KD * P]) for i in range(2)]
        lg = [sb(ctx, f"lg{i}", [P, INNER]) for i in range(2)]
        ex = [sb(ctx, f"ex{i}", [P, INNER]) for i in range(2)]
        sw = [sb(ctx, f"sw{i}", [P, INNER]) for i in range(2)]
        swT = [sb(ctx, f"swT{i}", [128, 4 * P]) for i in range(2)]
        mx = [sb(ctx, f"mx{i}", [P, FH]) for i in range(2)]
        sm = [sb(ctx, f"sm{i}", [P, FH]) for i in range(2)]
        epsc = sb(ctx, "epscc", [128, 1])
        zer = sb(ctx, "zer", [128, TW])
        tok = sb(ctx, "tok", [128, 4, TW])
        tokT = sb(ctx, "tokT", [128, KD, 4, 128])
        wfx = sb(ctx, "wfx", [128, KD, INNER])
        bfx = sb(ctx, "bfx", [1, INNER])
        wqkv = sb(ctx, "wqkv", [FD, 3, FD])
        wo = sb(ctx, "wo", [FD, FH, D])
        nrow = sb(ctx, "nrow", [1, INNER])
        rrow = sb(ctx, "rrow", [1, INNER])
        rbc = sb(ctx, "rbc", [FD, INNER])
        stT = sb(ctx, "stT", [FD, INNER])
        qT = sb(ctx, "qT", [FD, INNER])
        kT = sb(ctx, "kT", [FD, INNER])
        vv = sb(ctx, "vv", [FD, INNER])
        sc = sb(ctx, "sc", [FD, INNER])
        se = sb(ctx, "se", [FD, INNER])
        aT = sb(ctx, "aT", [FD, INNER])
        smx = sb(ctx, "smx", [FD, FH])
        ssum = sb(ctx, "ssum", [FD, FH])
        osT = sb(ctx, "osT", [FD, INNER])
        mm = sb(ctx, "mm", [128, 4, D])
        back = [sb(ctx, f"back{i}", [128, 4 * P]) for i in range(Q)]
        ot = [sb(ctx, f"ot{i}", [P, D]) for i in range(Q)]
        res = [sb(ctx, f"res{i}", [P, D]) for i in range(Q)]
        psT = ps(ctx, "pC_T")
        psL = ps(ctx, "pC_L")
        psW = ps(ctx, "pC_W")
        psK = [ps(ctx, f"pC_K{i}") for i in range(4)]
        psY = ps(ctx, "pC_Y")
        names = """gm_ready sum_free x1_ready var_ready lnv_ready rstd_ready xn_ready xT_done xnT_ready lg_done lgb_ready mx_ready
            sub_ready ex_ready sm_ready sw_ready tok_done swT_done swT_ready swT_free chain apart consts weights_in swT_out
            pe_m dve_m act_m y_done y_read pchain""".split()
        S = {n: sem(ctx, "s_" + n) for n in names}
        mix_in = [sem(ctx, f"s_mix_in{i}") for i in range(2)]
        back_in = [sem(ctx, f"s_back_in{i}") for i in range(Q)]
        out_done = sem(ctx, "out_done")
        o_ready = sem(ctx, "o_ready")
        o_free = sem(ctx, "o_free")
        block = ctx.enter_context(nc.Block())

        def hd(a):
            return a.rearrange("p (h g) -> p h g", g=FD)

        def wide(a, p=P):
            return a.unsqueeze(2).broadcast_to([p, FH, FD])

        def pipeline(eng, head, body):
            head()
            with eng.Fori(0, NT // 2 - 1) as it:
                for u in range(2):
                    body(it * 2 + u, it, u, False)
            for u in range(2):
                body(NT - 2 + u, NT // 2 - 1, u, u == 1)

        @block.sync
        def _(sp):
            for u in range(2):
                sp.dma_start(mixt[u][:], mix_d[u * P:(u + 1) * P, :]).then_inc(mix_in[u], 16)
            sp.dma_start(wfx[:], v["W_fx"].rearrange("(k p) n -> p k n", p=128)).then_inc(S["weights_in"], 16)
            sp.dma_start(bfx[:], v["b_fx"].rearrange("(a n) -> a n", a=1)).then_inc(S["weights_in"], 16)
            for i, w in enumerate(("W_q", "W_k", "W_v")):
                sp.dma_start(wqkv[:, i, :], v[w]).then_inc(S["weights_in"], 16)
            sp.dma_start(wo[:], v["W_out"].rearrange("(h c) n -> c h n", c=FD)).then_inc(S["weights_in"], 16)

            def body(n, k, u, last):
                if not (isinstance(n, int)):
                    sp.wait_ge(S["x1_ready"], n + 1)
                    sp.dma_start(mixt[u][:], mix_d[bass.ds(n * P + 2 * P, P), :]).then_inc(mix_in[u], 16)
                sp.wait_ge(S["swT_ready"], n + 1)
                sp.dma_start(swT_d[bass.ds(n, 1), :, :].rearrange("a p n -> (a p) n"), swT[u][:]).then_inc(S["swT_out"], 16)
                sp.wait_ge(S["swT_out"], n * 16 + 16)
                sp.sem_inc(S["swT_free"], 1)
            pipeline(sp, lambda: None, body)
            for i in range(Q):
                sp.dma_start(back[i][:], swT_d[i, :, :]).then_inc(back_in[i], 16)
            with sp.Fori(0, NT // Q - 1) as it:
                for i in range(Q):
                    sp.wait_ge(S["y_done"], it * Q + i + 1)
                    sp.dma_start(back[i][:], swT_d[bass.ds(it * Q + (Q + i), 1), :, :].rearrange("a p n -> (a p) n")).then_inc(back_in[i], 16)

        @block.gpsimd
        def _(pool):
            g = nc.gpsimd

            def front(n, u, k):
                pool.wait_ge(S["gm_ready"], n + 1)
                g.tensor_tensor(gm[u][:], gm[u][:], rows[:, 0, :], ALU.add).then_inc(S["pchain"], 1)
                pool.wait_ge(S["pchain"], n + 1)
                pool.wait_ge(mix_in[u], k * 16 + 16)
                pool.sem_inc(S["apart"], 1)
                g.tensor_tensor(acc[:, bass.ds(n, 1), 0:D].rearrange("p a n -> p (a n)"), gm[u][:], mixt[u][:], ALU.add).then_inc(S["x1_ready"], 1)

            def body(n, k, u, last):
                pool.wait_ge(S["mx_ready"], n + 1)
                g.tensor_tensor(hd(lg[u][:]), hd(lg[u][:]), wide(mx[u][:]), ALU.subtract).then_inc(S["sub_ready"], 1)
                if not last:
                    front(n + 1, 1 - u, k + u)
                pool.wait_ge(S["sm_ready"], n + 1)
                g.tensor_tensor(hd(sw[u][:]), hd(ex[u][:]), wide(sm[u][:]), ALU.mult).then_inc(S["sw_ready"], 1)
            pipeline(pool, lambda: front(0, 0, 0), body)

        @block.scalar
        def _(act):
            s = nc.scalar
            act.preload_act_table_set("natural_log_exp_and_others")
            act.sem_inc(S["swT_free"], 2)
            act.wait_ge(S["consts"], 1)

            def front(n, u, k):
                act.wait_ge(S["var_ready"], n + 1)
                s.activation(lnv[:], mv[:, 1:2], ACT.Ln, bias=epsc[0:P, :]).then_inc(S["lnv_ready"], 1)
                act.wait_ge(S["lnv_ready"], n + 1)
                s.activation(rstd[:], lnv[:], ACT.Exp, scale=-0.5).then_inc(S["rstd_ready"], 1)
                act.wait_ge(S["xT_done"], n + 1)
                s.activation(xnT[u][:], psT[:, 0:KD * P], ACT.Copy).then_inc(S["xnT_ready"], 1)

            def body(n, k, u, last):
                act.wait_ge(S["sub_ready"], n + 1)
                s.activation(ex[u][:], lg[u][:], ACT.Exp).then_inc(S["ex_ready"], 1)
                if not last:
                    front(n + 1, 1 - u, k + u)
                act.wait_ge(S["swT_done"], n + 1)
                act.wait_ge(S["swT_free"], n + 1)
                s.activation(swT[u][:], psW[:, 0:4 * P], ACT.Copy).then_inc(S["swT_ready"], 1)
            pipeline(act, lambda: front(0, 0, 0), body)
            act.wait_ge(S["dve_m"], 9)
            s.activation(se[:], sc[:], ACT.Exp, scale=float(FD) ** -0.5).then_inc(S["act_m"], 1)
            act.sem_inc(o_free, Q)
            with act.Fori(0, NT // Q) as it:
                for i in range(Q):
                    act.wait_ge(o_ready, it * Q + i + 1)
                    act.dma_start(out[bass.ds((it * Q + i) * P, P), :], res[i][:]).then_inc(out_done, 16)
                act.wait_ge(out_done, it * (16 * Q) + 16 * Q)
                act.sem_inc(o_free, Q)

        @block.vector
        def _(dve):
            d = nc.vector
            d.memset(epsc[:], LN_EPS)
            d.memset(zer[:], 0.0)
            for u in range(2):
                la = d.memset(xn[u][:, D:TW], 1.0)
            la.then_inc(S["consts"], 1)
            dve.wait_ge(S["consts"], 1)
            KF, KS = 4, 1

            def front(n, u, k, lk):
                a = acc[:, bass.ds(n, 1), :].rearrange("p a (h c) -> p (a h) c", c=CW)
                lk(d.tensor_scalar(rden[:], a[:, :, C], DEN_EPS, None, ALU.add))
                lk(d.reciprocal(rden[:], rden[:]))
                d.tensor_tensor(gm[u][:].rearrange("p (h c) -> p h c", c=C), a[:, :, 0:C], rden[:].unsqueeze(2).broadcast_to([P, H, C]),
                                ALU.mult).then_inc(S["gm_ready"], 1)

            def front2(n, u, k, lk):
                x1 = acc[:, bass.ds(n, 1), 0:D].rearrange("p a n -> p (a n)")
                dve.wait_ge(S["x1_ready"], n + 1)
                dve.sem_inc(S["apart"], 1)
                lk(d.bn_stats(st6[:], x1))
                dve.sem_inc(S["apart"], 1)
                d.bn_aggr(mv[:], st6[:]).then_inc(S["var_ready"], 1)
                dve.wait_ge(S["rstd_ready"], n + 1)
                if not (isinstance(n, int) and n == 0):
                    dve.wait_ge(S["tok_done"], n)
                lk(d.scalar_tensor_tensor(nb[:], mv[:, 0:1], -1.0, rstd[:], ALU.mult, ALU.mult))
                d.tensor_scalar(xn[u][:, 0:D], x1, rstd[:], nb[:], ALU.mult, ALU.add).then_inc(S["xn_ready"], 1)

            def head():
                lk = linker(dve, S["chain"])
                front(0, 0, 0, lk)
                front2(0, 0, 0, lk)
                assert lk.count[0] == KF

            def body(n, k, u, last):
                lk = linker(dve, S["chain"], n * (KF + KS) + KF)
                dve.wait_ge(S["lg_done"], n + 1)
                d.tensor_tensor(lg[u][:], psL[0:P, :], bc[:], ALU.add).then_inc(S["lgb_ready"], 1)
                dve.wait_ge(S["lgb_ready"], n + 1)
                d.tensor_reduce(mx[u][:], hd(lg[u][:]), axis=X, op=ALU.max).then_inc(S["mx_ready"], 1)
                if not last:
                    front(n + 1, 1 - u, k + u, lk)
                dve.wait_ge(S["ex_ready"], n + 1)
                lk(d.tensor_reduce(sm[u][:], hd(ex[u][:]), axis=X, op=ALU.add))
                d.reciprocal(sm[u][:], sm[u][:]).then_inc(S["sm_ready"], 1)
                if not last:
                    front2(n + 1, 1 - u, k + u, lk)
                    assert lk.count[0] == KF + KS
            pipeline(dve, head, body)

            done = linker(dve, S["dve_m"])
            dve.wait_ge(S["pe_m"], 1)
            for j in range(4):
                la = d.tensor_copy(tok[:, j, :], psK[j][:, 0:TW])
            done(la)
            dve.wait_ge(S["pe_m"], 2)
            for k in range(KD):
                d.tensor_copy(tokT[:, k, :, :], psK[k][:, :].rearrange("p (j n) -> p j n", j=4))
            la = d.tensor_copy(nrow[:], psK[2][0:1, :])
            done(la)
            done(d.tensor_scalar(rrow[:], nrow[:], TOK_EPS, None, ALU.add))
            done(d.reciprocal(rrow[:], rrow[:]))
            dve.wait_ge(S["pe_m"], 3)
            done(d.tensor_copy(rbc[:], psK[3][0:FD, :]))
            done(d.tensor_tensor(stT[:], psL[0:FD, :], rbc[:], ALU.mult))
            dve.wait_ge(S["pe_m"], 4)
            d.tensor_copy(qT[:], psK[0][0:FD, :])
            d.tensor_copy(kT[:], psK[1][0:FD, :])
            done(d.tensor_copy(vv[:], psK[2][0:FD, :]))
            dve.wait_ge(S["pe_m"], 5)
            done(d.tensor_reduce(smx[:], hd(psL[0:FD, :]), axis=X, op=ALU.max))
            done(d.tensor_tensor(hd(sc[:]), hd(psL[0:FD, :]), wide(smx[:], FD), ALU.subtract))
            dve.wait_ge(S["act_m"], 1)
            done(d.tensor_reduce(ssum[:], hd(se[:]), axis=X, op=ALU.add))
            done(d.reciprocal(ssum[:], ssum[:]))
            done(d.tensor_tensor(hd(se[:]), hd(se[:]), wide(ssum[:], FD), ALU.mult))
            dve.wait_ge(S["pe_m"], 6)
            done(d.tensor_copy(aT[:], psK[3][0:FD, :]))
            dve.wait_ge(S["pe_m"], 7)
            done(d.tensor_copy(osT[:], psL[0:FD, :]))
            dve.wait_ge(S["pe_m"], 8)
            for j in range(4):
                d.tensor_copy(mm[0:FD, j, :], psK[j][0:FD, 0:D])
                la = d.tensor_copy(mm[FD:, j, :], psK[j][FD:, D:2 * D])
            done(la)
            with dve.Fori(0, NT // Q) as it:
                for i in range(Q):
                    n = it * Q + i
                    dve.wait_ge(S["y_done"], n + 1)
                    d.tensor_tensor(ot[i][:], psK[i % 4][0:P, 0:D] if i < 4 else psL[0:P, 0:D], rows[:, 3, :], ALU.add).then_inc(S["y_read"], 1)
                    dve.wait_ge(S["y_read"], n + (Q + 1))
                    dve.wait_ge(o_free, n + 1)
                    d.tensor_tensor(res[i][:], ot[i][:], acc[:, bass.ds(n, 1), 0:D].rearrange("p a n -> p (a n)"), ALU.add).then_inc(o_ready, 1)

        @block.tensor
        def _(pe):
            t_ = nc.tensor

            def front(n, u, k):
                pe.wait_ge(S["xn_ready"], n + 1)
                for c in range(KD):
                    la = t_.transpose(psT[:, c * P:(c + 1) * P], xn[u][:, c * 128:(c + 1) * 128], ident[0:P, 0:P])
                la.then_inc(S["xT_done"], 1)
                pe.wait_ge(S["xnT_ready"], n + 1)
                for c in range(KD):
                    la = t_.matmul(psL[0:P, :], xnT[u][:, c * P:(c + 1) * P], wc[:, c, :], start=(c == 0), stop=(c == KD - 1))
                la.then_inc(S["lg_done"], 1)

            def body(n, k, u, last):
                if not last:
                    front(n + 1, 1 - u, k + u)
                pe.wait_ge(S["sw_ready"], n + 1)
                for j in range(4):
                    la = t_.matmul(psK[j][:, 0:TW], sw[u][:, j * 128:(j + 1) * 128], xn[u][:], start=False, stop=False)
                la.then_inc(S["tok_done"], 1)
                for j in range(4):
                    la = t_.transpose(psW[:, j * P:(j + 1) * P], sw[u][:, j * 128:(j + 1) * 128], ident[0:P, 0:P])
                la.then_inc(S["swT_done"], 1)

            def head():
                pe.wait_ge(S["consts"], 1)
                for j in range(4):
                    t_.matmul(psK[j][:, 0:TW], zer[:, 0:128], zer[:, 0:TW], start=True, stop=False)
                pe.sem_inc(S["tok_done"], 1)
                front(0, 0, 0)
            pipeline(pe, head, body)
            for j in range(4):
                la = t_.matmul(psK[j][:, 0:TW], zer[:, 0:128], zer[:, 0:TW], start=False, stop=True)
            la.then_inc(S["pe_m"], 1)
            pe.wait_ge(S["dve_m"], 1)
            for k in range(KD):
                for j in range(4):
                    t_.transpose(psK[k][:, j * 128:(j + 1) * 128], tok[:, j, k * 128:(k + 1) * 128], ident[:])
            for j in range(4):
                la = t_.matmul(psK[2][0:1, j * 128:(j + 1) * 128], tok[:, j, D:TW], ident[:], start=True, stop=True)
            la.then_inc(S["pe_m"], 1)
            pe.wait_ge(S["dve_m"], 4)
            pe.wait_ge(S["weights_in"], 16 * 6)
            t_.matmul(psK[3][0:FD, :], ones[0:1, 0:FD], rrow[:], start=True, stop=True)
            for h in range(FH):
                q = slice(h * FD, (h + 1) * FD)
                for k in range(KD):
                    t_.matmul(psL[0:FD, q], wfx[:, k, q], tokT[:, k, :, :].rearrange("p j n -> p (j n)")[:, q], start=(k == 0), stop=False)
                la = t_.matmul(psL[0:FD, q], bfx[:, q], nrow[:, q], start=False, stop=True)
            la.then_inc(S["pe_m"], 1)
            pe.wait_ge(S["dve_m"], 6)
            for i in range(2):
                t_.matmul(psK[i][0:FD, :], wqkv[:, i, :], stT[:], start=True, stop=True)
            for h in range(FH):
                q = slice(h * FD, (h + 1) * FD)
                la = t_.matmul(psK[2][0:FD, q], stT[:, q], wqkv[:, 2, :], start=True, stop=True)
            la.then_inc(S["pe_m"], 1)
            pe.wait_ge(S["dve_m"], 7)
            for h in range(FH):
                q = slice(h * FD, (h + 1) * FD)
                la = t_.matmul(psL[0:FD, q], qT[:, q], kT[:, q], start=True, stop=True)
            la.then_inc(S["pe_m"], 1)
            pe.wait_ge(S["dve_m"], 12)
            for h in range(FH):
                q = slice(h * FD, (h + 1) * FD)
                la = t_.transpose(psK[3][0:FD, q], se[:, q], ident[0:FD, 0:FD])
            la.then_inc(S["pe_m"], 1)
            pe.wait_ge(S["dve_m"], 13)
            for h in range(FH):
                q = slice(h * FD, (h + 1) * FD)
                la = t_.matmul(psL[0:FD, q], vv[:, q], aT[:, q], start=True, stop=True)
            la.then_inc(S["pe_m"], 1)
            pe.wait_ge(S["dve_m"], 14)
            for j in range(4):
                for i in range(2):
                    la = t_.matmul(psK[j][:, i * D:(i + 1) * D], osT[:, j * 128:(j + 1) * 128], wo[:, 2 * j + i, :], start=True, stop=True)
            la.then_inc(S["pe_m"], 1)
            pe.wait_ge(S["dve_m"], 15)
            pe.sem_inc(S["y_read"], Q)
            with pe.Fori(0, NT // Q) as it:
                for i in range(Q):
                    n = it * Q + i
                    pe.wait_ge(back_in[i], it * 16 + 16)
                    bank = psK[i % 4] if i < 4 else psL
                    pe.wait_ge(S["y_read"], n + 1)
                    for j in range(4):
                        la = t_.matmul(bank[0:P, 0:D], back[i][:, j * P:(j + 1) * P], mm[:, j, :], start=(j == 0), stop=(j == 3))
                    la.then_inc(S["y_done"], 1)


_INS = ['x', 'src', 'dst', 'L0_gnn_W', 'L0_gnn_att_src', 'L0_gnn_att_dst', 'L0_gnn_bias', 'L0_mix_Wq', 'L0_mix_Wk', 'L0_mix_Wv',
        'L0_mix_Wm', 'L0_mix_W1', 'L0_mix_W2', 'L0_mix_g1', 'L0_mix_b1', 'L0_mix_g2', 'L0_mix_b2', 'L0_ffn_W_fx', 'L0_ffn_b_fx',
        'L0_ffn_W_x', 'L0_ffn_b_x', 'L0_ffn_W_slice', 'L0_ffn_b_slice', 'L0_ffn_W_q', 'L0_ffn_W_k', 'L0_ffn_W_v', 'L0_ffn_W_out',
        'L0_ffn_b_out', 'L0_ffn_temperature']


def kernel(**inputs):
    import numpy as _np
    import concourse.bacc as _bacc
    from concourse import mybir as _mybir
    from concourse.bass_utils import run_bass_kernel_spmd as _run

    nc = _bacc.Bacc("TRN2", target_bir_lowering=False, num_devices=1)
    arrays, args = {}, []
    for name in _INS:
        a = _np.ascontiguousarray(inputs[name])
        arrays[f"in_{name}_dram"] = a
        args.append(nc.dram_tensor(f"in_{name}_dram", a.shape, _mybir.dt.from_np(a.dtype), kind="ExternalInput").ap())
    out = nc.dram_tensor("out_0_dram", (N, D), F32, kind="ExternalOutput").ap()
    program(nc, *args, out)
    r = _run(nc, [arrays], core_ids=[0])
    return r.results[0]["out_0_dram"]
```

```python
import concourse.bass as bass
from concourse import mybir
from contextlib import ExitStack

F32 = mybir.dt.float32
I32 = mybir.dt.int32
BF16 = mybir.dt.bfloat16
ALU = mybir.AluOpType
ACT = mybir.ActivationFunctionType
X = mybir.AxisListType.X

N, E, D = 6250, 200000, 256
H, C = 8, 32
P = 125
NT = N // P
KD = D // 128
CW = C + 1
ROW = H * CW
W1C = NT + 1
T = 4
GE = 128 * T
NG = 448
assert NG >= -(-E // GE) + NT
B = 4
NB = NG // B
HALF = E // P
FH, FD = 8, 64
INNER = FH * FD
BIG = 1.0e38
SLOPE = 0.2
LN_EPS = 1e-5
MIX_EPS = 1e-6
TOK_EPS = 1e-5
DEN_EPS = 1e-16
MW = ROW + H + 1


def program(nc, x, src, dst, gnn_W, att_src, att_dst, gnn_bias, Wq, Wk, Wv, Wm, W1, W2, g1, b1, g2, b2,
            W_fx, b_fx, W_x, b_x, W_slice, b_slice, W_q, W_k, W_v, W_out, b_out, temperature, out):
    h_tab = nc.dram_tensor("h_tab", (N, ROW), F32, kind="Internal").ap()
    rec = nc.dram_tensor("rec", (E + GE, 4), I32, kind="Internal").ap()
    pen = nc.dram_tensor("pen", (E + GE + 8,), F32, kind="Internal").ap()
    xnT_d = nc.dram_tensor("xnT_d", (NT + 2, 128, KD * P), F32, kind="Internal").ap()
    mix_d = nc.dram_tensor("mix_d", (N, D), F32, kind="Internal").ap()
    xpx_d = nc.dram_tensor("xpx_d", (N, D), F32, kind="Internal").ap()
    swT_d = nc.dram_tensor("swT_d", (NT, 128, 4 * P), F32, kind="Internal").ap()

    top = ExitStack()

    def sb(ctx, name, shape, dt=F32):
        return ctx.enter_context(nc.sbuf_tensor(name, shape, dt))

    def ps(ctx, name, shape=(128, 512)):
        return ctx.enter_context(nc.psum_tensor(name, list(shape), F32))

    def sem(ctx, name):
        return ctx.enter_context(nc.semaphore(name))

    def linker(eng, s, base=0):
        n = [0]

        def link(ins):
            n[0] += 1
            ins.then_inc(s, 1)
            eng.wait_ge(s, base + n[0])
        link.count = n
        return link

    with top:
        ident = sb(top, "ident", [128, 128])
        ones = sb(top, "ones", [128, 128])
        iota_d = sb(top, "iota_d", [128, P])
        wbase = sb(top, "wbase", [128, NG])
        sched = sb(top, "sched", [1, 2, B + NG], I32)
        acc = sb(top, "acc", [P, W1C, ROW])
        ad_all = sb(top, "ad_all", [P, W1C, H])
        m_run = sb(top, "m_run", [P, W1C, H])
        wq = sb(top, "wq", [128, KD, D])
        wm = sb(top, "wm", [128, KD, D])
        w1 = sb(top, "w1", [128, 2 * KD, 2 * D])
        bias1 = sb(top, "bias1", [128, 4])
        w2 = sb(top, "w2", [128, 2 * KD, D])
        rows = sb(top, "rows", [P, 4, D])
        wc = sb(top, "wc", [128, KD, INNER])
        bc = sb(top, "bc", [P, INNER])
        kvd = sb(top, "kvd", [128, KD, 128])
        ksd = sb(top, "ksd", [128, KD, 128])
        ad3 = sb(top, "ad3", [P, W1C, 3, H], BF16)

        apart = sem(top, "apart")
        mix_in, swT_out, back_in = ([sem(top, f"{name}{i}") for i in range(5)] for name in ("mix_in", "swT_out", "back_in"))

        out_done, o_free, o_ready = (sem(top, name) for name in ("out_done", "o_free", "o_ready"))

        prologue(nc, sb, ps, sem, linker, locals())
        edges_and_mix(nc, sb, ps, sem, linker, locals())
        slices(nc, sb, ps, sem, linker, locals())


def pipeline(eng, unroll, stages):
    lead = max(a for a, _ in stages)
    assert lead <= unroll and NT % unroll == 0
    for n in range(-lead, 0):
        for a, step in stages:
            if n + a >= 0:
                step(n + a, (n + a) // unroll, (n + a) % unroll)
    with eng.Fori(0, NT // unroll - 1) as it:
        for i in range(unroll):
            for a, step in stages:
                step(it * unroll + (i + a), it + (i + a) // unroll, (i + a) % unroll)
    for n in range(NT - unroll, NT):
        for a, step in stages:
            if n + a < NT:
                step(n + a, (n + a) // unroll, (n + a) % unroll)


def prologue(nc, sb, ps, sem, linker, v):
    x, src, dst = v["x"], v["src"], v["dst"]
    ident, ones, iota_d, wbase, sched = v["ident"], v["ones"], v["iota_d"], v["wbase"], v["sched"]
    acc, ad_all, m_run = v["acc"], v["ad_all"], v["m_run"]
    h_tab, rec, pen, xnT_d, xpx_d = v["h_tab"], v["rec"], v["pen"], v["xnT_d"], v["xpx_d"]
    wq, wm, w1, w2, rows, bias1, wc, bc, kvd, ksd, ad3 = (v[k] for k in "wq wm w1 w2 rows bias1 wc bc kvd ksd ad3".split())
    with ExitStack() as ctx:
        wkv = sb(ctx, "wkv", [128, KD, 2 * D])
        kex = sb(ctx, "kex", [P, D])
        krl = sb(ctx, "krl", [P, D])
        kk = sb(ctx, "kk", [P, 2, D])
        vst = sb(ctx, "vst", [P, 2, KD, 129])
        kvs = sb(ctx, "kvs", [128, KD, 129])
        zeros = sb(ctx, "zeros", [128, KD * 129])
        adr = sb(ctx, "adr", [P, NT, H])
        wg = sb(ctx, "wg", [128, KD, ROW + H])
        wraw = sb(ctx, "wraw", [128, KD, D])
        att = sb(ctx, "att", [128, 2, D])
        prod = sb(ctx, "prod", [128, 2, KD, D])
        src_i = sb(ctx, "src_i", [P, HALF], I32)
        dst_i = sb(ctx, "dst_i", [P, HALF + 1], I32)
        dst_f = sb(ctx, "dst_f", [P, HALF + 1])
        start = sb(ctx, "start", [P, HALF])
        recs = sb(ctx, "recs", [P, HALF, 4], I32)
        pad = sb(ctx, "pad", [128, T, 4], I32)
        padp = sb(ctx, "padp", [1, GE + 8])
        junk = sb(ctx, "junk", [P, HALF], mybir.dt.bfloat16)
        cnt = sb(ctx, "cnt", [P, W1C])
        cdiff = sb(ctx, "cdiff", [P, W1C])
        thr = sb(ctx, "thr", [P, W1C])
        iota_g = sb(ctx, "iota_g", [W1C, NG])
        iota_k = sb(ctx, "iota_k", [W1C, E // GE + 1])
        kjunk = sb(ctx, "kjunk", [W1C, E // GE + 1])
        wcol = sb(ctx, "wcol", [W1C, 1])
        wrep = sb(ctx, "wrep", [W1C, 128])
        below = sb(ctx, "below", [W1C, W1C])
        big50 = sb(ctx, "big50", [W1C, 1])
        cols = sb(ctx, "cols", [W1C, 6])
        ind = sb(ctx, "ind", [W1C, NG])
        ind2 = sb(ctx, "ind2", [W1C, NG])
        sch_f = sb(ctx, "sch_f", [1, 3, NG])
        xn = sb(ctx, "xn", [P, 2, D])
        xpx = sb(ctx, "xpx", [P, 2, D])
        st6 = sb(ctx, "st6", [P, 2, 6])
        mv = sb(ctx, "mv", [P, 2, 2])
        lnv = sb(ctx, "lnv", [P, 2, 1])
        rstd = sb(ctx, "rstd", [P, 2, 1])
        nb = sb(ctx, "nb", [P, 2, 1])
        xnT = sb(ctx, "xnT", [128, 2, KD * P])
        vcols = sb(ctx, "vcols", [128, 2, KD])
        wx = sb(ctx, "wx", [128, KD, INNER])
        wxT = sb(ctx, "wxT", [128, 4, D])
        wsl = sb(ctx, "wsl", [128, 128])
        bxc = sb(ctx, "bxc", [128, 4])
        brow = sb(ctx, "brow", [1, INNER])
        bsl = sb(ctx, "bsl", [1, FD])
        tmp1 = sb(ctx, "tmp1", [1, FH])
        itemp = sb(ctx, "itemp", [128, FH])
        zcol = sb(ctx, "zcol", [128, 2])
        psT = [ps(ctx, "pA_T"), ps(ctx, "pA_X")]
        psH = [ps(ctx, "pA_H"), ps(ctx, "pA_K")]
        psM = ps(ctx, "pA_M")
        psS = ps(ctx, "pA_S")
        psW = ps(ctx, "pA_W")
        psR = ps(ctx, "pA_R")

        edges_in = sem(ctx, "edges_in")
        weights_in = sem(ctx, "weights_in")
        late_in = sem(ctx, "late_in")
        x_in = sem(ctx, "x_in")
        x_read = sem(ctx, "x_read")
        xn_free = sem(ctx, "xn_free")
        xnT_free = sem(ctx, "xnT_free")
        consts = sem(ctx, "consts")
        dstf_ready = sem(ctx, "dstf_ready")
        pool_chain = sem(ctx, "pool_chain")
        dve_chain = sem(ctx, "dve_chain")
        pro_out = sem(ctx, "pro_out")
        var_ready = sem(ctx, "var_ready")
        lnv_ready = sem(ctx, "lnv_ready")
        st_ready = sem(ctx, "st_ready")
        nb_ready = sem(ctx, "nb_ready")
        rstd_ready = sem(ctx, "rstd_ready")
        xn_ready = sem(ctx, "xn_ready")
        xpx_ready = sem(ctx, "xpx_ready")
        xpx_out = [sem(ctx, f"xpx_out{i}") for i in range(2)]
        xpx_free = sem(ctx, "xpx_free")
        rows_in = sem(ctx, "rows_in")
        kvw_in = sem(ctx, "kvw_in")
        xT_done = sem(ctx, "xT_done")
        xnT_ready = sem(ctx, "xnT_ready")
        xnT_out = [sem(ctx, f"xnT_out{i}") for i in range(2)]
        k_done = sem(ctx, "k_done")
        kparts_ready = sem(ctx, "kparts_ready")
        v_saved = sem(ctx, "v_saved")
        kk_ready = sem(ctx, "kk_ready")
        kv_closed = sem(ctx, "kv_closed")
        setup = sem(ctx, "setup")
        wg_ready = sem(ctx, "wg_ready")
        h_done = sem(ctx, "h_done")
        h_saved = sem(ctx, "h_saved")
        ad_saved = sem(ctx, "ad_saved")
        tab_out = sem(ctx, "tab_out")
        cnt_ready = sem(ctx, "cnt_ready")
        pe_s = sem(ctx, "sched_products")
        dve_s = sem(ctx, "sched_steps")
        pe_w = sem(ctx, "weight_products")
        dve_w = sem(ctx, "weight_steps")
        apart = v["apart"]
        block = ctx.enter_context(nc.Block())

        @block.sync
        def _(sp):
            sp.dma_start(wraw[:], v["gnn_W"].rearrange("(k p) n -> p k n", p=128)).then_inc(weights_in, 16)
            sp.dma_start(att[:, 0, :], v["att_src"].rearrange("h c -> (h c)").partition_broadcast(128)).then_inc(weights_in, 16)
            sp.dma_start(att[:, 1, :], v["att_dst"].rearrange("h c -> (h c)").partition_broadcast(128)).then_inc(weights_in, 16)
            sp.wait_ge(edges_in, 48)
            sp.dma_start(acc[:, 0:NT, 0:D], x.rearrange("(t p) n -> p t n", p=P)).then_inc(x_in, 16)

            def store(t, q, u):
                sp.wait_ge(xnT_ready, t + 1)
                sp.dma_start(xnT_d[bass.ds(t, 1), :, :].rearrange("a p n -> (a p) n"), xnT[:, u, :]).then_inc(xnT_out[u], 16)

            def free(t, q, u):
                sp.wait_ge(h_saved, t + 1)
                sp.dma_start(h_tab[bass.ds(t * P, P), :], acc[:, bass.ds(t, 1), :].rearrange("p a n -> p (a n)")).then_inc(tab_out, 16)
                sp.wait_ge(xnT_out[u], q * 16 + 16)
                sp.sem_inc(xnT_free, 1)
            pipeline(sp, 2, [(1, store), (0, free)])
            for u in range(2):
                sp.dma_start(xnT_d[NT + u, :, :], xnT[:, u, :]).then_inc(xnT_out[u], 16)
            for u in range(2):
                sp.wait_ge(xnT_out[u], 16 * (NT // 2 + 1))
            sp.wait_ge(tab_out, 16 * NT)

        @block.gpsimd
        def _(pool):
            link = linker(pool, pool_chain)
            g = nc.gpsimd
            g.memset(dst_i[0:1, 0:1], -1).then_inc(consts, 1)
            pool.wait_ge(consts, 1)
            pool.dma_start(src_i[:], src.rearrange("(p n) -> p n", p=P)).then_inc(edges_in, 16)
            pool.dma_start(dst_i[:, 1:], dst.rearrange("(p n) -> p n", p=P)).then_inc(edges_in, 16)
            pool.dma_start(dst_i[1:P, 0:1], dst.rearrange("(p n) -> p n", p=P)[0:P - 1, HALF - 1:HALF],
                           allow_slow_non_contiguous=True).then_inc(edges_in, 16)
            link(g.memset(ident[:], 0.0))
            g.affine_select(out=ident[:], in_=ident[:], compare_op=ALU.not_equal, fill=1.0, base=0,
                            pattern=[[-1, 128]], channel_multiplier=1).then_inc(consts, 1)
            g.memset(ones[:], 1.0).then_inc(consts, 1)
            g.iota(iota_d[:], [[1, P]], base=0, channel_multiplier=0, allow_small_or_imprecise_dtypes=True).then_inc(consts, 1)
            g.iota(thr[:], [[P, W1C]], base=0, channel_multiplier=0, allow_small_or_imprecise_dtypes=True).then_inc(consts, 1)
            g.iota(iota_g[:], [[1, NG]], base=0, channel_multiplier=0, allow_small_or_imprecise_dtypes=True).then_inc(consts, 1)
            g.iota(iota_k[:], [[GE, E // GE + 1]], base=0, channel_multiplier=0, allow_small_or_imprecise_dtypes=True).then_inc(consts, 1)
            g.iota(wcol[:], [[0, 1]], base=0, channel_multiplier=1, allow_small_or_imprecise_dtypes=True).then_inc(consts, 1)
            g.iota(wrep[:], [[0, 128]], base=0, channel_multiplier=P, allow_small_or_imprecise_dtypes=True).then_inc(consts, 1)
            link(g.memset(below[:], 1.0))
            g.affine_select(out=below[:], in_=below[:], compare_op=ALU.is_gt, fill=0.0, base=0,
                            pattern=[[1, W1C]], channel_multiplier=-1).then_inc(consts, 1)
            link(g.memset(big50[:], 0.0))
            g.affine_select(out=big50[:], in_=big50[:], compare_op=ALU.not_equal, fill=1.0e6, base=-NT,
                            pattern=[[0, 1]], channel_multiplier=1).then_inc(consts, 1)
            g.memset(zcol[:], LN_EPS).then_inc(consts, 1)
            g.memset(acc[:, NT, :], 0.0)
            g.memset(ad_all[:, NT, :], 0.0)
            g.memset(m_run[:, NT, :], 0.0)
            g.memset(wsl[:], 0.0).then_inc(consts, 1)
            g.memset(pad[:, :, 0], 0)
            g.memset(pad[:, :, 1].bitcast(F32), -1.0)
            g.memset(pad[:, :, 2].bitcast(F32), 1.0)
            g.memset(pad[:, :, 3], 0)
            link(g.memset(padp[:], -BIG))
            pool.dma_start(rec[E:E + GE, :].rearrange("(p t) f -> p (t f)", p=128), pad[:].rearrange("p t f -> p (t f)")).then_inc(pro_out, 16)
            pool.dma_start(pen[E:E + GE + 8].rearrange("(a n) -> a n", a=1), padp[:]).then_inc(pro_out, 16)
            pool.wait_ge(edges_in, 48)
            g.tensor_copy(dst_f[:], dst_i[:]).then_inc(dstf_ready, 1)
            pool.wait_ge(dstf_ready, 1)
            link(g.tensor_tensor(start[:], dst_f[:, 1:], dst_f[:, :HALF], ALU.subtract))
            link(g.tensor_scalar(start[:], start[:], 0.0, None, ALU.is_gt))
            g.tensor_copy(recs[:, :, 0], src_i[:])
            g.tensor_copy(recs[:, :, 1].bitcast(F32), dst_f[:, 1:])
            g.memset(recs[:, :, 3], 0)
            link(g.tensor_copy(recs[:, :, 2].bitcast(F32), start[:]))
            pool.dma_start(rec[0:E, :].rearrange("(p n) f -> p (n f)", p=P), recs[:].rearrange("p n f -> p (n f)")).then_inc(pro_out, 16)
            link(g.tensor_scalar(start[:], start[:], -BIG, None, ALU.mult))
            pool.dma_start(pen[0:E].rearrange("(p n) -> p n", p=P), start[:]).then_inc(pro_out, 16)
            pool.wait_ge(rows_in, 64)
            link(g.tensor_tensor(rows[:, 2, :], rows[:, 2, :], rows[:, 0, :], ALU.add))

            def residual(t, q, u):
                pool.wait_ge(xn_ready, t + 1)
                pool.wait_ge(xpx_free, t + 1)
                pool.sem_inc(apart, 1)
                g.tensor_tensor(xpx[:, u, :], acc[:, bass.ds(t, 1), 0:D].rearrange("p a n -> p (a n)"), xn[:, u, :], ALU.add).then_inc(x_read, 1)
                pool.wait_ge(x_read, t + 1)
                g.tensor_tensor(xpx[:, u, :], xpx[:, u, :], rows[:, 2, :], ALU.add).then_inc(xpx_ready, 1)
                pool.wait_ge(xpx_ready, t + 1)
                pool.sem_inc(xn_free, 1)
                pool.dma_start(xpx_d[bass.ds(t * P, P), :], xpx[:, u, :]).then_inc(xpx_out[u], 16)

            def stored(t, q, u):
                pool.wait_ge(xpx_out[u], q * 16 + 16)
                pool.sem_inc(xpx_free, 1)
            pipeline(pool, 2, [(1, residual), (0, stored)])
            pool.wait_ge(pro_out, 64)

        @block.scalar
        def _(act):
            s = nc.scalar
            act.preload_act_table_set("natural_log_exp_and_others")
            act.sem_inc(xnT_free, 2)
            act.sem_inc(xn_free, 2)
            act.sem_inc(xpx_free, 2)

            def load(dstt, srca, sm=late_in):
                act.dma_start(dstt, srca).then_inc(sm, 16)
            load(wkv[:, :, 0:D], v["Wk"].rearrange("(k p) n -> p k n", p=128), kvw_in)
            load(wkv[:, :, D:], v["Wv"].rearrange("(k p) n -> p k n", p=128), kvw_in)
            for i, r in enumerate(("gnn_bias", "g2", "b2", "b_out")):
                load(rows[:, i, :], v[r].partition_broadcast(P), rows_in)
            load(wq[:], v["Wq"].rearrange("(k p) n -> p k n", p=128))
            load(wm[:], v["Wm"].rearrange("(k p) n -> p k n", p=128))
            load(w1[:], v["W1"].rearrange("(k p) n -> p k n", p=128))
            load(w2[:], v["W2"].rearrange("(k p) n -> p k n", p=128))
            with nc.allow_non_contiguous_dma(reason="a few columns"):
                load(vcols[:, 0, :], v["g1"].rearrange("(k p) -> p k", p=128))
                load(vcols[:, 1, :], v["b1"].rearrange("(k p) -> p k", p=128))
                load(bxc[:], v["b_x"].rearrange("(k p) -> p k", p=128))
            load(wx[:], v["W_x"].rearrange("(k p) n -> p k n", p=128))
            act.wait_ge(consts, 13)
            load(wsl[0:FD, 0:FD], v["W_slice"])
            load(wsl[FD:, FD:], v["W_slice"])
            load(bsl[:], v["b_slice"].rearrange("(a n) -> a n", a=1))
            load(itemp[:], v["temperature"].rearrange("a h b c -> (a h b c)").partition_broadcast(128))
            act.wait_ge(setup, 1)

            def deviations(t, q, u):
                act.wait_ge(var_ready, t + 1)
                s.activation(lnv[:, u, :], mv[:, u, 1:2], ACT.Ln, bias=zcol[0:P, 0:1]).then_inc(lnv_ready, 1)
                act.wait_ge(lnv_ready, t + 1)
                s.activation(rstd[:, u, :], lnv[:, u, :], ACT.Exp, scale=-0.5).then_inc(rstd_ready, 1)

            def transposed(t, q, u):
                act.wait_ge(xT_done, t + 1)
                act.wait_ge(xnT_free, t + 1)
                s.activation(xnT[:, u, :], psT[0][:, 0:KD * P], ACT.Copy).then_inc(xnT_ready, 1)

            def keys_values(t, q, u):
                act.wait_ge(k_done, t + 1)
                s.activation(kex[:], psH[1][0:P, 0:D], ACT.Exp)
                s.activation(krl[:], psH[1][0:P, 0:D], ACT.Relu).then_inc(kparts_ready, 1)
                s.activation(vst[:, u, :, 0:128], psH[1][0:P, D:].rearrange("p (m c) -> p m c", m=KD), ACT.Copy).then_inc(v_saved, 1)

            def projected(t, q, u):
                act.wait_ge(h_done, t + 1)
                act.wait_ge(x_read, t + 1)
                s.activation(acc[:, bass.ds(t, 1), :].rearrange("p a n -> p (a n)"), psH[0][0:P, 0:ROW], ACT.Copy).then_inc(h_saved, 1)
                s.activation(ad_all[:, bass.ds(t, 1), :].rearrange("p a n -> p (a n)"), psH[0][0:P, ROW:ROW + H], ACT.Copy).then_inc(ad_saved, 1)
            act.sem_inc(v_saved, 1)
            act.sem_inc(ad_saved, 1)
            pipeline(act, 2, [(2, deviations), (0, keys_values), (1, transposed), (0, projected)])

        @block.vector
        def _(dve):
            d = nc.vector
            link = linker(dve, dve_chain)
            dve.wait_ge(weights_in, 48)
            for i in range(2):
                for k in range(KD):
                    d.tensor_tensor(prod[:, i, k, :], wraw[:, k, :], att[:, i, :], ALU.mult)
            wgv = wg[:, :, 0:ROW].rearrange("p k (h c) -> p k h c", c=CW)
            for k in range(KD):
                last = d.tensor_copy(wgv[:, k, :, 0:C], wraw[:, k, :].rearrange("p (h c) -> p h c", c=C))
            link(last)
            for k in range(KD):
                d.tensor_reduce(wgv[:, k, :, C], prod[:, 0, k, :].rearrange("p (h c) -> p h c", c=C), axis=X, op=ALU.add)
                last = d.tensor_reduce(wg[:, k, ROW:], prod[:, 1, k, :].rearrange("p (h c) -> p h c", c=C), axis=X, op=ALU.add)
            last.then_inc(wg_ready, 1)
            d.memset(zeros[:], 0.0)
            d.memset(kvd[:], 0.0)
            d.memset(ksd[:], 0.0)
            d.memset(vst[:, :, :, 128], 1.0).then_inc(setup, 1)
            dve.wait_ge(x_in, 16)
            dve.wait_ge(dstf_ready, 1)
            dve.wait_ge(consts, 13)

            def count(w):
                d.tensor_scalar(junk[:], dst_f[:, 1:], thr[:, bass.ds(w, 1)], 0.0, ALU.is_lt, ALU.add,
                                accum_out=cnt[:, bass.ds(w, 1)]).then_inc(cnt_ready, 1)

            def stats(t, q, u):
                d.bn_stats(st6[:, u, :], acc[:, bass.ds(t, 1), 0:D].rearrange("p a n -> p (a n)")).then_inc(st_ready, 1)
                dve.wait_ge(st_ready, t + 1)
                dve.sem_inc(apart, 1)
                d.bn_aggr(mv[:, u, :], st6[:, u, :]).then_inc(var_ready, 1)

            def normed(t, q, u):
                dve.wait_ge(rstd_ready, t + 1)
                d.scalar_tensor_tensor(nb[:, u, :], mv[:, u, 0:1], -1.0, rstd[:, u, :], ALU.mult, ALU.mult).then_inc(nb_ready, 1)
                dve.wait_ge(nb_ready, t + 1)
                dve.wait_ge(xn_free, t + 1)
                d.tensor_scalar(xn[:, u, :], acc[:, bass.ds(t, 1), 0:D].rearrange("p a n -> p (a n)"), rstd[:, u, :], nb[:, u, :],
                                ALU.mult, ALU.add).then_inc(xn_ready, 1)

            def keys(t, q, u):
                dve.wait_ge(kparts_ready, t + 1)
                d.scalar_tensor_tensor(kk[:, u, :], kex[:], 1.0, krl[:], ALU.min, ALU.add).then_inc(kk_ready, 1)

            def counted(t, q, u):
                dve.wait_ge(cnt_ready, t + 1)
                count(t)
            d.memset(junk[:], 0.0).then_inc(cnt_ready, 1)
            pipeline(dve, 2, [(1, normed), (2, stats), (0, keys), (0, counted)])
            dve.wait_ge(cnt_ready, NT + 1)
            count(NT)
            dve.wait_ge(cnt_ready, NT + 2)
            link(d.memset(cdiff[:, NT:], 0.0))
            d.tensor_tensor(cdiff[:, 0:NT], cnt[:, 1:], cnt[:, 0:NT], ALU.subtract).then_inc(dve_s, 1)
            dve.wait_ge(pe_s, 1)
            link(d.tensor_copy(cols[:, 0:2], psS[0:W1C, 0:2]))
            d.tensor_scalar(kjunk[:], iota_k[:], cols[:, 1:2], 0.0, ALU.is_lt, ALU.add, accum_out=cols[:, 2:3]).then_inc(dve_s, 1)
            dve.wait_ge(dve_s, 2)
            dve.wait_ge(pe_s, 2)
            link(d.tensor_copy(cols[:, 3:4], psS[0:W1C, 2:3]))
            link(d.scalar_tensor_tensor(cols[:, 4:5], cols[:, 3:4], cols[:, 2:3], big50[:], ALU.add, ALU.add))
            d.tensor_scalar(ind[:], iota_g[:], cols[:, 3:4], None, ALU.is_ge)
            link(d.tensor_scalar(ind2[:], iota_g[:], cols[:, 4:5], None, ALU.is_ge))
            link(d.scalar_tensor_tensor(cols[:, 5:6], cols[:, 3:4], float(-GE), cols[:, 0:1], ALU.mult, ALU.add))
            link(d.tensor_tensor(ind[:], ind[:], ind2[:], ALU.subtract))
            dve.sem_inc(dve_s, 1)
            dve.wait_ge(pe_s, 3)
            link(d.scalar_tensor_tensor(sch_f[:, 0, :], iota_g[0:1, :], float(GE), psS[0:1, 0:NG], ALU.mult, ALU.add))
            link(d.tensor_scalar(sch_f[:, 1, :], sch_f[:, 0, :], float(E), None, ALU.min))
            d.tensor_copy(sched[:, 0, B:], sch_f[:, 1, :])
            dve.wait_ge(pe_s, 4)
            link(d.tensor_copy(sched[:, 1, B:], psR[0:1, 0:NG]))
            link(d.memset(sched[:, :, 0:B], NT))
            dve.wait_ge(pe_s, 5)
            link(d.tensor_copy(wbase[:], psT[1][:, 0:NG]))
            dve.wait_ge(ad_saved, NT + 1)
            dve.wait_ge(h_saved, NT)
            accv = acc[:].rearrange("p w (h c) -> p w h c", c=CW)
            link(d.tensor_tensor(m_run[:, 0:NT, :], accv[:, 0:NT, :, C], ad_all[:, 0:NT, :], ALU.add))
            link(d.scalar_tensor_tensor(m_run[:, 0:NT, :], m_run[:, 0:NT, :], SLOPE, m_run[:, 0:NT, :], ALU.mult, ALU.max))
            dve.wait_ge(tab_out, 16 * NT)
            link(d.memset(accv[:, 0:NT, :, C], 1.0))
            rest = ad_all[:, 0:NT, :]
            link(d.memset(ad3[:, NT, :, :], 0.0))
            for i in range(3):
                link(d.tensor_copy(ad3[:, 0:NT, i, :], rest))
                if i < 2:
                    link(d.tensor_tensor(adr[:], rest, ad3[:, 0:NT, i, :], ALU.subtract))
                    rest = adr[:]
            dve.wait_ge(kv_closed, 1)
            link(d.tensor_copy(kvs[:], psM[:, 0:KD * 129].rearrange("p (m c) -> p m c", m=KD)))
            for m in range(KD):
                for i in range(4):
                    q = slice(32 * i, 32 * i + 32)
                    d.tensor_scalar(kvd[q, m, q], kvs[q, m, q], 1.0 / N, None, ALU.mult)
                    d.tensor_scalar(ksd[q, m, q], ones[q, 0:32], kvs[q, m, 128:129], None, ALU.mult)
            dve.wait_ge(late_in, 16 * 12)
            link(d.tensor_scalar(itemp[:], itemp[:], 0.1, 5.0, ALU.max, ALU.min))
            link(d.reciprocal(itemp[:], itemp[:]))
            dve.wait_ge(pe_w, 1)
            link(d.tensor_copy(bias1[:], psW[:, 0:4]))
            for k in range(KD):
                d.tensor_scalar(w1[:, KD + k, :], w1[:, KD + k, :], vcols[:, 0, k:k + 1], None, ALU.mult)
            for k in range(KD):
                dve.wait_ge(pe_w, 2 + 2 * k)
                link(d.tensor_copy(wxT[:, :, k * 128:(k + 1) * 128], psT[k][:, :].rearrange("p (j n) -> p j n", j=4)))
                dve.sem_inc(dve_w, 1)
                dve.wait_ge(pe_w, 3 + 2 * k)
                d.tensor_tensor(wc[:, k, :].rearrange("p (h g) -> p h g", g=FD), psH[k][:, :].rearrange("p (h g) -> p h g", g=FD),
                                itemp[:, :].unsqueeze(2).broadcast_to([128, FH, FD]), ALU.mult)
            dve.wait_ge(pe_w, 6)
            bv = brow[:].rearrange("p (h g) -> p h g", g=FD)
            link(d.tensor_tensor(bv, psW[0:1, :].rearrange("p (h g) -> p h g", g=FD),
                                 bsl[:].unsqueeze(1).broadcast_to([1, FH, FD]), ALU.add))
            link(d.tensor_tensor(bv, bv, itemp[0:1, :].unsqueeze(2).broadcast_to([1, FH, FD]), ALU.mult))
            dve.sem_inc(dve_w, 1)
            dve.wait_ge(pe_w, 7)
            link(d.tensor_copy(bc[:], psW[0:P, :]))

        @block.tensor
        def _(pe):
            t = nc.tensor
            pe.wait_ge(consts, 13)
            pe.wait_ge(wg_ready, 1)
            pe.wait_ge(kvw_in, 32)
            pe.wait_ge(setup, 1)
            t.matmul(psM[:, 0:KD * 129], zeros[:, 0:128], zeros[:], start=True, stop=False)

            def turned(n, q, u):
                pe.wait_ge(xn_ready, n + 1)
                for k in range(KD):
                    last = t.transpose(psT[0][:, k * P:(k + 1) * P], xn[:, u, k * 128:(k + 1) * 128], ident[0:P, 0:P])
                last.then_inc(xT_done, 1)

            def products(n, q, u):
                pe.wait_ge(xnT_ready, n + 1)
                pe.wait_ge(v_saved, n + 1)
                for k in range(KD):
                    last = t.matmul(psH[1][0:P, :], xnT[:, u, k * P:(k + 1) * P], wkv[:, k, :], start=(k == 0), stop=(k == KD - 1))
                last.then_inc(k_done, 1)
                pe.wait_ge(ad_saved, n + 1)
                for k in range(KD):
                    last = t.matmul(psH[0][0:P, 0:ROW + H], xnT[:, u, k * P:(k + 1) * P], wg[:, k, :], start=(k == 0), stop=(k == KD - 1))
                last.then_inc(h_done, 1)

            def sums(n, q, u):
                pe.wait_ge(kk_ready, n + 1)
                pe.wait_ge(v_saved, n + 2)
                for m in range(KD):
                    t.matmul(psM[:, m * 129:(m + 1) * 129], kk[:, u, m * 128:(m + 1) * 128], vst[:, u, m, :], start=False, stop=False)
            pipeline(pe, 2, [(0, products), (1, turned), (0, sums)])
            t.matmul(psM[:, 0:KD * 129], zeros[:, 0:128], zeros[:], start=False, stop=True).then_inc(kv_closed, 1)
            pe.wait_ge(late_in, 16 * 12)
            for m in range(4):
                for k in range(KD):
                    last = t.matmul(psW[:, m:m + 1], w1[:, KD + k, m * 128:(m + 1) * 128], vcols[:, 1, k:k + 1], start=(k == 0), stop=(k == KD - 1))
            last.then_inc(pe_w, 1)
            pe.wait_ge(dve_s, 1)
            t.matmul(psS[0:W1C, 0:1], cnt[:], ones[0:P, 0:1], start=True, stop=True)
            t.matmul(psS[0:W1C, 1:2], cdiff[:], ones[0:P, 0:1], start=True, stop=True).then_inc(pe_s, 1)
            pe.wait_ge(dve_s, 2)
            t.matmul(psS[0:W1C, 2:3], below[:], cols[:, 2:3], start=True, stop=True).then_inc(pe_s, 1)
            pe.wait_ge(dve_s, 3)
            t.matmul(psS[0:1, 0:NG], cols[:, 5:6], ind[:], start=True, stop=True).then_inc(pe_s, 1)
            t.matmul(psR[0:1, 0:NG], wcol[:], ind[:], start=True, stop=True).then_inc(pe_s, 1)
            t.matmul(psT[1][:, 0:NG], wrep[:], ind[:], start=True, stop=True).then_inc(pe_s, 1)
            pe.wait_ge(h_saved, NT)
            pe.wait_ge(ad_saved, NT + 1)
            for k in range(KD):
                for j in range(4):
                    last = t.transpose(psT[k][:, j * 128:(j + 1) * 128], wx[:, k, j * 128:(j + 1) * 128], ident[:])
                last.then_inc(pe_w, 1)
                pe.wait_ge(dve_w, k + 1)
                for j in range(4):
                    last = t.matmul(psH[k][:, j * 128:(j + 1) * 128], wxT[:, j, k * 128:(k + 1) * 128], wsl[:], start=True, stop=True)
                last.then_inc(pe_w, 1)
            for j in range(4):
                last = t.matmul(psW[0:1, j * 128:(j + 1) * 128], bxc[:, j:j + 1], wsl[:], start=True, stop=True)
            last.then_inc(pe_w, 1)
            pe.wait_ge(dve_w, 3)
            t.matmul(psW[0:P, :], ones[0:1, 0:P], brow[:], start=True, stop=True).then_inc(pe_w, 1)


def edges_and_mix(nc, sb, ps, sem, linker, v):
    ident, iota_d, wbase, sched = v["ident"], v["iota_d"], v["wbase"], v["sched"]
    acc, ad3, m_run, kvd, ksd = v["acc"], v["ad3"], v["m_run"], v["kvd"], v["ksd"]
    h_tab, rec, pen, xnT_d, xpx_d, mix_d = v["h_tab"], v["rec"], v["pen"], v["xnT_d"], v["xpx_d"], v["mix_d"]
    wq, wm, w1, w2, rows, bias1 = (v[k] for k in "wq wm w1 w2 rows bias1".split())
    BT = B * T
    HB = H * B
    AW = 3 * H
    GD = 3
    with ExitStack() as ctx:
        ring = [sb(ctx, f"ring{i}", [128, BT, MW]) for i in range(2)]
        recs = [sb(ctx, f"recb{i}", [128, B, T * 4], I32) for i in range(2)]
        pens = [sb(ctx, f"penb{i}", [HB, GE + 1]) for i in range(2)]
        oh = [sb(ctx, f"oh{i}", [128, BT, P]) for i in range(2)]
        ohT = [sb(ctx, f"ohT{i}", [P, GE], BF16) for i in range(2)]
        adst = sb(ctx, "adst", [P, B, AW], BF16)
        dloc = sb(ctx, "dloc", [128, B, T])
        first = sb(ctx, "first", [128, B, T])
        asc = sb(ctx, "asc", [128, T, B * H])
        scf = sb(ctx, "scf", [HB, GE])
        scb = sb(ctx, "scb", [HB, GE])
        ad_e = sb(ctx, "ad_e", [128, BT, H])
        zz = sb(ctx, "zz", [128, 2, BT, H])
        df = sb(ctx, "df", [128, BT, H])
        part = [sb(ctx, f"part{i}", [P, B, MW]) for i in range(2)]
        pm = sb(ctx, "pm", [P, B, 1])
        sg = sb(ctx, "sg", [P, B, H])
        mns = sb(ctx, "mns", [P, B, H])
        dd = [sb(ctx, f"dd{i}", [P, 2, B, H]) for i in range(2)]
        ww = [sb(ctx, f"ww{i}", [P, 2, B, H]) for i in range(2)]
        xm = [sb(ctx, f"xm{i}", [128, KD * P]) for i in range(2)]
        xr = [sb(ctx, f"xr{i}", [P, D]) for i in range(2)]
        mo = [sb(ctx, f"mo{i}", [P, D]) for i in range(2)]
        qex = sb(ctx, "qex", [128, KD * P])
        qrl = sb(ctx, "qrl", [128, KD * P])
        qq = sb(ctx, "qq", [128, KD * P])
        den = sb(ctx, "den", [128, KD * P])
        msgT = sb(ctx, "msgT", [128, KD * P])
        st6 = sb(ctx, "st6b", [P, 2, 6])
        mv = sb(ctx, "mvb", [P, 2, 2])
        lnv = sb(ctx, "lnvb", [P, 2, 1])
        rstd = sb(ctx, "rstdb", [P, 2, 1])
        nb = sb(ctx, "nbb", [P, 2, 1])
        n1 = sb(ctx, "n1", [P, D])
        n1T = sb(ctx, "n1T", [128, KD * P])
        hT = sb(ctx, "hT", [128, 4, P])
        n2 = sb(ctx, "n2", [P, D])
        n2s = sb(ctx, "n2s", [P, D])
        nm = sb(ctx, "nm", [P, 2, 1])
        fix = sb(ctx, "fix", [128, KD * P])
        lden = sb(ctx, "lden", [128, KD * P])
        epsc = sb(ctx, "epsc", [128, 4])
        apart_d = sb(ctx, "apart_d", [128, T, P])
        hrow = sb(ctx, "hrow", [P, INNER])
        psT = ps(ctx, "pB_T")
        psE = ps(ctx, "pB_E")
        psO = [ps(ctx, f"pB_O{i}") for i in range(2)]
        psP = [ps(ctx, f"pB_P{i}") for i in range(2)]
        M0 = ps(ctx, "pB_M0")
        M1 = ps(ctx, "pB_M1")

        names = """asc_ready main_done asT_done ad_summed scans_done sT_done zz_ready al_ready flags_ready eprep_done ex_done
            msg_ready part_saved dloc_ready oh_ready oh_apart ohs_ready w1_saved h_turned ad_staged ohT_done ohT_saved adE_done dd_ready ww_ready pm_ready sg_ready
            m_steps a_steps p_scaled consts
            q_done qparts_ready qq_ready nd_done den_ready rden_ready fix_ready msgT_ready wm_done st_ready var_ready norm_steps
            n1_ready n1_turned n1T_ready w1_done hT_ready w2_done n2_ready n2_scaled mo_ready mo_free""".split()
        S = {n: sem(ctx, "e_" + n) for n in names}
        rec_in = [sem(ctx, f"rec_in{i}") for i in range(2)]
        pen_in = [sem(ctx, f"pen_in{i}") for i in range(2)]
        gathered = [sem(ctx, f"gathered{i}") for i in range(2)]
        xm_in = [sem(ctx, f"xm_in{i}") for i in range(2)]
        xr_in = [sem(ctx, f"xr_in{i}") for i in range(2)]
        mo_out = sem(ctx, "mo_out")
        block = ctx.enter_context(nc.Block())

        def steps(eng, body):
            with eng.Fori(0, NT // 2) as it:
                for i in range(4):
                    body(it * 4 + i, it * 2 + i // 2, i % 2, it * 2 + i // 2, it, i // 2, False)
            with eng.Fori(0, NB // 2 - NT - 1) as it:
                for u in range(2):
                    body(it * 2 + u + 2 * NT, it + NT, u, None, None, None, False)
            for u in range(2):
                body(NB - 2 + u, NB // 2 - 1, u, None, None, None, u == 1)

        def ringv(u):
            return ring[u][:, :, 0:ROW].rearrange("p t (h c) -> p t h c", c=CW)

        @block.sync
        def _(sp):
            def edge_loads(b, u):
                for g in range(B):
                    e0 = sp.value_load(sched[0:1, 0, bass.ds(b * B + (B + g), 1)], min_val=0, max_val=E)
                    sp.dma_start(recs[u][:, g, :], rec[bass.ds(e0, GE), :].rearrange("(p t) f -> p (t f)", t=T)).then_inc(rec_in[u], 16)
                    sp.dma_start(pens[u][g * H:(g + 1) * H, :], pen[bass.ds(e0, GE + 1)].partition_broadcast(H)).then_inc(pen_in[u], 16)

            for u in range(2):
                edge_loads(u, u)
                sp.dma_start(xm[u][:], xnT_d[u, :, :]).then_inc(xm_in[u], 16)

            def step(b, k, u, n, nk, j, last):
                if not (isinstance(b, int)):
                    sp.wait_ge(S["eprep_done"], b + 1)
                    edge_loads(b + 2, u)
                if n is not None and u == 0:
                    sp.dma_start(xr[j][:], xpx_d[bass.ds(n * P, P), :]).then_inc(xr_in[j], 16)
                if n is not None and u == 1:
                    sp.wait_ge(S["w1_done"], n + 1)
                    sp.dma_start(xm[j][:], xnT_d[bass.ds(n + 2, 1), :, :].rearrange("a p n -> (a p) n")).then_inc(xm_in[j], 16)
                    sp.wait_ge(S["mo_ready"], n + 1)
                    sp.dma_start(mix_d[bass.ds(n * P, P), :], mo[j][:]).then_inc(mo_out, 16)
                    sp.wait_ge(mo_out, n * 16 + 16)
                    sp.sem_inc(S["mo_free"], 1)
            steps(sp, step)
            for u in range(2):
                sp.wait_ge(xm_in[u], 16 * (NT // 2 + 1))
            sp.wait_ge(mo_out, 16 * NT)

        @block.gpsimd
        def _(pool):
            def gather(b, k, u, between=None):
                pool.wait_ge(rec_in[u], k * (16 * B) + 16 * B)
                for g in range(B):
                    if g == B // 2 and between:
                        between()
                    pool.wait_ge(S["main_done"], b * B + g + 1)
                    pool.sem_inc(v["apart"], 1)
                    for t in range(T):
                        pool.indirect_dma_start(out=ring[u][:, g * T + t, 0:ROW], out_offset=None, in_=h_tab[:, :],
                                                in_offset=bass.IndirectOffsetOnAxis(ap=recs[u][:, g, t * 4:t * 4 + 1], axis=0)
                                                ).then_inc(gathered[u], 16)

            def step(b, k, u, n, nk, j, last):
                def mixed():
                    pool.wait_ge(S["n2_ready"], n + 1)
                    nc.gpsimd.tensor_tensor(n2s[:], n2[:], rows[:, 1, :], ALU.mult).then_inc(S["n2_scaled"], 1)
                    pool.wait_ge(S["n2_scaled"], n + 2)
                    pool.wait_ge(S["mo_free"], n + 1)
                    pool.wait_ge(xr_in[j], nk * 16 + 16)
                    nc.gpsimd.tensor_tensor(mo[j][:], n2s[:], xr[j][:], ALU.add).then_inc(S["mo_ready"], 1)
                if not isinstance(b, int):
                    gather(b + 2, k + 1, u, mixed if n is not None and u == 1 else None)
            for u in range(2):
                gather(u, 0, u)
            steps(pool, step)

        @block.tensor
        def _(pe):
            t_ = nc.tensor

            def onehots_T(b, u):
                def tr(g):
                    if g < GD:
                        pe.wait_ge(S["oh_ready"], b * GD + g + 1)
                    else:
                        pe.wait_ge(S["ohs_ready"], b * (B - GD) + (g - GD + 2))
                    pe.wait_ge(S["ohT_saved"], b * B + g + 1)
                    for t in range(T):
                        last = t_.transpose(psO[g % 2][0:P, t * 128:(t + 1) * 128], oh[u][:, g * T + t, :], ident[:])
                    last.then_inc(S["ohT_done"], 1)

                def mm(g):
                    pe.wait_ge(S["ohT_saved"], b * B + g + 3)
                    if g == 0:
                        pe.wait_ge(S["ad_staged"], b + 1)
                    for t in range(T):
                        i = g * T + t
                        last = t_.matmul(psE[:, i * AW:(i + 1) * AW], ohT[g % 2][:, t * 128:(t + 1) * 128], adst[:, g, :], start=True, stop=True)
                    if g == B - 1:
                        last.then_inc(S["adE_done"], 1)

                def first_half():
                    tr(0)
                    tr(1)

                def second_half():
                    if not (isinstance(b, int) and b == 0):
                        pe.wait_ge(S["zz_ready"], b)
                    mm(0)
                    tr(2)
                    mm(1)
                    tr(3)
                    mm(2)
                    mm(3)
                return first_half, second_half

            def logits_T(b):
                pe.wait_ge(S["asc_ready"], b + 1)
                for t in range(T):
                    la = t_.transpose(psT[0:HB, t:GE:T], asc[:, t, :], ident[:])
                la.then_inc(S["asT_done"], 1)

            def main(b, u, g):
                pe.wait_ge(S["msg_ready"], b * B + g + 1)
                pe.wait_ge(S["part_saved"], b * B + g + 1)
                for t in range(T):
                    last = t_.matmul(psP[g % 2][0:P, 0:MW], oh[u][:, g * T + t, :], ring[u][:, g * T + t, :], start=(t == 0), stop=(t == T - 1))
                last.then_inc(S["main_done"], 1)

            pe.sem_inc(S["main_done"], 2 * B)
            for half in onehots_T(0, 0):
                half()
            logits_T(0)

            def step(b, k, u, n, nk, j, last):
                if n is not None and u == 0:
                    pe.wait_ge(xm_in[j], nk * 16 + 16)
                    for m in range(KD):
                        for c in range(KD):
                            la = t_.matmul(M0[:, m * P:(m + 1) * P], wq[:, c, m * 128:(m + 1) * 128], xm[j][:, c * P:(c + 1) * P], start=(c == 0), stop=(c == KD - 1))
                    la.then_inc(S["q_done"], 1)
                elif n is not None:
                    pe.wait_ge(S["n1_ready"], n + 1)
                    for m in range(KD):
                        la = t_.transpose(M1[:, m * P:(m + 1) * P], n1[:, m * 128:(m + 1) * 128], ident[0:P, 0:P])
                    la.then_inc(S["n1_turned"], 1)
                    for c in range(KD):
                        t_.matmul(M0[0:P, :], xm[j][:, c * P:(c + 1) * P], w1[:, c, :], start=(c == 0), stop=False)
                pe.wait_ge(S["scans_done"], b * 2 + 2)
                pe.sem_inc(v["apart"], 1)
                for t in range(T):
                    la = t_.transpose(psE[:, 384 + t * HB:384 + (t + 1) * HB], scb[:, t:GE:T], ident[0:HB, 0:HB])
                la.then_inc(S["sT_done"], 1)
                if not last:
                    first_half, second_half = onehots_T(b + 1, 1 - u)
                    first_half()
                if n is not None and u == 0:
                    pe.wait_ge(S["qq_ready"], n + 1)
                    for i, w in enumerate((kvd, ksd)):
                        for m in range(KD):
                            o = (i * KD + m) * P
                            la = t_.matmul(M1[:, o:o + P], w[:, m, :], qq[:, m * P:(m + 1) * P], start=True, stop=True)
                    la.then_inc(S["nd_done"], 1)
                elif n is not None:
                    pe.wait_ge(S["n1T_ready"], n + 1)
                    for c in range(KD):
                        la = t_.matmul(M0[0:P, :], n1T[:, c * P:(c + 1) * P], w1[:, KD + c, :], start=False, stop=(c == KD - 1))
                    la.then_inc(S["w1_done"], 1)
                if not last:
                    second_half()
                main(b, u, 0)
                if n is not None and u == 1:
                    pe.wait_ge(S["w1_saved"], n + 1)
                    for m in range(4):
                        la = t_.transpose(M0[:, m * P:(m + 1) * P], hrow[:, m * 128:(m + 1) * 128], ident[0:P, 0:P])
                    la.then_inc(S["h_turned"], 1)
                main(b, u, 1)
                if n is None or u == 0:
                    main(b, u, 2)
                if n is not None and u == 0:
                    pe.wait_ge(S["msgT_ready"], n + 1)
                    for m in range(KD):
                        la = t_.matmul(M0[0:P, 0:D], msgT[:, m * P:(m + 1) * P], wm[:, m, :], start=(m == 0), stop=(m == KD - 1))
                    la.then_inc(S["wm_done"], 1)
                if n is not None and u == 1:
                    pe.wait_ge(S["hT_ready"], n + 1)
                    for m in range(4):
                        la = t_.matmul(M1[0:P, 0:D], hT[:, m, :], w2[:, m, :], start=(m == 0), stop=(m == 3))
                    la.then_inc(S["w2_done"], 1)
                    main(b, u, 2)
                if not last:
                    logits_T(b + 1)
                main(b, u, 3)
            steps(pe, step)

        @block.scalar
        def _(act):
            s = nc.scalar
            act.preload_act_table_set("natural_log_exp_and_others")
            act.sem_inc(S["ohT_saved"], 2)
            act.sem_inc(S["part_saved"], 2)
            act.sem_inc(S["ohs_ready"], 1)
            act.sem_inc(S["n2_scaled"], 1)
            act.sem_inc(S["mo_free"], 2)
            act.wait_ge(S["consts"], 1)

            def windows(b):
                return nc.values_load_multi_w_load_instructions(sched[0:1, 1, bass.ds(b * B + B, B)], engines=(act.engine,), min_val=0, max_val=NT)[1]

            def stage_logits(b):
                w = windows(b)
                if not (isinstance(b, int) and b == 0):
                    act.wait_ge(S["adE_done"], b)
                for g in range(B):
                    la = s.activation(adst[:, g, :], ad3[:, bass.ds(w[g], 1), :, :].rearrange("p a c h -> p (a c h)"), ACT.Copy)
                la.then_inc(S["ad_staged"], 1)

            def onehots_T(b, groups):
                for g in groups:
                    act.wait_ge(S["ohT_done"], b * B + g + 1)
                    s.activation(ohT[g % 2][:], psO[g % 2][0:P, :], ACT.Copy).then_inc(S["ohT_saved"], 1)

            def onehots(b, u, g):
                act.wait_ge(S["dloc_ready"], b + 1)
                act.wait_ge(S["ohs_ready"], b * (B - GD) + (g - GD + 1))
                for t in range(T):
                    la = s.activation(apart_d[:, t, :], iota_d[:], ACT.Abs, scale=-1.0, bias=dloc[:, g, t:t + 1])
                la.then_inc(S["oh_apart"], 1)
                act.wait_ge(S["oh_apart"], b * (B - GD) + (g - GD + 1))
                s.activation(oh[u][:, g * T:(g + 1) * T, :], apart_d[:], ACT.Relu, scale=-1.0, bias=epsc[:, 3:4]).then_inc(S["ohs_ready"], 1)
            stage_logits(0)
            for g in range(GD, B):
                onehots(0, 0, g)
            onehots_T(0, range(B))

            def save(b, u, g):
                act.wait_ge(S["main_done"], b * B + (2 * B + g + 1))
                s.activation(part[u][:, g, :], psP[g % 2][0:P, 0:MW], ACT.Copy).then_inc(S["part_saved"], 1)

            def normalised(i, x, y, src):
                act.wait_ge(S["var_ready"], x + 1)
                s.activation(lnv[:, i, :], mv[:, i, 1:2], ACT.Ln, bias=epsc[0:P, 0:1]).then_inc(S["norm_steps"], 1)
                s.activation(nm[:, i, :], mv[:, i, 0:1], ACT.Copy, scale=-1.0)
                act.wait_ge(S["norm_steps"], x * 3 + 1)
                s.activation(rstd[:, i, :], lnv[:, i, :], ACT.Exp, scale=-0.5).then_inc(S["norm_steps"], 1)
                act.wait_ge(S["norm_steps"], x * 3 + 2)
                s.activation(nb[:, i, :], nm[:, i, :], ACT.Identity, scale=rstd[:, i, :], bias=epsc[0:P, 2:3]).then_inc(S["norm_steps"], 1)
                act.wait_ge(S["norm_steps"], x * 3 + 3)
                return s.activation(y[:], src, ACT.Identity, scale=rstd[:, i, :], bias=nb[:, i, :])

            def source_logits(k, u):
                act.wait_ge(gathered[u], k * (16 * BT) + 16 * BT)
                s.activation(asc[:].rearrange("p t (g h) -> p g t h", h=H), ringv(u)[:, :, :, C].rearrange("p (g t) h -> p g t h", t=T),
                             ACT.Copy).then_inc(S["asc_ready"], 1)
            source_logits(0, 0)

            def step(b, k, u, n, nk, j, last):
                if n is not None and u == 0:
                    act.wait_ge(S["q_done"], n + 1)
                    s.activation(qex[:], M0[:, 0:KD * P], ACT.Exp)
                    s.activation(qrl[:], M0[:, 0:KD * P], ACT.Relu).then_inc(S["qparts_ready"], 1)
                elif n is not None:
                    act.wait_ge(S["n1_turned"], n + 1)
                    s.activation(n1T[:], M1[:, 0:KD * P], ACT.Copy).then_inc(S["n1T_ready"], 1)
                if not last:
                    for g in range(GD, B):
                        onehots(b + 1, 1 - u, g)
                    stage_logits(b + 1)
                    onehots_T(b + 1, range(2))
                act.wait_ge(S["eprep_done"], b + 1)
                s.activation(ringv(u)[:, :, :, C], df[:], ACT.Exp).then_inc(S["ex_done"], 1)
                if not last:
                    onehots_T(b + 1, range(2, B))
                if n is not None and u == 0:
                    act.wait_ge(S["nd_done"], n + 1)
                    s.activation(lden[:], M1[:, KD * P:2 * KD * P], ACT.Ln, bias=epsc[:, 1:2]).then_inc(S["den_ready"], 1)
                    act.wait_ge(S["den_ready"], n + 1)
                    s.activation(den[:], lden[:], ACT.Exp, scale=-1.0).then_inc(S["rden_ready"], 1)
                    save(b, u, 0)
                elif n is not None:
                    act.wait_ge(S["w1_done"], n + 1)
                    s.activation(hrow[:], M0[0:P, :], ACT.Copy).then_inc(S["w1_saved"], 1)
                    save(b, u, 0)
                    act.wait_ge(S["h_turned"], n + 1)
                    for m in range(4):
                        la = s.activation(hT[:, m, :], M0[:, m * P:(m + 1) * P], ACT.Relu, bias=bias1[:, m:m + 1])
                    la.then_inc(S["hT_ready"], 1)
                rescale(b, 1 - u)
                if n is not None:
                    save(b, u, 1)
                if n is None:
                    save(b, u, 0)
                    save(b, u, 1)
                save(b, u, 2)
                if not last:
                    source_logits(k + u, 1 - u)
                if n is not None and u == 1:
                    act.wait_ge(S["w2_done"], n + 1)
                    act.wait_ge(S["n2_scaled"], n + 1)
                    normalised(1, n * 2 + 1, n2, M1[0:P, 0:D]).then_inc(S["n2_ready"], 1)
                save(b, u, 3)
                if n is not None and u == 0:
                    act.wait_ge(S["wm_done"], n + 1)
                    normalised(0, n * 2, n1, M0[0:P, 0:D]).then_inc(S["n1_ready"], 1)

            def rescale(b, u):
                act.wait_ge(S["dd_ready"], b + 1)
                s.activation(ww[u][:], dd[u][:], ACT.Exp).then_inc(S["ww_ready"], 1)
            steps(act, step)
            rescale(NB, 1)

        @block.vector
        def _(dve):
            d = nc.vector

            def places(b, u):
                dst = recs[u][:].bitcast(F32).rearrange("p g (t f) -> p g t f", f=4)[:, :, :, 1]
                d.tensor_tensor(dloc[:], dst, wbase[:, bass.ds(b * B, B)].unsqueeze(2).broadcast_to([128, B, T]), ALU.subtract).then_inc(S["dloc_ready"], 1)

            def onehots(b, u):
                dve.wait_ge(S["dloc_ready"], b + 1)
                for g in range(GD):
                    d.tensor_tensor(oh[u][:, g * T:(g + 1) * T, :], iota_d[:].unsqueeze(1).broadcast_to([128, T, P]),
                                    dloc[:, g, :].unsqueeze(2).broadcast_to([128, T, P]), ALU.is_equal).then_inc(S["oh_ready"], 1)

            def windows(b):
                return nc.values_load_multi_w_load_instructions(sched[0:1, 1, bass.ds(b * B, B)], engines=(dve.engine,), min_val=0, max_val=NT)[1]

            d.memset(epsc[:, 0:1], LN_EPS)
            d.memset(epsc[:, 1:2], MIX_EPS)
            d.memset(epsc[:, 2:3], 0.0)
            d.memset(epsc[:, 3:4], 1.0)
            d.memset(first[:], 0.0).then_inc(S["consts"], 1)
            dve.wait_ge(S["consts"], 1)
            d.memset(first[0:1, :, 0], 1.0).then_inc(S["consts"], 1)
            dve.wait_ge(rec_in[0], 16 * B)
            places(0, 0)
            onehots(0, 0)

            def accv(w):
                return acc[:, bass.ds(w, 1), :].rearrange("p a (h c) -> p (a h) c", c=CW)

            def statistics(i, x, src):
                d.bn_stats(st6[:, i, :], src).then_inc(S["st_ready"], 1)
                dve.wait_ge(S["st_ready"], x + 1)
                dve.sem_inc(v["apart"], 1)
                d.bn_aggr(mv[:, i, :], st6[:, i, :]).then_inc(S["var_ready"], 1)

            def presence(b, u):
                dve.wait_ge(S["part_saved"], b * B + 2)
                d.tensor_scalar(pm[:], part[u][:, :, MW - 1:MW], 1.0, BIG, ALU.subtract, ALU.mult).then_inc(S["pm_ready"], 1)

            def present_maxima(b, u):
                dve.wait_ge(S["pm_ready"], b + 1)
                d.tensor_tensor(sg[:], part[u][:, :, ROW:ROW + H], pm[:].broadcast_to([P, B, H]), ALU.add).then_inc(S["sg_ready"], 1)

            def running(w, g):
                return m_run[:, bass.ds(w[g], 1), :].rearrange("p a h -> p (a h)")

            def new_maximum(b, w, g):
                if g == 0:
                    dve.wait_ge(S["sg_ready"], b + 1)
                else:
                    dve.wait_ge(S["m_steps"], b * (3 * B) + 3 * g)
                d.tensor_tensor(mns[:, g, :], running(w, g), sg[:, g, :], ALU.max).then_inc(S["m_steps"], 1)

            def old_under_new(b, w, g, u):
                dve.wait_ge(S["m_steps"], b * (3 * B) + (3 * g + 1))
                d.tensor_tensor(dd[u][:, 0, g, :], running(w, g), mns[:, g, :], ALU.subtract).then_inc(S["m_steps"], 1)

            def kept_maximum(b, w, g):
                dve.wait_ge(S["m_steps"], b * (3 * B) + (3 * g + 2))
                d.tensor_tensor(running(w, g), running(w, g), sg[:, g, :], ALU.max).then_inc(S["m_steps"], 1)

            def batch_under_new(u):
                d.tensor_tensor(dd[u][:, 1], sg[:], mns[:], ALU.subtract).then_inc(S["dd_ready"], 1)

            def scaled_part(u, g):
                v = part[u][:, g, 0:ROW].rearrange("p (h c) -> p h c", c=CW)
                d.tensor_tensor(v, v, ww[u][:, 1, g, :].unsqueeze(2).broadcast_to([P, H, CW]), ALU.mult).then_inc(S["p_scaled"], 1)

            def scaled_sum(b, u, w, g):
                if g > 0:
                    dve.wait_ge(S["a_steps"], b * (2 * B) + 2 * g)
                a = accv(w[g])
                d.tensor_tensor(a, a, ww[u][:, 0, g, :].unsqueeze(2).broadcast_to([P, H, CW]), ALU.mult).then_inc(S["a_steps"], 1)

            def added(b, u, w, g):
                dve.wait_ge(S["p_scaled"], b * B + g + 1)
                dve.wait_ge(S["a_steps"], b * (2 * B) + (2 * g + 1))
                a = accv(w[g])
                d.tensor_tensor(a, a, part[u][:, g, 0:ROW].rearrange("p (h c) -> p h c", c=CW), ALU.add).then_inc(S["a_steps"], 1)

            def sums_added(b, u, w, between=None):
                dve.wait_ge(S["ww_ready"], b + 1)
                scaled_part(u, 0)
                for g in range(B):
                    scaled_sum(b, u, w, g)
                    if g + 1 < B:
                        scaled_part(u, g + 1)
                    added(b, u, w, g)
                    if g == 1 and between:
                        between()

            def step(b, k, u, n, nk, j, last):
                rv = ringv(u)
                o = 1 - u
                dve.wait_ge(S["adE_done"], b + 1)
                if not last:
                    dve.wait_ge(rec_in[o], (k + u) * (16 * B) + 16 * B)
                    places(b + 1, o)
                d.tensor_reduce(ad_e[:], psE[:, 0:BT * AW].rearrange("p (i c h) -> p i h c", c=3, h=H), axis=X, op=ALU.add).then_inc(S["ad_summed"], 1)
                dve.wait_ge(pen_in[u], k * (16 * B) + 16 * B)
                dve.wait_ge(S["asT_done"], b + 1)
                d.tensor_tensor_scan(scf[:], pens[u][:, 0:GE], psT[0:HB, :], -BIG, ALU.add, ALU.max).then_inc(S["scans_done"], 1)
                flags = recs[u][:].bitcast(F32).rearrange("p g (t f) -> p g t f", f=4)[:, :, :, 2]
                d.tensor_tensor(ring[u][:, :, MW - 1].rearrange("p (g t) -> p g t", t=T), flags, first[:], ALU.max).then_inc(S["flags_ready"], 1)
                dve.wait_ge(S["scans_done"], b * 2 + 1)
                d.tensor_tensor_scan(scb[:, ::-1], pens[u][:, GE:0:-1], scf[:, ::-1], -BIG, ALU.add, ALU.max).then_inc(S["scans_done"], 1)
                presence(b, o)
                if n is not None and u == 0:
                    dve.wait_ge(S["qparts_ready"], n + 1)
                    d.scalar_tensor_tensor(qq[:], qex[:], 1.0, qrl[:], ALU.min, ALU.add).then_inc(S["qq_ready"], 1)
                present_maxima(b, o)
                if not last:
                    onehots(b + 1, o)
                w = windows(b)
                dve.wait_ge(S["ad_summed"], b + 1)
                d.tensor_tensor(zz[:, 0], rv[:, :, :, C], ad_e[:], ALU.add)
                new_maximum(b, w, 0)
                dve.wait_ge(S["sT_done"], b + 1)
                d.tensor_tensor(zz[:, 1].rearrange("p (g t) h -> p t g h", t=T), psE[:, 384:512].rearrange("p (t g h) -> p t g h", t=T, h=H),
                                ad_e[:].rearrange("p (g t) h -> p t g h", t=T), ALU.add).then_inc(S["zz_ready"], 1)
                old_under_new(b, w, 0, o)
                dve.wait_ge(S["zz_ready"], b + 1)
                d.scalar_tensor_tensor(zz[:], zz[:], SLOPE, zz[:], ALU.mult, ALU.max).then_inc(S["al_ready"], 1)
                kept_maximum(b, w, 0)
                dve.wait_ge(S["al_ready"], b + 1)
                d.tensor_tensor(df[:], zz[:, 0], zz[:, 1], ALU.subtract).then_inc(S["eprep_done"], 1)
                new_maximum(b, w, 1)
                dve.wait_ge(S["flags_ready"], b + 1)
                d.tensor_tensor(ring[u][:, :, ROW:ROW + H], zz[:, 1], ring[u][:, :, MW - 1:MW].broadcast_to([128, BT, H]), ALU.mult)
                old_under_new(b, w, 1, o)

                def weigh(g):
                    if g == 0:
                        dve.wait_ge(S["ex_done"], b + 1)
                    q = slice(g * T, (g + 1) * T)
                    d.tensor_tensor(rv[:, q, :, 0:C], rv[:, q, :, 0:C], rv[:, q, :, C:CW].broadcast_to([128, T, H, C]), ALU.mult).then_inc(S["msg_ready"], 1)
                weigh(0)
                kept_maximum(b, w, 1)
                weigh(1)
                new_maximum(b, w, 2)
                old_under_new(b, w, 2, o)
                weigh(2)
                kept_maximum(b, w, 2)
                if n is not None and u == 0:
                    dve.wait_ge(S["rden_ready"], n + 1)
                    d.scalar_tensor_tensor(fix[:], M1[:, KD * P:2 * KD * P], MIX_EPS, den[:], ALU.add, ALU.mult).then_inc(S["fix_ready"], 1)
                weigh(3)
                if n is not None and u == 0:
                    dve.wait_ge(S["fix_ready"], n * 2 + 1)
                    d.scalar_tensor_tensor(den[:], fix[:], 2.0, den[:], ALU.subtract, ALU.mult).then_inc(S["fix_ready"], 1)
                new_maximum(b, w, 3)
                if n is not None and u == 0:
                    dve.wait_ge(S["fix_ready"], n * 2 + 2)
                    d.scalar_tensor_tensor(msgT[:], M1[:, 0:KD * P], float(-N), den[:], ALU.mult, ALU.mult).then_inc(S["msgT_ready"], 1)
                old_under_new(b, w, 3, o)
                batch_under_new(o)
                kept_maximum(b, w, 3)

                def mixed():
                    if n is not None:
                        dve.wait_ge(S["wm_done"] if u == 0 else S["w2_done"], n + 1)
                        statistics(u, n * 2 + u, (M0 if u == 0 else M1)[0:P, 0:D])
                sums_added(b, o, w, mixed)

            d.memset(part[1][:], 0.0).then_inc(S["consts"], 1)
            dve.wait_ge(S["consts"], 3)
            steps(dve, step)
            w = windows(NB)
            presence(NB, 1)
            present_maxima(NB, 1)
            for g in range(B):
                new_maximum(NB, w, g)
                old_under_new(NB, w, g, 1)
                kept_maximum(NB, w, g)
            batch_under_new(1)
            sums_added(NB, 1, w)


def slices(nc, sb, ps, sem, linker, v):
    ident, ones, acc, wc, bc, rows = (v[k] for k in "ident ones acc wc bc rows".split())
    mix_d, swT_d, out = v["mix_d"], v["swT_d"], v["out"]
    TW = D + 1
    Q = 5
    with ExitStack() as ctx:
        gm = [sb(ctx, f"gm{i}", [P, D]) for i in range(Q)]
        mixt = [sb(ctx, f"mixt{i}", [P, D]) for i in range(Q)]
        rden = sb(ctx, "rden", [P, NT, H])
        st6 = sb(ctx, "st6c", [P, Q, 6])
        mv = sb(ctx, "mvc", [P, Q, 2])
        lnv = sb(ctx, "lnvc", [P, Q, 1])
        nm = sb(ctx, "nmc", [P, Q, 1])
        rstd = sb(ctx, "rstdc", [P, Q, 1])
        nb = sb(ctx, "nbc", [P, Q, 1])
        xn = [sb(ctx, f"xnc{i}", [P, TW]) for i in range(Q)]
        xnT = [sb(ctx, f"xnTc{i}", [128, KD * P]) for i in range(Q)]
        lg = [sb(ctx, f"lg{i}", [P, INNER]) for i in range(Q)]
        ex = [sb(ctx, f"ex{i}", [P, INNER]) for i in range(Q)]
        sw = [sb(ctx, f"sw{i}", [P, INNER]) for i in range(Q)]
        swT = [sb(ctx, f"swT{i}", [128, 4 * P]) for i in range(Q)]
        mx = [sb(ctx, f"mx{i}", [P, FH]) for i in range(Q)]
        sm = [sb(ctx, f"sm{i}", [P, FH]) for i in range(Q)]
        epsc = sb(ctx, "epscc", [128, 2])
        zer = sb(ctx, "zer", [128, TW])
        tok = sb(ctx, "tok", [128, 4, TW])
        tokT = sb(ctx, "tokT", [128, KD, 4, 128])
        wfx = sb(ctx, "wfx", [128, KD, INNER])
        bfx = sb(ctx, "bfx", [1, INNER])
        wqkv = sb(ctx, "wqkv", [FD, 3, FD])
        wo = sb(ctx, "wo", [FD, FH, D])
        nrow = sb(ctx, "nrow", [1, INNER])
        rrow = sb(ctx, "rrow", [1, INNER])
        rbc, stT, qT, kT, vv = (lg[i][0:FD, :] for i in range(Q))
        sc, se, aT, osT = (ex[i][0:FD, :] for i in range(4))
        smx = sb(ctx, "smx", [FD, FH])
        ssum = sb(ctx, "ssum", [FD, FH])
        mm = sb(ctx, "mm", [128, 4, D])
        back, ot, res = swT, mixt, gm
        psT = ps(ctx, "pC_T")
        psL = ps(ctx, "pC_L")
        psW = ps(ctx, "pC_W")
        psK = [ps(ctx, f"pC_K{i}") for i in range(4)]
        names = """rden_ready gm_ready x1_ready st_ready var_ready norm_steps xn_ready xT_done
            xnT_ready lg_done lgb_ready mx_ready sub_ready ex_ready sm_ready rsm_ready sw_ready swT_done swT_ready
            swT_free consts weights_in pe_m dve_m act_m y_done y_read""".split()
        S = {n: sem(ctx, "s_" + n) for n in names}
        mix_in, swT_out, back_in = v["mix_in"], v["swT_out"], v["back_in"]
        out_done, o_free, o_ready = v["out_done"], v["o_free"], v["o_ready"]
        block = ctx.enter_context(nc.Block())

        def hd(a):
            return a.rearrange("p (h g) -> p h g", g=FD)

        def wide(a, p=P):
            return a.unsqueeze(2).broadcast_to([p, FH, FD])

        def later(t, k):
            return not (isinstance(t, int) and t < k)

        @block.sync
        def _(sp):
            def load(t, q, u):
                if later(t, Q):
                    sp.wait_ge(S["x1_ready"], t - (Q - 1))
                sp.dma_start(mixt[u][:], mix_d[bass.ds(t * P, P), :]).then_inc(mix_in[u], 16)
                if isinstance(t, int) and t == Q - 1:
                    slice_weights()

            def slice_weights():
                sp.dma_start(wfx[:], v["W_fx"].rearrange("(k p) n -> p k n", p=128)).then_inc(S["weights_in"], 16)
                sp.dma_start(bfx[:], v["b_fx"].rearrange("(a n) -> a n", a=1)).then_inc(S["weights_in"], 16)
                for i, w in enumerate(("W_q", "W_k", "W_v")):
                    sp.dma_start(wqkv[:, i, :], v[w]).then_inc(S["weights_in"], 16)
                sp.dma_start(wo[:], v["W_out"].rearrange("(h c) n -> c h n", c=FD)).then_inc(S["weights_in"], 16)

            def free(t, q, u):
                sp.wait_ge(swT_out[u], q * 16 + 16)
                sp.sem_inc(S["swT_free"], 1)
            pipeline(sp, Q, [(5, load), (0, free)])
            for i in range(Q):
                sp.dma_start(back[i][:], swT_d[i, :, :]).then_inc(back_in[i], 16)
            with sp.Fori(0, NT // Q - 1) as it:
                for i in range(Q):
                    sp.wait_ge(S["y_done"], it * Q + i + 1)
                    sp.dma_start(back[i][:], swT_d[bass.ds(it * Q + (Q + i), 1), :, :].rearrange("a p n -> (a p) n")).then_inc(back_in[i], 16)

        @block.gpsimd
        def _(pool):
            g = nc.gpsimd

            def residual(t, q, u):
                pool.wait_ge(S["gm_ready"], t + 1)
                pool.wait_ge(mix_in[u], q * 16 + 16)
                pool.sem_inc(v["apart"], 1)
                g.tensor_tensor(acc[:, bass.ds(t, 1), 0:D].rearrange("p a n -> p (a n)"), gm[u][:], mixt[u][:], ALU.add).then_inc(S["x1_ready"], 1)

            def under_maximum(t, q, u):
                pool.wait_ge(S["mx_ready"], t + 1)
                g.tensor_tensor(hd(lg[u][:]), hd(lg[u][:]), wide(mx[u][:]), ALU.subtract).then_inc(S["sub_ready"], 1)

            def weights(t, q, u):
                pool.wait_ge(S["rsm_ready"], t + 1)
                g.tensor_tensor(hd(sw[u][:]), hd(ex[u][:]), wide(sm[u][:]), ALU.mult).then_inc(S["sw_ready"], 1)
            pipeline(pool, Q, [(1, under_maximum), (0, weights), (4, residual)])

        @block.scalar
        def _(act):
            s = nc.scalar
            act.preload_act_table_set("natural_log_exp_and_others")
            act.sem_inc(S["swT_free"], Q)
            act.sem_inc(S["swT_ready"], 1)
            act.wait_ge(S["consts"], 1)

            def exponentials(t, q, u):
                act.wait_ge(S["sub_ready"], t + 1)
                s.activation(ex[u][:], lg[u][:], ACT.Exp).then_inc(S["ex_ready"], 1)

            def normalised(t, q, u):
                act.wait_ge(S["var_ready"], t + 1)
                s.activation(lnv[:, u, :], mv[:, u, 1:2], ACT.Ln, bias=epsc[0:P, 0:1]).then_inc(S["norm_steps"], 1)
                s.activation(nm[:, u, :], mv[:, u, 0:1], ACT.Copy, scale=-1.0)
                act.wait_ge(S["norm_steps"], t * 3 + 1)
                s.activation(rstd[:, u, :], lnv[:, u, :], ACT.Exp, scale=-0.5).then_inc(S["norm_steps"], 1)
                act.wait_ge(S["norm_steps"], t * 3 + 2)
                s.activation(nb[:, u, :], nm[:, u, :], ACT.Identity, scale=rstd[:, u, :], bias=epsc[0:P, 1:2]).then_inc(S["norm_steps"], 1)
                act.wait_ge(S["norm_steps"], t * 3 + 3)
                s.activation(xn[u][:, 0:D], acc[:, bass.ds(t, 1), 0:D].rearrange("p a n -> p (a n)"), ACT.Identity,
                             scale=rstd[:, u, :], bias=nb[:, u, :]).then_inc(S["xn_ready"], 1)

            def transposed(t, q, u):
                act.wait_ge(S["xT_done"], t + 1)
                s.activation(xnT[u][:], psT[:, 0:KD * P], ACT.Copy).then_inc(S["xnT_ready"], 1)

            def stored(t, q, u):
                act.wait_ge(S["swT_done"], t + 1)
                act.wait_ge(S["swT_free"], t + 1)
                s.activation(swT[u][:], psW[:, 0:4 * P], ACT.Copy).then_inc(S["swT_ready"], 1)
                act.wait_ge(S["swT_ready"], t + 2)
                act.dma_start(swT_d[bass.ds(t, 1), :, :].rearrange("a p n -> (a p) n"), swT[u][:]).then_inc(swT_out[u], 16)
            pipeline(act, Q, [(1, exponentials), (3, normalised), (3, transposed), (0, stored)])
            act.wait_ge(S["dve_m"], 9)
            s.activation(se, sc, ACT.Exp, scale=float(FD) ** -0.5).then_inc(S["act_m"], 1)
            act.sem_inc(o_free, Q)
            with act.Fori(0, NT // Q) as it:
                for i in range(Q):
                    act.wait_ge(o_ready, it * Q + i + 1)
                    act.dma_start(out[bass.ds((it * Q + i) * P, P), :], res[i][:]).then_inc(out_done, 16)
                act.wait_ge(out_done, it * (16 * Q) + 16 * Q)
                act.sem_inc(o_free, Q)

        @block.vector
        def _(dve):
            d = nc.vector
            d.memset(epsc[:, 0:1], LN_EPS)
            d.memset(epsc[:, 1:2], 0.0)
            d.memset(zer[:], 0.0)
            for u in range(Q):
                la = d.memset(xn[u][:, D:TW], 1.0)
            la.then_inc(S["consts"], 1)
            d.tensor_scalar(rden[:], acc[:, 0:NT, :].rearrange("p n (h c) -> p n h c", c=CW)[:, :, :, C], DEN_EPS, None, ALU.add).then_inc(S["rden_ready"], 1)
            dve.wait_ge(S["rden_ready"], 1)
            d.reciprocal(rden[:], rden[:]).then_inc(S["rden_ready"], 1)
            dve.wait_ge(S["rden_ready"], 2)

            def messages(t, q, u):
                a = acc[:, bass.ds(t, 1), :].rearrange("p a (h c) -> p (a h) c", c=CW)
                d.tensor_tensor(gm[u][:].rearrange("p (h c) -> p h c", c=C), a[:, :, 0:C],
                                rden[:, bass.ds(t, 1), :].rearrange("p a h -> p (a h)").unsqueeze(2).broadcast_to([P, H, C]),
                                ALU.mult).then_inc(S["gm_ready"], 1)

            def statistics(t, q, u):
                dve.wait_ge(S["x1_ready"], t + 1)
                dve.sem_inc(v["apart"], 1)
                d.bn_stats(st6[:, u, :], acc[:, bass.ds(t, 1), 0:D].rearrange("p a n -> p (a n)")).then_inc(S["st_ready"], 1)
                dve.wait_ge(S["st_ready"], t + 1)
                dve.sem_inc(v["apart"], 1)
                d.bn_aggr(mv[:, u, :], st6[:, u, :]).then_inc(S["var_ready"], 1)

            def logits(t, q, u):
                dve.wait_ge(S["lg_done"], t + 1)
                d.tensor_tensor(lg[u][:], psL[0:P, :], bc[:], ALU.add).then_inc(S["lgb_ready"], 1)
                dve.wait_ge(S["lgb_ready"], t + 1)
                d.tensor_reduce(mx[u][:], hd(lg[u][:]), axis=X, op=ALU.max).then_inc(S["mx_ready"], 1)

            def sums(t, q, u):
                dve.wait_ge(S["ex_ready"], t + 1)
                d.tensor_reduce(sm[u][:], hd(ex[u][:]), axis=X, op=ALU.add).then_inc(S["sm_ready"], 1)
                dve.wait_ge(S["sm_ready"], t + 1)
                d.reciprocal(sm[u][:], sm[u][:]).then_inc(S["rsm_ready"], 1)
            pipeline(dve, Q, [(0, sums), (3, statistics), (2, logits), (5, messages)])

            done = linker(dve, S["dve_m"])
            dve.wait_ge(S["pe_m"], 1)
            for j in range(4):
                la = d.tensor_copy(tok[:, j, :], psK[j][:, 0:TW])
            done(la)
            dve.wait_ge(S["pe_m"], 2)
            for k in range(KD):
                d.tensor_copy(tokT[:, k, :, :], psK[k][:, :].rearrange("p (j n) -> p j n", j=4))
            la = d.tensor_copy(nrow[:], psK[2][0:1, :])
            done(la)
            done(d.tensor_scalar(rrow[:], nrow[:], TOK_EPS, None, ALU.add))
            done(d.reciprocal(rrow[:], rrow[:]))
            dve.wait_ge(S["pe_m"], 3)
            done(d.tensor_copy(rbc, psK[3][0:FD, :]))
            done(d.tensor_tensor(stT, psL[0:FD, :], rbc, ALU.mult))
            dve.wait_ge(S["pe_m"], 4)
            d.tensor_copy(qT, psK[0][0:FD, :])
            d.tensor_copy(kT, psK[1][0:FD, :])
            done(d.tensor_copy(vv, psK[2][0:FD, :]))
            dve.wait_ge(S["pe_m"], 5)
            done(d.tensor_reduce(smx[:], hd(psL[0:FD, :]), axis=X, op=ALU.max))
            done(d.tensor_tensor(hd(sc), hd(psL[0:FD, :]), wide(smx[:], FD), ALU.subtract))
            dve.wait_ge(S["act_m"], 1)
            done(d.tensor_reduce(ssum[:], hd(se), axis=X, op=ALU.add))
            done(d.reciprocal(ssum[:], ssum[:]))
            done(d.tensor_tensor(hd(se), hd(se), wide(ssum[:], FD), ALU.mult))
            dve.wait_ge(S["pe_m"], 6)
            done(d.tensor_copy(aT, psK[3][0:FD, :]))
            dve.wait_ge(S["pe_m"], 7)
            done(d.tensor_copy(osT, psL[0:FD, :]))
            dve.wait_ge(S["pe_m"], 8)
            for j in range(4):
                d.tensor_copy(mm[0:FD, j, :], psK[j][0:FD, 0:D])
                la = d.tensor_copy(mm[FD:, j, :], psK[j][FD:, D:2 * D])
            done(la)
            with dve.Fori(0, NT // Q) as it:
                for i in range(Q):
                    n = it * Q + i
                    dve.wait_ge(S["y_done"], n + 1)
                    d.tensor_tensor(ot[i][:], psK[i % 4][0:P, 0:D] if i < 4 else psL[0:P, 0:D], rows[:, 3, :], ALU.add).then_inc(S["y_read"], 1)
                    dve.wait_ge(S["y_read"], n + (Q + 1))
                    dve.wait_ge(o_free, n + 1)
                    d.tensor_tensor(res[i][:], ot[i][:], acc[:, bass.ds(n, 1), 0:D].rearrange("p a n -> p (a n)"), ALU.add).then_inc(o_ready, 1)

        @block.tensor
        def _(pe):
            t_ = nc.tensor

            def turned(t, q, u):
                pe.wait_ge(S["xn_ready"], t + 1)
                for c in range(KD):
                    la = t_.transpose(psT[:, c * P:(c + 1) * P], xn[u][:, c * 128:(c + 1) * 128], ident[0:P, 0:P])
                la.then_inc(S["xT_done"], 1)

            def logits(t, q, u):
                pe.wait_ge(S["xnT_ready"], t + 1)
                if later(t, 1):
                    pe.wait_ge(S["lgb_ready"], t)
                for c in range(KD):
                    la = t_.matmul(psL[0:P, :], xnT[u][:, c * P:(c + 1) * P], wc[:, c, :], start=(c == 0), stop=(c == KD - 1))
                la.then_inc(S["lg_done"], 1)

            def slice_sums(t, q, u):
                pe.wait_ge(S["sw_ready"], t + 1)
                for j in range(4):
                    t_.matmul(psK[j][:, 0:TW], sw[u][:, j * 128:(j + 1) * 128], xn[u][:], start=False, stop=False)

            def weights_turned(t, q, u):
                pe.wait_ge(S["swT_ready"], t + 1)
                for j in range(4):
                    la = t_.transpose(psW[:, j * P:(j + 1) * P], sw[u][:, j * 128:(j + 1) * 128], ident[0:P, 0:P])
                la.then_inc(S["swT_done"], 1)

            pe.wait_ge(S["consts"], 1)
            for j in range(4):
                t_.matmul(psK[j][:, 0:TW], zer[:, 0:128], zer[:, 0:TW], start=True, stop=False)
            pipeline(pe, Q, [(2, logits), (0, slice_sums), (3, turned), (0, weights_turned)])
            for j in range(4):
                la = t_.matmul(psK[j][:, 0:TW], zer[:, 0:128], zer[:, 0:TW], start=False, stop=True)
            la.then_inc(S["pe_m"], 1)
            pe.wait_ge(S["dve_m"], 1)
            for k in range(KD):
                for j in range(4):
                    t_.transpose(psK[k][:, j * 128:(j + 1) * 128], tok[:, j, k * 128:(k + 1) * 128], ident[:])
            for j in range(4):
                la = t_.matmul(psK[2][0:1, j * 128:(j + 1) * 128], tok[:, j, D:TW], ident[:], start=True, stop=True)
            la.then_inc(S["pe_m"], 1)
            pe.wait_ge(S["dve_m"], 4)
            pe.wait_ge(S["weights_in"], 16 * 6)
            t_.matmul(psK[3][0:FD, :], ones[0:1, 0:FD], rrow[:], start=True, stop=True)
            for h in range(FH):
                q = slice(h * FD, (h + 1) * FD)
                for k in range(KD):
                    t_.matmul(psL[0:FD, q], wfx[:, k, q], tokT[:, k, :, :].rearrange("p j n -> p (j n)")[:, q], start=(k == 0), stop=False)
                la = t_.matmul(psL[0:FD, q], bfx[:, q], nrow[:, q], start=False, stop=True)
            la.then_inc(S["pe_m"], 1)
            pe.wait_ge(S["dve_m"], 6)
            for i in range(2):
                t_.matmul(psK[i][0:FD, :], wqkv[:, i, :], stT, start=True, stop=True)
            for h in range(FH):
                q = slice(h * FD, (h + 1) * FD)
                la = t_.matmul(psK[2][0:FD, q], stT[:, q], wqkv[:, 2, :], start=True, stop=True)
            la.then_inc(S["pe_m"], 1)
            pe.wait_ge(S["dve_m"], 7)
            for h in range(FH):
                q = slice(h * FD, (h + 1) * FD)
                la = t_.matmul(psL[0:FD, q], qT[:, q], kT[:, q], start=True, stop=True)
            la.then_inc(S["pe_m"], 1)
            pe.wait_ge(S["dve_m"], 12)
            for h in range(FH):
                q = slice(h * FD, (h + 1) * FD)
                la = t_.transpose(psK[3][0:FD, q], se[:, q], ident[0:FD, 0:FD])
            la.then_inc(S["pe_m"], 1)
            pe.wait_ge(S["dve_m"], 13)
            for h in range(FH):
                q = slice(h * FD, (h + 1) * FD)
                la = t_.matmul(psL[0:FD, q], vv[:, q], aT[:, q], start=True, stop=True)
            la.then_inc(S["pe_m"], 1)
            pe.wait_ge(S["dve_m"], 14)
            for j in range(4):
                for i in range(2):
                    la = t_.matmul(psK[j][:, i * D:(i + 1) * D], osT[:, j * 128:(j + 1) * 128], wo[:, 2 * j + i, :], start=True, stop=True)
            la.then_inc(S["pe_m"], 1)
            pe.wait_ge(S["dve_m"], 15)
            pe.sem_inc(S["y_read"], Q)
            with pe.Fori(0, NT // Q) as it:
                for i in range(Q):
                    n = it * Q + i
                    pe.wait_ge(back_in[i], it * 16 + 16)
                    bank = psK[i % 4] if i < 4 else psL
                    pe.wait_ge(S["y_read"], n + 1)
                    for j in range(4):
                        la = t_.matmul(bank[0:P, 0:D], back[i][:, j * P:(j + 1) * P], mm[:, j, :], start=(j == 0), stop=(j == 3))
                    la.then_inc(S["y_done"], 1)


_INS = ['x', 'src', 'dst', 'L0_gnn_W', 'L0_gnn_att_src', 'L0_gnn_att_dst', 'L0_gnn_bias', 'L0_mix_Wq', 'L0_mix_Wk', 'L0_mix_Wv',
        'L0_mix_Wm', 'L0_mix_W1', 'L0_mix_W2', 'L0_mix_g1', 'L0_mix_b1', 'L0_mix_g2', 'L0_mix_b2', 'L0_ffn_W_fx', 'L0_ffn_b_fx',
        'L0_ffn_W_x', 'L0_ffn_b_x', 'L0_ffn_W_slice', 'L0_ffn_b_slice', 'L0_ffn_W_q', 'L0_ffn_W_k', 'L0_ffn_W_v', 'L0_ffn_W_out',
        'L0_ffn_b_out', 'L0_ffn_temperature']


def kernel(**inputs):
    import numpy as _np
    import concourse.bacc as _bacc
    from concourse import mybir as _mybir
    from concourse.bass_utils import run_bass_kernel_spmd as _run

    nc = _bacc.Bacc("TRN2", target_bir_lowering=False, num_devices=1)
    arrays, args = {}, []
    for name in _INS:
        a = _np.ascontiguousarray(inputs[name])
        arrays[f"in_{name}_dram"] = a
        args.append(nc.dram_tensor(f"in_{name}_dram", a.shape, _mybir.dt.from_np(a.dtype), kind="ExternalInput").ap())
    out = nc.dram_tensor("out_0_dram", (N, D), F32, kind="ExternalOutput").ap()
    program(nc, *args, out)
    r = _run(nc, [arrays], core_ids=[0])
    return r.results[0]["out_0_dram"]
```
